# Optimizing a Trainium2 kernel written in Bass

```python
import numpy as np
import jax
import jax.numpy as jnp

def _softmax(x, axis=-1):
    return jax.nn.softmax(x, axis=axis)

def _gelu(x):
    return jax.nn.gelu(x, approximate=True)

def _silu(x):
    return jax.nn.silu(x)

def _sigmoid(x):
    return jax.nn.sigmoid(x)

def _layernorm(x, axis=-1, eps=1e-05):
    m = jnp.mean(x, axis=axis, keepdims=True)
    v = jnp.var(x, axis=axis, keepdims=True)
    return (x - m) / jnp.sqrt(v + eps)

def _scatter_add(tgt, idx, src, axis=0):
    return tgt.at[idx].add(src)

def _segment_sum(src, seg, n):
    return jax.ops.segment_sum(src, seg, n)
kernel_name = 'mk_perceiver_d2_seqx_r8_99e5c0'

def setup_inputs(seed: int=0):
    np.random.seed(seed)
    _w = jnp.asarray

    def _rec_inputs():
        import jax
        import jax.numpy as jnp
        _rk = jax.random.key(seed)
        x = -0.0003929 + 0.9999 * jax.random.normal(jax.random.fold_in(_rk, 1), (16, 64, 128), jnp.float32)
        _lenS = 64 - jax.random.randint(jax.random.fold_in(_rk, 7), (16,), 0, max(1, 64 // 4) + 1, jnp.int32)
        _lenS2 = 1601 - jax.random.randint(jax.random.fold_in(_rk, 8), (16,), 0, max(1, 1601 // 4) + 1, jnp.int32)
        _ctx_1024P = jax.random.normal(jax.random.fold_in(_rk, 11), (16, 16, 128), jnp.float32)
        _ctx_1024c = jax.random.dirichlet(jax.random.fold_in(_rk, 511), 0.3 * jnp.ones((16,), jnp.float32), (16, 1601))
        _ctx_1024t = jnp.einsum('bsk,bkd->bsd', _ctx_1024c, _ctx_1024P)
        _ctx_1024t = _ctx_1024t * jax.lax.rsqrt(jnp.mean(jnp.square(_ctx_1024t)) + 1e-12) * 0.953939
        ctx_1024 = 2.81802e-05 + 1.00001 * (_ctx_1024t + 0.3 * jax.random.normal(jax.random.fold_in(_rk, 611), (16, 1601, 128), jnp.float32))
        _validS = jnp.arange(64)[None, :] < _lenS[:, None]
        _validS2 = jnp.arange(1601)[None, :] < _lenS2[:, None]
        _causal = jnp.tril(jnp.ones((64, 64), dtype=bool))
        mask_Bx1x1xS2_ff0 = jnp.where(jnp.ones((16, 1, 1, 1601), dtype=bool), 0.0, -1000000000.0).astype(jnp.float32)
        return (x, ctx_1024, mask_Bx1x1xS2_ff0)
    x, ctx_1024, mask_Bx1x1xS2_ff0 = _rec_inputs()

    def _L0_xattn_setup():
        import jax, jax.numpy as jnp
        import numpy as np
        DIM = 128
        key = jax.random.key(seed)
        ks = jax.random.split(key, 8)
        B, S, D = (8, 256, DIM)
        scale = 1.0 / np.sqrt(D)
        x1 = jax.random.normal(ks[0], (B, S, D), dtype=jnp.float32)
        x2 = jax.random.normal(ks[1], (B, S, D), dtype=jnp.float32)
        Wq = jax.random.normal(ks[2], (D, D), dtype=jnp.float32) * scale
        bq = jnp.zeros((D,), dtype=jnp.float32)
        Wk = jax.random.normal(ks[3], (D, D), dtype=jnp.float32) * scale
        bk = jnp.zeros((D,), dtype=jnp.float32)
        Wv = jax.random.normal(ks[4], (D, D), dtype=jnp.float32) * scale
        bv = jnp.zeros((D,), dtype=jnp.float32)
        return {'x1': x1, 'x2': x2, 'Wq': Wq, 'bq': bq, 'Wk': Wk, 'bk': bk, 'Wv': Wv, 'bv': bv}
    _L0_xattn_all = _L0_xattn_setup()
    _L0_xattn_in = {k: v for k, v in _L0_xattn_all.items() if k in ('Wq', 'bq', 'Wk', 'bk', 'Wv', 'bv')}
    del _L0_xattn_all

    def _L0_attn_setup():
        import jax, jax.numpy as jnp
        import numpy as np
        D_MODEL = 128
        N_HEADS = 16
        D_HEAD = D_MODEL // N_HEADS
        SEQ = 512
        BATCH = 1
        key = jax.random.key(seed)
        kx, kq, kk, kv, ko = jax.random.split(key, 5)
        scale = (1.0 / D_MODEL) ** 0.5
        return {'x': jax.random.normal(kx, (BATCH, SEQ, D_MODEL), dtype=jnp.float32), 'W_Q': jax.random.normal(kq, (D_MODEL, D_MODEL), dtype=jnp.float32) * scale, 'W_K': jax.random.normal(kk, (D_MODEL, D_MODEL), dtype=jnp.float32) * scale, 'W_V': jax.random.normal(kv, (D_MODEL, D_MODEL), dtype=jnp.float32) * scale, 'W_o': jax.random.normal(ko, (D_MODEL, D_MODEL), dtype=jnp.float32) * scale}
    _L0_attn_all = _L0_attn_setup()
    _L0_attn_in = {k: v for k, v in _L0_attn_all.items() if k in ('W_Q', 'W_K', 'W_V', 'W_o')}
    del _L0_attn_all

    def _L0_ffn_setup():
        import jax, jax.numpy as jnp
        import numpy as np
        W_SCALE = 0.02
        TOP_K = 2
        key = jax.random.key(seed)
        ks = jax.random.split(key, 5)
        B, S, H, I, E = (2, 128, 128, 512, 8)
        return {'x': jax.random.normal(ks[0], (B, S, H), dtype=jnp.float32), 'gate': jax.random.normal(ks[1], (H, E), dtype=jnp.float32) * W_SCALE, 'experts_w1': jax.random.normal(ks[2], (E, H, I), dtype=jnp.float32) * W_SCALE, 'experts_w2': jax.random.normal(ks[3], (E, I, H), dtype=jnp.float32) * W_SCALE, 'experts_w3': jax.random.normal(ks[4], (E, H, I), dtype=jnp.float32) * W_SCALE}
    _L0_ffn_all = _L0_ffn_setup()
    _L0_ffn_in = {k: v for k, v in _L0_ffn_all.items() if k in ('gate', 'experts_w1', 'experts_w2', 'experts_w3')}
    del _L0_ffn_all

    def _L1_xattn_setup():
        import jax, jax.numpy as jnp
        import numpy as np
        H = 16
        D = 128
        F = 512
        LN_EPS = 1e-05

        def _glorot(key, shape):
            fan_in, fan_out = (shape[0], shape[1])
            lim = np.sqrt(6.0 / (fan_in + fan_out))
            return jax.random.uniform(key, shape, jnp.float32, -lim, lim)

        def _split_heads(x):
            b, l, _ = x.shape
            return x.reshape(b, l, H, D // H)

        def _mha(x, ctx, mask, qw, qb, kw, kb, vw, vb):
            q = _split_heads(x @ qw + qb)
            k = _split_heads(ctx @ kw + kb)
            v = _split_heads(ctx @ vw + vb)
            scores = jnp.einsum('bqhd,bkhd->bhqk', q, k) / np.sqrt(D // H).astype(np.float32)
            if mask is not None:
                scores = scores + mask
            probs = jax.nn.softmax(scores, axis=-1)
            out = jnp.einsum('bhqk,bkhd->bqhd', probs, v)
            return out.reshape(x.shape[0], x.shape[1], D)

        def _self_output(h, residual, w, b, g, be):
            h = h @ w + b
            h = h + residual
            mu = jnp.mean(h, axis=-1, keepdims=True)
            var = jnp.mean(jnp.square(h - mu), axis=-1, keepdims=True)
            return (h - mu) * jax.lax.rsqrt(var + LN_EPS) * g + be
        key = jax.random.key(seed)
        ks = jax.random.split(key, 16)
        inp = {'input_tensor': jax.random.normal(ks[0], (4, 128, D), jnp.float32), 'ctx_tensor': jax.random.normal(ks[1], (4, 256, D), jnp.float32), 'ctx_attn_mask': jnp.zeros((4, 1, 1, 256), jnp.float32), 'cq_w': _glorot(ks[2], (D, D)), 'cq_b': jnp.zeros((D,)), 'ck_w': _glorot(ks[3], (D, D)), 'ck_b': jnp.zeros((D,)), 'cv_w': _glorot(ks[4], (D, D)), 'cv_b': jnp.zeros((D,)), 'co_w': _glorot(ks[5], (D, D)), 'co_b': jnp.zeros((D,)), 'co_g': jnp.ones((D,)), 'co_be': jnp.zeros((D,)), 'sq_w': _glorot(ks[6], (D, D)), 'sq_b': jnp.zeros((D,)), 'sk_w': _glorot(ks[7], (D, D)), 'sk_b': jnp.zeros((D,)), 'sv_w': _glorot(ks[8], (D, D)), 'sv_b': jnp.zeros((D,)), 'so_w': _glorot(ks[9], (D, D)), 'so_b': jnp.zeros((D,)), 'so_g': jnp.ones((D,)), 'so_be': jnp.zeros((D,)), 'fi_w': _glorot(ks[10], (D, F)), 'fi_b': jnp.zeros((F,)), 'fo_w': _glorot(ks[11], (F, D)), 'fo_b': jnp.zeros((D,)), 'fo_g': jnp.ones((D,)), 'fo_be': jnp.zeros((D,))}
        return inp
    _L1_xattn_all = _L1_xattn_setup()
    _L1_xattn_in = {k: v for k, v in _L1_xattn_all.items() if k in ('cq_w', 'cq_b', 'ck_w', 'ck_b', 'cv_w', 'cv_b', 'co_w', 'co_b', 'co_g', 'co_be', 'sq_w', 'sq_b', 'sk_w', 'sk_b', 'sv_w', 'sv_b', 'so_w', 'so_b', 'so_g', 'so_be', 'fi_w', 'fi_b', 'fo_w', 'fo_b', 'fo_g', 'fo_be')}
    del _L1_xattn_all

    def _L1_attn_setup():
        import jax, jax.numpy as jnp
        import numpy as np
        import math
        E = 128
        H = 16
        HD = E // H
        NBITS = 8

        def fake_quant(x, n_bits=NBITS):
            qmax = 2.0 ** (n_bits - 1) - 1.0
            qmin = -2.0 ** (n_bits - 1)
            scale = jnp.maximum(jnp.max(jnp.abs(x)) / qmax, 1e-08)
            xq = jnp.round(jnp.clip(x / scale, qmin, qmax)) * scale
            return x + jax.lax.stop_gradient(xq - x)
        key = jax.random.key(seed)
        ks = jax.random.split(key, 7)
        L, B = (256, 2)
        query = jax.random.normal(ks[0], (L, B, E), dtype=jnp.float32)
        k_in = jax.random.normal(ks[1], (L, B, E), dtype=jnp.float32)
        v_in = jax.random.normal(ks[2], (L, B, E), dtype=jnp.float32)
        in_w = jax.random.normal(ks[3], (3 * E, E), dtype=jnp.float32) * (1.0 / math.sqrt(E))
        in_b = jax.random.normal(ks[4], (3 * E,), dtype=jnp.float32) * 0.01
        out_w = jax.random.normal(ks[5], (E, E), dtype=jnp.float32) * (1.0 / math.sqrt(E))
        out_b = jax.random.normal(ks[6], (E,), dtype=jnp.float32) * 0.01
        return {'query': query, 'key': k_in, 'value': v_in, 'in_w': in_w, 'in_b': in_b, 'out_w': out_w, 'out_b': out_b}
    _L1_attn_all = _L1_attn_setup()
    _L1_attn_in = {k: v for k, v in _L1_attn_all.items() if k in ('key', 'value', 'in_w', 'in_b', 'out_w', 'out_b')}
    del _L1_attn_all

    def _L1_ffn_setup():
        import jax, jax.numpy as jnp
        import numpy as np
        N_EMBD = 128
        NUM_EXPERTS = 8
        TOP_K = 2
        D_FF = 4 * N_EMBD
        B, S = (4, 256)
        key = jax.random.key(seed)
        ks = jax.random.split(key, 7)
        scale = lambda fan_in: 1.0 / np.sqrt(fan_in)
        x = jax.random.normal(ks[0], (B, S, N_EMBD), dtype=jnp.float32)
        W_router = jax.random.normal(ks[1], (N_EMBD, NUM_EXPERTS), dtype=jnp.float32) * scale(N_EMBD)
        b_router = jnp.zeros((NUM_EXPERTS,), dtype=jnp.float32)
        W1 = jax.random.normal(ks[2], (NUM_EXPERTS, N_EMBD, D_FF), dtype=jnp.float32) * scale(N_EMBD)
        b1 = jnp.zeros((NUM_EXPERTS, D_FF), dtype=jnp.float32)
        W2 = jax.random.normal(ks[3], (NUM_EXPERTS, D_FF, N_EMBD), dtype=jnp.float32) * scale(D_FF)
        b2 = jnpp = jnp.zeros((NUM_EXPERTS, N_EMBD), dtype=jnp.float32)
        return {'x': x, 'W_router': W_router, 'b_router': b_router, 'W1': W1, 'b1': b1, 'W2': W2, 'b2': b2}
    _L1_ffn_all = _L1_ffn_setup()
    _L1_ffn_in = {k: v for k, v in _L1_ffn_all.items() if k in ('W_router', 'b_router', 'W1', 'b1', 'W2', 'b2')}
    del _L1_ffn_all
    return {'x': x, 'ctx_1024': ctx_1024, 'mask_Bx1x1xS2_ff0': mask_Bx1x1xS2_ff0, 'L0_xattn_Wq': _L0_xattn_in['Wq'], 'L0_xattn_bq': _L0_xattn_in['bq'], 'L0_xattn_Wk': _L0_xattn_in['Wk'], 'L0_xattn_bk': _L0_xattn_in['bk'], 'L0_xattn_Wv': _L0_xattn_in['Wv'], 'L0_xattn_bv': _L0_xattn_in['bv'], 'L0_attn_W_Q': _L0_attn_in['W_Q'], 'L0_attn_W_K': _L0_attn_in['W_K'], 'L0_attn_W_V': _L0_attn_in['W_V'], 'L0_attn_W_o': _L0_attn_in['W_o'], 'L0_ffn_gate': _L0_ffn_in['gate'], 'L0_ffn_experts_w1': _L0_ffn_in['experts_w1'], 'L0_ffn_experts_w2': _L0_ffn_in['experts_w2'], 'L0_ffn_experts_w3': _L0_ffn_in['experts_w3'], 'L1_xattn_cq_w': _L1_xattn_in['cq_w'], 'L1_xattn_cq_b': _L1_xattn_in['cq_b'], 'L1_xattn_ck_w': _L1_xattn_in['ck_w'], 'L1_xattn_ck_b': _L1_xattn_in['ck_b'], 'L1_xattn_cv_w': _L1_xattn_in['cv_w'], 'L1_xattn_cv_b': _L1_xattn_in['cv_b'], 'L1_xattn_co_w': _L1_xattn_in['co_w'], 'L1_xattn_co_b': _L1_xattn_in['co_b'], 'L1_xattn_co_g': _L1_xattn_in['co_g'], 'L1_xattn_co_be': _L1_xattn_in['co_be'], 'L1_xattn_sq_w': _L1_xattn_in['sq_w'], 'L1_xattn_sq_b': _L1_xattn_in['sq_b'], 'L1_xattn_sk_w': _L1_xattn_in['sk_w'], 'L1_xattn_sk_b': _L1_xattn_in['sk_b'], 'L1_xattn_sv_w': _L1_xattn_in['sv_w'], 'L1_xattn_sv_b': _L1_xattn_in['sv_b'], 'L1_xattn_so_w': _L1_xattn_in['so_w'], 'L1_xattn_so_b': _L1_xattn_in['so_b'], 'L1_xattn_so_g': _L1_xattn_in['so_g'], 'L1_xattn_so_be': _L1_xattn_in['so_be'], 'L1_xattn_fi_w': _L1_xattn_in['fi_w'], 'L1_xattn_fi_b': _L1_xattn_in['fi_b'], 'L1_xattn_fo_w': _L1_xattn_in['fo_w'], 'L1_xattn_fo_b': _L1_xattn_in['fo_b'], 'L1_xattn_fo_g': _L1_xattn_in['fo_g'], 'L1_xattn_fo_be': _L1_xattn_in['fo_be'], 'L1_attn_key': _L1_attn_in['key'], 'L1_attn_value': _L1_attn_in['value'], 'L1_attn_in_w': _L1_attn_in['in_w'], 'L1_attn_in_b': _L1_attn_in['in_b'], 'L1_attn_out_w': _L1_attn_in['out_w'], 'L1_attn_out_b': _L1_attn_in['out_b'], 'L1_ffn_W_router': _L1_ffn_in['W_router'], 'L1_ffn_b_router': _L1_ffn_in['b_router'], 'L1_ffn_W1': _L1_ffn_in['W1'], 'L1_ffn_b1': _L1_ffn_in['b1'], 'L1_ffn_W2': _L1_ffn_in['W2'], 'L1_ffn_b2': _L1_ffn_in['b2']}

def reference(x, ctx_1024, mask_Bx1x1xS2_ff0, L0_xattn_Wq, L0_xattn_bq, L0_xattn_Wk, L0_xattn_bk, L0_xattn_Wv, L0_xattn_bv, L0_attn_W_Q, L0_attn_W_K, L0_attn_W_V, L0_attn_W_o, L0_ffn_gate, L0_ffn_experts_w1, L0_ffn_experts_w2, L0_ffn_experts_w3, L1_xattn_cq_w, L1_xattn_cq_b, L1_xattn_ck_w, L1_xattn_ck_b, L1_xattn_cv_w, L1_xattn_cv_b, L1_xattn_co_w, L1_xattn_co_b, L1_xattn_co_g, L1_xattn_co_be, L1_xattn_sq_w, L1_xattn_sq_b, L1_xattn_sk_w, L1_xattn_sk_b, L1_xattn_sv_w, L1_xattn_sv_b, L1_xattn_so_w, L1_xattn_so_b, L1_xattn_so_g, L1_xattn_so_be, L1_xattn_fi_w, L1_xattn_fi_b, L1_xattn_fo_w, L1_xattn_fo_b, L1_xattn_fo_g, L1_xattn_fo_be, L1_attn_key, L1_attn_value, L1_attn_in_w, L1_attn_in_b, L1_attn_out_w, L1_attn_out_b, L1_ffn_W_router, L1_ffn_b_router, L1_ffn_W1, L1_ffn_b1, L1_ffn_W2, L1_ffn_b2):
    import jax
    import jax.numpy as jnp

    def _L0_xattn_ref(x1, x2, Wq, bq, Wk, bk, Wv, bv):
        import jax, jax.numpy as jnp
        import numpy as np
        DIM = 128
        q = jnp.einsum('bsd,ed->bse', x1, Wq) + bq
        k = jnp.einsum('bsd,ed->bse', x2, Wk) + bk
        v = jnp.einsum('bsd,ed->bse', x2, Wv) + bv
        scale = jnp.asarray(q.shape[-1], q.dtype) ** (-0.5)
        attn = jnp.einsum('bqd,bkd->bqk', q, k) * scale
        attn = jax.nn.softmax(attn, axis=-1)
        return jnp.einsum('bqk,bkd->bqd', attn, v)

    def _L0_attn_ref(x, W_Q, W_K, W_V, W_o):
        import jax, jax.numpy as jnp
        import numpy as np
        D_MODEL = 128
        N_HEADS = 16
        D_HEAD = D_MODEL // N_HEADS
        SEQ = 512
        BATCH = 1
        B, S, _ = x.shape

        def heads(w):
            return (x @ w).reshape(B, S, N_HEADS, D_HEAD).transpose(0, 2, 1, 3)
        Q, K, V = (heads(W_Q), heads(W_K), heads(W_V))
        scores = jnp.einsum('bhqd,bhkd->bhqk', Q, K) / D_HEAD ** 0.5
        causal = jnp.triu(jnp.full((S, S), -jnp.inf, dtype=scores.dtype), k=1)
        scores = scores + causal
        probs = jax.nn.softmax(scores, axis=-1)
        out = jnp.einsum('bhqk,bhkd->bhqd', probs, V)
        out = out.transpose(0, 2, 1, 3).reshape(B, S, D_MODEL)
        return out @ W_o

    def _L0_ffn_ref(x, gate, experts_w1, experts_w2, experts_w3):
        import jax, jax.numpy as jnp
        import numpy as np
        W_SCALE = 0.02
        TOP_K = 2
        E = experts_w1.shape[0]
        router_logits = jnp.einsum('bsh,he->bse', x, gate)
        routing_weights, selected = jax.lax.top_k(router_logits, TOP_K)
        routing_weights = jax.nn.softmax(routing_weights, axis=-1)
        onehot = jax.nn.one_hot(selected, E, dtype=x.dtype)
        tok_w = jnp.einsum('bsk,bske->bse', routing_weights, onehot)
        g = jnp.einsum('bsh,ehi->ebsi', x, experts_w1)
        u = jnp.einsum('bsh,ehi->ebsi', x, experts_w3)
        hid = jax.nn.silu(g) * u
        eo = jnp.einsum('ebsi,eih->ebsh', hid, experts_w2)
        out = jnp.einsum('ebsh,bse->bsh', eo, tok_w)
        return out

    def _L1_xattn_ref(input_tensor, ctx_tensor, ctx_attn_mask, cq_w, cq_b, ck_w, ck_b, cv_w, cv_b, co_w, co_b, co_g, co_be, sq_w, sq_b, sk_w, sk_b, sv_w, sv_b, so_w, so_b, so_g, so_be, fi_w, fi_b, fo_w, fo_b, fo_g, fo_be):
        import jax, jax.numpy as jnp
        import numpy as np
        H = 16
        D = 128
        F = 512
        LN_EPS = 1e-05

        def _glorot(key, shape):
            fan_in, fan_out = (shape[0], shape[1])
            lim = np.sqrt(6.0 / (fan_in + fan_out))
            return jax.random.uniform(key, shape, jnp.float32, -lim, lim)

        def _split_heads(x):
            b, l, _ = x.shape
            return x.reshape(b, l, H, D // H)

        def _mha(x, ctx, mask, qw, qb, kw, kb, vw, vb):
            q = _split_heads(x @ qw + qb)
            k = _split_heads(ctx @ kw + kb)
            v = _split_heads(ctx @ vw + vb)
            scores = jnp.einsum('bqhd,bkhd->bhqk', q, k) / np.sqrt(D // H).astype(np.float32)
            if mask is not None:
                scores = scores + mask
            probs = jax.nn.softmax(scores, axis=-1)
            out = jnp.einsum('bhqk,bkhd->bqhd', probs, v)
            return out.reshape(x.shape[0], x.shape[1], D)

        def _self_output(h, residual, w, b, g, be):
            h = h @ w + b
            h = h + residual
            mu = jnp.mean(h, axis=-1, keepdims=True)
            var = jnp.mean(jnp.square(h - mu), axis=-1, keepdims=True)
            return (h - mu) * jax.lax.rsqrt(var + LN_EPS) * g + be
        ca = _mha(input_tensor, ctx_tensor, ctx_attn_mask, cq_w, cq_b, ck_w, ck_b, cv_w, cv_b)
        x = _self_output(ca, input_tensor, co_w, co_b, co_g, co_be)
        sa = _mha(x, x, None, sq_w, sq_b, sk_w, sk_b, sv_w, sv_b)
        x = _self_output(sa, x, so_w, so_b, so_g, so_be)
        inter = jax.nn.gelu(x @ fi_w + fi_b, approximate=False)
        x = _self_output(inter, x, fo_w, fo_b, fo_g, fo_be)
        return x

    def _L1_attn_ref(query, key, value, in_w, in_b, out_w, out_b):
        import jax, jax.numpy as jnp
        import numpy as np
        import math
        E = 128
        H = 16
        HD = E // H
        NBITS = 8

        def fake_quant(x, n_bits=NBITS):
            qmax = 2.0 ** (n_bits - 1) - 1.0
            qmin = -2.0 ** (n_bits - 1)
            scale = jnp.maximum(jnp.max(jnp.abs(x)) / qmax, 1e-08)
            xq = jnp.round(jnp.clip(x / scale, qmin, qmax)) * scale
            return x + jax.lax.stop_gradient(xq - x)
        L, B, _ = query.shape
        Wi = fake_quant(in_w)
        Wo = fake_quant(out_w)
        X = jnp.einsum('lbe,fe->lbf', query, Wi) + in_b
        X = fake_quant(X)
        Q, K, V = jnp.split(X, 3, axis=-1)
        q = Q.reshape(L, B * H, HD).transpose(1, 0, 2)
        k = K.reshape(L, B * H, HD).transpose(1, 0, 2)
        v = V.reshape(L, B * H, HD).transpose(1, 0, 2)
        q = q / math.sqrt(HD)
        q = fake_quant(q)
        attn = jnp.einsum('bqd,bkd->bqk', q, k)
        attn = jax.nn.softmax(attn, axis=-1)
        heads = jnp.einsum('bqk,bkd->bqd', attn, v)
        heads = fake_quant(heads)
        heads_r = heads.transpose(1, 0, 2).reshape(L * B, E)
        y = heads_r @ Wo.T + out_b
        y = y.reshape(L, B, E)
        return fake_quant(y)

    def _L1_ffn_ref(x, W_router, b_router, W1, b1, W2, b2):
        import jax, jax.numpy as jnp
        import numpy as np
        N_EMBD = 128
        NUM_EXPERTS = 8
        TOP_K = 2
        D_FF = 4 * N_EMBD
        B, S = (4, 256)
        Bv, Sv, D = x.shape
        flat_x = x.reshape(-1, D)
        T = flat_x.shape[0]
        logits = flat_x @ W_router + b_router
        top_vals, top_idx = jax.lax.top_k(logits, TOP_K)
        neg_inf = jnp.full_like(logits, -jnp.inf)
        sparse_logits = neg_inf.at[jnp.arange(T)[:, None], top_idx].set(top_vals)
        router_weights = jax.nn.softmax(sparse_logits, axis=-1)
        final_output = jnp.zeros_like(flat_x)
        for e in range(NUM_EXPERTS):
            expert_mask = jnp.any(top_idx == e, axis=-1)
            h = jax.nn.relu(flat_x @ W1[e] + b1[e])
            y = h @ W2[e] + b2[e]
            w = router_weights[:, e] * expert_mask.astype(x.dtype)
            final_output = final_output + y * w[:, None]
        return final_output.reshape(Bv, Sv, D)
    x = x + _L0_xattn_ref(_layernorm(x, axis=-1), ctx_1024, L0_xattn_Wq, L0_xattn_bq, L0_xattn_Wk, L0_xattn_bk, L0_xattn_Wv, L0_xattn_bv)
    x = x + _L0_attn_ref(_layernorm(x, axis=-1), L0_attn_W_Q, L0_attn_W_K, L0_attn_W_V, L0_attn_W_o)
    x = x + _L0_ffn_ref(_layernorm(x, axis=-1), L0_ffn_gate, L0_ffn_experts_w1, L0_ffn_experts_w2, L0_ffn_experts_w3)
    x = x + _L1_xattn_ref(_layernorm(x, axis=-1), ctx_1024, mask_Bx1x1xS2_ff0, L1_xattn_cq_w, L1_xattn_cq_b, L1_xattn_ck_w, L1_xattn_ck_b, L1_xattn_cv_w, L1_xattn_cv_b, L1_xattn_co_w, L1_xattn_co_b, L1_xattn_co_g, L1_xattn_co_be, L1_xattn_sq_w, L1_xattn_sq_b, L1_xattn_sk_w, L1_xattn_sk_b, L1_xattn_sv_w, L1_xattn_sv_b, L1_xattn_so_w, L1_xattn_so_b, L1_xattn_so_g, L1_xattn_so_be, L1_xattn_fi_w, L1_xattn_fi_b, L1_xattn_fo_w, L1_xattn_fo_b, L1_xattn_fo_g, L1_xattn_fo_be)
    x = x + _L1_attn_ref(_layernorm(x, axis=-1), L1_attn_key, L1_attn_value, L1_attn_in_w, L1_attn_in_b, L1_attn_out_w, L1_attn_out_b)
    x = x + _L1_ffn_ref(_layernorm(x, axis=-1), L1_ffn_W_router, L1_ffn_b_router, L1_ffn_W1, L1_ffn_b1, L1_ffn_W2, L1_ffn_b2)
    return x

_drawn_inputs = setup_inputs


def setup_inputs(seed=0):
    import zlib

    import numpy as np

    out = dict(_drawn_inputs(seed))
    spreads = {'L0_xattn_bq': (0.0, 0.1),
     'L0_xattn_bk': (0.0, 2.0),
     'L0_xattn_bv': (0.0, 0.1),
     'L1_xattn_cq_b': (0.0, 0.329),
     'L1_xattn_ck_b': (0.0, 2.0),
     'L1_xattn_cv_b': (0.0, 0.1),
     'L1_xattn_co_b': (0.0, 0.1),
     'L1_xattn_co_g': (1.0, 0.2),
     'L1_xattn_co_be': (0.0, 0.1),
     'L1_xattn_sq_b': (0.0, 0.37),
     'L1_xattn_sk_b': (0.0, 2.0),
     'L1_xattn_sv_b': (0.0, 0.1),
     'L1_xattn_so_b': (0.0, 0.1),
     'L1_xattn_so_g': (1.0, 0.2),
     'L1_xattn_so_be': (0.0, 0.1),
     'L1_xattn_fi_b': (0.0, 0.1),
     'L1_xattn_fo_b': (0.0, 0.1),
     'L1_xattn_fo_g': (1.0, 0.2),
     'L1_xattn_fo_be': (0.0, 0.1),
     'L1_ffn_b_router': (0.0, 0.1),
     'L1_ffn_b1': (0.0, 0.311),
     'L1_ffn_b2': (0.0, 0.1)}
    factors = {'L0_ffn_gate': 3.18,
     'L0_ffn_experts_w1': 3.101,
     'L0_ffn_experts_w2': 3.078,
     'L0_ffn_experts_w3': 3.225,
     'L1_attn_in_b': 3.643,
     'L1_attn_out_b': 2.997}
    for name, (base, spread) in spreads.items():
        noise = np.random.default_rng([zlib.crc32(name.encode()), seed]).standard_normal(out[name].shape)
        drawn = base * np.exp(spread * noise) if base else spread * noise
        out[name] = jnp.asarray(drawn.astype(out[name].dtype))
    for name, factor in factors.items():
        out[name] = (out[name] * factor).astype(out[name].dtype)
    return out
```

```python
from contextlib import ExitStack

import concourse.bass as bass
from concourse import mybir

F32 = mybir.dt.float32
F32R = mybir.dt.float32r
U32 = mybir.dt.uint32
ALU = mybir.AluOpType
ACT = mybir.ActivationFunctionType
AX = mybir.AxisListType.X
ABSMAX = bass.bass_isa.ReduceOp.max

STOP = "F"

BATCH, SEQ, DIM = 16, 64, 128
TOKENS = BATCH * SEQ
PAIRS = TOKENS // 128
HEADS, HD = 16, 8
KEYS = 1601
FULL = KEYS // 128
TAIL = KEYS - FULL * 128
KT = FULL + 1
KPAD = KEYS + 1
CHUNKS = [(0, 512), (512, 512), (1024, 512), (1536, KPAD - 1536)]
EXPERTS, FF = 8, 512
FC = FF // 128
EPS = 1e-5
QMAX = 127.0
ROUND = 12582912.0
NEG = -1e30

C_ID, C_HM, C_VM2, C_VM4, C_CAUSAL, C_BLK, C_QM, C_SEL, C_OM, C_IOTA, C_KROW, C_QROW, C_HALF, C_END = (
    0, 128, 144, 272, 400, 464, 496, 500, 628, 630, 638, 639, 640, 641)


class Progress:

    def __init__(self, sem, steps):
        self.sem, self.at, self.n = sem, {s: k + 1 for k, s in enumerate(steps)}, len(steps)
        assert len(self.at) == self.n
        self.order = list(steps)

    def done(self, ins, step):
        assert self.order and self.order[0] == step, (step, self.order[:1])
        self.order.pop(0)
        ins.then_inc(self.sem, 1)

    def value(self, step, i=0):
        return i * self.n + self.at[step]


def build(nc, A, out, scratch, mask_parts):
    ctx = ExitStack()
    with ctx:
        def sb(name, shape, dt=F32):
            return ctx.enter_context(nc.sbuf_tensor(name, shape, dt))

        def sem(name):
            return ctx.enter_context(nc.semaphore(name))

        PS = ctx.enter_context(nc.psum_tensor("PS", [128, 8 * 512], F32))

        def bank(k, n=512, parts=128):
            return PS[0:parts, 512 * k:512 * k + n]

        consts = sb("consts", [128, C_END])
        ident = consts[:, C_ID:C_ID + 128]
        head_mask = consts[:, C_HM:C_HM + 16]
        causal = consts[:, C_CAUSAL:C_CAUSAL + 64]
        block_mask = consts[:, C_BLK:C_BLK + 32]
        minus_half = consts[:, C_HALF:C_HALF + 1]
        iota8 = consts[:, C_IOTA:C_IOTA + 8]

        W = {}
        for name in ("L0_xattn_Wq", "L0_xattn_Wk", "L0_xattn_Wv", "L0_attn_W_Q", "L0_attn_W_K", "L0_attn_W_V",
                     "L0_attn_W_o", "L1_xattn_cq_w", "L1_xattn_ck_w", "L1_xattn_cv_w", "L1_xattn_sq_w",
                     "L1_xattn_sk_w", "L1_xattn_sv_w", "L1_xattn_so_w", "L1_attn_out_w"):
            W[name] = sb("w_" + name, [128, 128])
        W["L1_xattn_fi_w"] = sb("w_fi", [128, FF])
        W["L1_xattn_fo_w"] = sb("w_fo", [128, FC, 128])
        W["L1_attn_in_w"] = sb("w_in", [128, 3, 128])
        W["L0_ffn_gate"] = sb("w_gate", [128, EXPERTS])
        W["L1_ffn_W_router"] = sb("w_router", [128, EXPERTS])
        W["L1_ffn_b2"] = sb("w_b2", [EXPERTS, 128])
        co_w = sb("co_w", [128, 2, 128])
        COLS = {}
        for name, n in (("L0_xattn_bq", 1), ("L0_xattn_bk", 1), ("L1_xattn_cq_b", 1), ("L1_xattn_ck_b", 1),
                        ("L1_xattn_sq_b", 1), ("L1_xattn_sk_b", 1), ("L1_xattn_fi_b", FC), ("L1_attn_in_b", 3)):
            COLS[name] = sb("c_" + name, [128, n])
        cv_b = sb("cv_b", [128, 2])
        ROWS = {}
        for name in ("L0_xattn_bv", "L1_xattn_sv_b", "L1_xattn_co_b", "L1_xattn_co_g", "L1_xattn_co_be",
                     "L1_xattn_so_b", "L1_xattn_so_g", "L1_xattn_so_be", "L1_xattn_fo_b", "L1_xattn_fo_g",
                     "L1_xattn_fo_be", "L1_attn_out_b"):
            ROWS[name] = sb("r_" + name, [128, 128])
        router_b = sb("router_b", [128, EXPERTS])

        x = sb("x", [128, PAIRS, 128])
        xn = sb("xn", [128, 128])
        xnT = sb("xnT", [128, 128])
        xT_all = sb("xT_all", [128, TOKENS])
        tok_w = sb("tok_w", [128, PAIRS, EXPERTS])

        stats = sb("stats", [128, 6])
        mv = sb("mv", [128, 2])
        var_eps = sb("var_eps", [128, 1])
        rstd = sb("rstd", [128, 1])

        qT = sb("qT", [128, 128])
        kbd = sb("kbd", [128, 2048])
        vbd = sb("vbd", [128, 512])
        pr = sb("pr", [128, 1024])
        prT = sb("prT", [128, 1024])
        smax = sb("smax", [128, HEADS])
        ssum = sb("ssum", [128, HEADS])
        o_sb = sb("o_sb", [128, 128])
        oT = sb("oT", [128, 128])

        ctx_nat = sb("ctx_nat", [128, 2, KT, 128])
        ctxT = sb("ctxT", [128, 2, KPAD])
        P0 = sb("P0", [128, KEYS])
        P0T = sb("P0T", [128, KT, 128])
        WqT = sb("WqT", [128, 128])
        WvT = sb("WvT", [128, 128])
        l0q = sb("l0q", [128, 128])
        l0qk = sb("l0qk", [128, 128])
        l0s = sb("l0s", [128, 8])
        pcT = sb("pcT", [128, 128])

        kh = sb("kh", [128, KPAD], F32R)
        kl = sb("kl", [128, KPAD], F32R)
        KS = sb("KS", [128, 4, KPAD], F32R)
        qf = sb("qf", [128, 128])
        qh = sb("qh", [128, 128], F32R)
        ql = sb("ql", [128, 128], F32R)
        QS = sb("QS", [128, 4, 2, SEQ], F32R)
        QB = sb("QB", [128, 1024], F32R)
        mask_sb = sb("mask_sb", [BATCH, KPAD])
        mask_hi = sb("mask_hi", [BATCH, KPAD], F32R)
        mask_lo = sb("mask_lo", [BATCH, KPAD], F32R)
        VA = sb("VA", [128, KT, HEADS // 2, 32])
        PT = sb("PT", [128, 2, 1024])
        mx = sb("mx", [128, 8, 4])
        nm = sb("nm", [128, 8])
        nmh = sb("nmh", [8, 128], F32R)
        nml = sb("nml", [8, 128], F32R)
        acc_sb = sb("acc_sb", [128, 2, 2, SEQ])
        rsum = sb("rsum", [128, 256])
        onT = sb("onT", [128, 2, 2, SEQ])
        u = sb("u", [128, 128])
        hid = sb("hid", [128, FC, 128])
        t1 = sb("t1", [128, 128])

        w1 = sb("w1", [128, 2, FF])
        w3 = sb("w3", [128, 2, FF])
        w2 = sb("w2", [128, 2, FC, 128])
        b1 = sb("b1", [128, 2, FC])
        g_act = P0[:, 0:1024].rearrange("p (a n) -> p a n", a=2)
        hidT = ctx_nat[:, :, :, :].rearrange("p b k d -> p (b k d)")[:, 0:FC * 512].rearrange("p (c n) -> p c n", c=FC)
        wcol = sb("wcol", [128, 2, PAIRS])
        top8 = sb("top8", [128, 8])
        topi = sb("topi", [128, 8], U32)
        topf = sb("topf", [128, 8])
        tops = sb("tops", [128, 8])
        lg = sb("lg", [128, 8])
        one8 = sb("one8", [128, 8])

        X = ctxT[:, :, :].rearrange("p b k -> p (b k)")[:, 0:3 * TOKENS].rearrange("p (s t) -> p s t", s=3)
        O_all = P0T[:, 0:PAIRS, :]
        nat = ctx_nat[:, :, :, :].rearrange("p b k d -> p (b k d)")
        OT_all = nat[:, 0:TOKENS]
        Y_all = nat[:, TOKENS:2 * TOKENS].rearrange("p (t d) -> p t d", t=PAIRS)
        WiT = sb("WiT", [128, 3, 128])
        WoT = sb("WoT", [128, 128])
        kT_t = sb("kT_t", [128, 128])
        vT_t = sb("vT_t", [128, 128])
        amax = sb("amax", [128, 8])
        gmax = sb("gmax", [128, 8])
        qscale = sb("qscale", [128, 8])
        qinv = sb("qinv", [128, 8])
        unit = sb("unit", [128, 2])
        blank = sb("blank", [128, 1])
        w_t = sb("w_t", [128, EXPERTS])
        w_tT = sb("w_tT", [EXPERTS, 128])

        P = {}

        def progress(name, steps):
            P[name] = Progress(sem(name), steps)

        def at(eng, name, step, i=0):
            eng.wait_ge(P[name].sem, P[name].value(step, i))

        loads = sem("weights_loaded")
        consts_loaded = sem("consts_loaded")
        n_loads = [0]
        x_loaded = sem("x_loaded")
        dve_link = sem("dve_link")
        state = {"links": 0, "base": 0}

        def link(ins):
            ins.then_inc(dve_link, 1)
            state["links"] += 1
            nc.vector.wait_ge(dve_link, state["base"] + state["links"])

        def vdone(ins, name, step, i=0):
            P[name].done(ins, step)
            at(nc.vector, name, step, i)

        def in_loop(i, per_round, body):
            base, start = state["base"], state["links"]
            state["base"], state["links"] = base + start + i * per_round, 0
            body()
            if state["links"] != per_round:
                print("LINKS", state["links"], per_round)
            state["base"], state["links"] = base, start

        def apart():
            nc.vector.memset(blank[:, :], 0.0)

        V, T, S, G = nc.vector, nc.tensor, nc.scalar, nc.gpsimd

        def mm(o, l, r, start=True, stop=True, **k):
            return T.matmul(o, l, r, start=start, stop=stop, **k)

        def ln_vector(src, dst, name, pre, i):
            apart()
            link(V.bn_stats(stats[:, :], src))
            apart()
            link(V.bn_aggr(mv[:, :], stats[:, :]))
            vdone(V.tensor_scalar(var_eps[:, :], mv[:, 1:2], EPS, None, ALU.add), name + "_v", pre + "var", i)
            at(V, name + "_g", pre + "rstd", i)
            return V.tensor_scalar(dst, src, mv[:, 0:1], rstd[:, 0:1], ALU.subtract, ALU.mult)

        def ln_gpsimd(name, pre, i):
            at(G, name + "_v", pre + "var", i)
            P[name + "_g"].done(G.tensor_tensor(rstd[:, :], var_eps[:, :], minus_half, ALU.pow), pre + "rstd")

        def self_tensor(name, pre, i, grp, xT, wv, wo):
            ng, rep = 128 // grp, 128 // grp
            nb = HEADS // rep
            for g in range(ng):
                for r in range(rep):
                    last = mm(PS[r * grp:(r + 1) * grp, 512 + g * 128:512 + (g + 1) * 128],
                              xT[:, g * grp:(g + 1) * grp], wv)
            P[name + "_p"].done(last, pre + "v")
            core_tensor(name, pre, i, grp, wo)

        def core_tensor(name, pre, i, grp, wo):
            ng, rep = 128 // grp, 128 // grp
            nb, width = HEADS // rep, HEADS * grp
            at(T, name + "_v", pre + "kbd", i)
            for g in range(ng):
                for c in range(0, width, 512):
                    last = mm(PS[g * grp:(g + 1) * grp, 1024 + c:1024 + c + 512], qT[:, g * grp:(g + 1) * grp],
                              kbd[:, g * width + c:g * width + c + 512])
            P[name + "_p"].done(last, pre + "s")
            at(T, name + "_a", pre + "exp", i)
            for b in range(nb):
                last = T.transpose(PS[:, 2048 + b * 128:2048 + (b + 1) * 128], pr[:, b * 128:(b + 1) * 128], ident)
            P[name + "_p"].done(last, pre + "pT")
            at(T, name + "_a", pre + "pT", i)
            at(T, name + "_v", pre + "vbd", i)
            for g in range(ng):
                for b in range(nb):
                    last = mm(PS[g * grp:(g + 1) * grp, 3072 + b * rep * HD:3072 + (b + 1) * rep * HD],
                              prT[:, b * 128 + g * grp:b * 128 + (g + 1) * grp],
                              vbd[:, g * 128 + b * rep * HD:g * 128 + (b + 1) * rep * HD])
            P[name + "_p"].done(last, pre + "o")
            if wo is None:
                return
            at(T, name + "_v", pre + "o", i)
            P[name + "_p"].done(T.transpose(bank(7, 128), o_sb[:, :], ident), pre + "oT")
            at(T, name + "_v", pre + "oT", i)
            P[name + "_p"].done(mm(bank(6, 128), oT[:, :], wo), pre + "y")

        def self_scalar(name, pre, i, grp, scale=1.0):
            width = HEADS * grp
            at(S, name + "_v", pre + "sub", i)
            P[name + "_a"].done(S.activation(pr[:, 0:width], pr[:, 0:width], ACT.Exp, scale=scale), pre + "exp")
            at(S, name + "_p", pre + "pT", i)
            P[name + "_a"].done(S.activation(prT[:, 0:width], PS[:, 2048:2048 + width], ACT.Copy), pre + "pT")

        def core_vector(name, pre, i, grp, mask, bias, unit=None):
            width = HEADS * grp
            at(V, name + "_p", pre + "s", i)
            sc = PS[:, 1024:1024 + width].rearrange("p (h k) -> p h k", h=HEADS)
            p3 = pr[:, 0:width].rearrange("p (h k) -> p h k", h=HEADS)
            if mask is not None:
                link(V.tensor_tensor(p3, sc, mask.unsqueeze(1).broadcast_to([128, HEADS, grp]), ALU.add))
                sc = p3
            link(V.reduce_max(smax[:, :], sc, AX))
            vdone(V.tensor_tensor(p3, sc, smax[:, :].unsqueeze(2).broadcast_to([128, HEADS, grp]), ALU.subtract),
                  name + "_v", pre + "sub", i)
            at(V, name + "_a", pre + "exp", i)
            link(V.reduce_sum(ssum[:, :], p3, AX))
            link(V.reciprocal(ssum[:, :], ssum[:, :]))
            if unit is not None:
                link(V.tensor_scalar(ssum[:, :], ssum[:, :], unit, None, ALU.mult))
            at(V, name + "_p", pre + "o", i)
            o3 = o_sb[:, :].rearrange("p (h d) -> p h d", h=HEADS)
            norm = V.tensor_tensor(o3, bank(6, 128).rearrange("p (h d) -> p h d", h=HEADS),
                                   ssum[:, :].unsqueeze(2).broadcast_to([128, HEADS, HD]), ALU.mult)
            if bias is not None:
                link(norm)
                norm = V.tensor_tensor(o_sb[:, :], o_sb[:, :], bias, ALU.add)
            vdone(norm, name + "_v", pre + "o", i)

        def out_vector(name, pre, i):
            at(V, name + "_p", pre + "oT", i)
            vdone(V.tensor_copy(oT[:, :], bank(7, 128)), name + "_v", pre + "oT", i)
            at(V, name + "_p", pre + "y", i)

        def kbd_vector(name, pre, i, grp, k_src, k_bias, v_src):
            ng, rep, width = 128 // grp, 128 // grp, HEADS * grp
            hm = head_mask.unsqueeze(2).broadcast_to([128, HEADS, grp])
            for g in range(ng):
                dst = kbd[:, g * width:(g + 1) * width].rearrange("p (h k) -> p h k", h=HEADS)
                src = k_src[:, g * grp:(g + 1) * grp].unsqueeze(1).broadcast_to([128, HEADS, grp])
                if k_bias is None:
                    last = V.tensor_tensor(dst, src, hm, ALU.mult)
                else:
                    last = V.scalar_tensor_tensor(dst, src, k_bias, hm, ALU.add, ALU.mult)
                if g < ng - 1:
                    link(last)
            vdone(last, name + "_v", pre + "kbd", i)
            at(V, name + "_p", pre + "v", i)
            vm = consts[:, (C_VM2 if rep == 2 else C_VM4):(C_VM2 if rep == 2 else C_VM4) + 128]
            vdone(V.tensor_tensor(vbd[:, 0:ng * 128].rearrange("p (g c) -> p g c", g=ng),
                                  v_src.rearrange("p (g c) -> p g c", g=ng),
                                  vm.unsqueeze(1).broadcast_to([128, ng, 128]), ALU.mult),
                  name + "_v", pre + "vbd", i)

        SELF_P = ["v", "s", "pT", "o"]
        SELF_V = ["kbd", "vbd", "sub", "o"]
        SELF_A = ["exp", "pT"]

        def route_vector(dst, name, pre, i):
            apart()
            link(V.max(top8[:, :], lg[:, :]))
            apart()
            link(V.max_index(topi[:, :], top8[:, :], lg[:, :]))
            link(V.tensor_copy(topf[:, 0:2], topi[:, 0:2]))
            vdone(V.tensor_scalar(tops[:, 0:2], top8[:, 0:2], top8[:, 0:1], None, ALU.subtract),
                  name + "_v", pre + "gap", i)
            at(V, name + "_a", pre + "gate", i)
            link(V.reduce_sum(tops[:, 4:5], tops[:, 2:4], AX))
            link(V.reciprocal(tops[:, 5:6], tops[:, 4:5]))
            link(V.tensor_scalar(tops[:, 6:8], tops[:, 2:4], tops[:, 5:6], None, ALU.mult))
            link(V.tensor_scalar(one8[:, :], iota8, topf[:, 0:1], tops[:, 6:7], ALU.is_equal, ALU.mult))
            link(V.tensor_scalar(lg[:, :], iota8, topf[:, 1:2], tops[:, 7:8], ALU.is_equal, ALU.mult))
            return V.tensor_tensor(dst, one8[:, :], lg[:, :], ALU.add)

        def route_scalar(name, pre, i):
            at(S, name + "_v", pre + "gap", i)
            P[name + "_a"].done(S.activation(tops[:, 2:4], tops[:, 0:2], ACT.Exp), pre + "gate")

        CH = range(FC)
        JT = [(j, t) for j in range(2) for t in range(2)]

        def moe_progress(name, gated):
            progress(name + "_p", [s for j, t in JT for s in [f"h{j}{t}{c}" for c in CH] + [f"y{j}{t}"]])
            progress(name + "_a", [f"h{j}{t}{c}" for j, t in JT for c in CH])
            progress(name + "_v", [s for j, t in JT for s in ([f"w{j}"] if t == 0 else [])
                                   + ([f"h{j}{t}{c}" for c in CH] if gated else []) + [f"y{j}{t}"]])
            P[name + "_w"] = [sem(name + f"_weights{j}") for j in range(2)]

        def moe_load(name, srcs, e, j):
            W1, W3, W2, B1 = srcs
            ld = P[name + "_w"][j]

            def dma(dst, src):
                nc.sync.dma_start(dst, src).then_inc(ld, 16)

            dma(w1[:, j, :], W1[bass.ds(e, 1), :, :].rearrange("e h f -> (e h) f"))
            dma(w2[:, j, :, :], W2[bass.ds(e, 1), :, :].rearrange("e (c p) n -> p (e c) n", p=128))
            if W3 is not None:
                dma(w3[:, j, :], W3[bass.ds(e, 1), :, :].rearrange("e h f -> (e h) f"))
            else:
                dma(b1[:, j, :], B1[bass.ds(e, 1), :].rearrange("e (c p) -> p (e c)", p=128))

        def moe_sync(sp, name, srcs):
            for j in range(2):
                moe_load(name, srcs, j, j)
            with sp.Fori(0, EXPERTS // 2 - 1) as i:
                for j in range(2):
                    at(sp, name + "_p", f"y{j}1", i)
                    moe_load(name, srcs, 2 * i + 2 + j, j)

        def moe_tensor(name, gated, i):
            used = name + ("_v" if gated else "_a")
            for n, (j, t) in enumerate(JT):
                if t == 0:
                    T.wait_ge(P[name + "_w"][j], 48 * i + 48)
                toks = xT_all[:, t * 512:(t + 1) * 512]
                for c in CH:
                    if c >= 2:
                        at(T, used, f"h{j}{t}{c - 2}", i)
                    elif n:
                        at(T, used, "h%d%d%d" % (*JT[n - 1], c + 2), i)
                    else:
                        T.wait_ge(P[used].sem, i * P[used].n)
                    b = 2 * (c % 2)
                    last = mm(bank(b), w1[:, j, c * 128:(c + 1) * 128], toks)
                    if gated:
                        last = mm(bank(b + 1), w3[:, j, c * 128:(c + 1) * 128], toks)
                    P[name + "_p"].done(last, f"h{j}{t}{c}")
                at(T, used, f"h{j}{t}3", i)
                if n >= 2:
                    at(T, name + "_v", "y%d%d" % JT[n - 2], i)
                else:
                    T.wait_ge(P[name + "_v"].sem, i * P[name + "_v"].n)
                for q in range(4):
                    for c in CH:
                        last = mm(PS[:, 512 * (4 + t) + q * 128:512 * (4 + t) + (q + 1) * 128],
                                  hidT[:, c, q * 128:(q + 1) * 128], w2[:, j, c, :], start=c == 0, stop=c == FC - 1)
                P[name + "_p"].done(last, f"y{j}{t}")

        def moe_scalar(name, gated, i):
            for j, t in JT:
                for c in CH:
                    at(S, name + "_p", f"h{j}{t}{c}", i)
                    if gated:
                        ins = S.activation(g_act[:, c % 2, :], bank(2 * (c % 2)), ACT.Silu)
                    else:
                        ins = S.activation(hidT[:, c, :], bank(2 * (c % 2)), ACT.Relu, bias=b1[:, j, c:c + 1])
                    P[name + "_a"].done(ins, f"h{j}{t}{c}")

        def moe_vector(name, gated, i):
            for j, t in JT:
                if t == 0:
                    vdone(V.tensor_copy(wcol[:, j, :].unsqueeze(2), tok_w[:, :, bass.ds(2 * i + j, 1)]), name + "_v", f"w{j}", i)
                if gated:
                    for c in CH:
                        at(V, name + "_a", f"h{j}{t}{c}", i)
                        P[name + "_v"].done(V.tensor_tensor(hidT[:, c, :], g_act[:, c % 2, :],
                                                            bank(2 * (c % 2) + 1), ALU.mult), f"h{j}{t}{c}")
                at(V, name + "_p", f"y{j}{t}", i)
                for q in range(4):
                    last = V.scalar_tensor_tensor(x[:, 4 * t + q, :],
                                                  PS[:, 512 * (4 + t) + q * 128:512 * (4 + t) + (q + 1) * 128],
                                                  wcol[:, j, 4 * t + q:4 * t + q + 1], x[:, 4 * t + q, :],
                                                  ALU.mult, ALU.add)
                    if q < 3:
                        link(last)
                vdone(last, name + "_v", f"y{j}{t}", i)

        QUANT = ["wi", "wo", "X", "Q", "O", "Y"]

        TG = [(0, 4), (4, 4), (8, 4), (12, 1)]
        progress("pre_p", ["WqT", "WvT"])
        progress("pre_v", ["WqT", "WvT"])
        progress("l0_p", ["xT", "q", "qk"] + [f"ct{b}{n}" for b in range(2) for n in range(4)] + ["s"]
                 + [f"p{n}" for n in range(4)] + ["pc", "y"] + ["axT", "aqk"] + ["a" + s for s in SELF_P + ["oT", "y"]]
                 + ["gxT", "glog"])
        progress("l0_v", ["var", "xn", "xT", "q", "qk", "max", "pc"] + ["avar", "axn", "axT", "aq"]
                 + ["a" + s for s in SELF_V + ["oT"]] + ["gvar", "gxn", "gxT", "ggap", "gend"])
        progress("l0_g", ["rstd", "arstd", "grstd"])
        progress("l0_a", [f"ct{b}{n}" for b in range(2) for n in range(4)] + ["exp"] + [f"p{n}" for n in range(4)]
                 + ["a" + s for s in SELF_A] + ["ggate"])
        ctx_loaded = sem("ctx_loaded")
        ctxT_saved = sem("ctxT_saved")

        XS = ["var", "xn", "xT", "q", "qh", "ql"]
        for_b = lambda f: [s for b in range(2) for s in f(b)]
        progress("l1_p", ["xT", "q"]
                 + for_b(lambda b: [f"k{b}{c}" for c in range(4)] + [f"v{b}{n}" for n in range(4)]
                         + [f"m{b}{p}{c}" for p in range(8) for c in range(4)] + [f"nm{b}"]
                         + [f"s{b}{k}" for k in range(KT)] + [f"pv{b}{k}" for k in range(KT)][:0] + [f"acc{b}", f"sum{b}"])
                 + ["cy", "sxT", "sqk"] + ["s" + s for s in SELF_P + ["oT", "y"]] + ["fxT"]
                 + [f"f{c}" for c in range(FC)] + ["fy"])
        P["l1_pv"] = Progress(sem("l1_pv"), [f"pv{b}{k}" for b in range(2) for k in range(KT)])
        progress("l1_v", XS + for_b(lambda b: [f"kl{b}{c}" for c in range(4)] + [f"qb{b}"]
                                    + [f"m{b}{p}{c}" for p in range(8) for c in range(4)] + [f"nm{b}", f"nmh{b}", f"nml{b}", f"on{b}"])
                 + ["cvar", "cx", "sxT", "sq"] + ["s" + s for s in SELF_V + ["oT"]] + ["svar", "sx", "fxT", "fvar", "fx"])
        progress("l1_g", ["rstd", "crstd", "srstd", "frstd"])
        progress("l1_a", for_b(lambda b: [f"kh{b}{c}" for c in range(4)] + [f"v{b}{n}" for n in range(4)]
                               + [f"e{b}{k}" for k in range(KT)] + [f"acc{b}"]) + ["s" + s for s in SELF_A]
                 + [f"f{c}" for c in range(FC)])
        ctxT_loaded = sem("ctxT_loaded")
        qs_stacked = sem("qs_stacked")
        ks_stacked = sem("ks_stacked")
        nm_stacked = sem("nm_stacked")
        mask_split = sem("mask_split")
        mask_saved = sem("mask_saved")

        moe_progress("e0", True)
        moe_progress("e1", False)

        TS = range(PAIRS)
        progress("qw_v", ["wi", "wo", "quantised", "wiT"])
        progress("qw_p", ["wiT", "woT"])
        progress("qn_v", ["var", "xn", "xT"])
        progress("qn_p", ["xT"])
        progress("qn_g", ["rstd"])
        progress("qx_p", [f"X{s}{h}" for s in range(3) for h in range(2)])
        progress("qx_v", ["X", "Q", "O", "Y", "x"])
        progress("q_all", ["wi", "wo", "X", "Q", "O", "Y"])
        progress("qa_v", ["load"] + SELF_V + ["saved"])
        progress("qa_p", SELF_P)
        progress("qa_a", SELF_A)
        progress("qo_v", ["Oint"] + [f"{s}{t}" for s in ("oT", "y") for t in TS])
        progress("qo_p", [f"{s}{t}" for s in ("oT", "y") for t in TS])
        progress("r_v", ["var", "xn", "xT", "gap", "w", "wT", "end"])
        progress("r_p", ["xT", "log", "wT", "b2"])
        progress("r_g", ["rstd"])
        progress("r_a", ["gate"])
        stored = sem("stored")
        consts_ready = sem("consts_ready")

        ctx.enter_context(nc.allow_non_contiguous_dma(reason="bias columns"))
        block = ctx.enter_context(nc.Block())
        ctx_in = A["ctx_1024"]
        x_view = A["x"].rearrange("b s d -> (b s) d").rearrange("(t p) d -> p t d", p=128)
        out_view = out.rearrange("b s d -> (b s) d").rearrange("(t p) d -> p t d", p=128)
        last_stage = "ABCDEF".index(STOP)

        WLOADS = []
        for name, t in W.items():
            src = A[name]
            if name == "L1_xattn_fo_w":
                src = src.rearrange("(c p) n -> p c n", p=128)
            elif name == "L1_attn_in_w":
                src = src.rearrange("(c p) n -> p c n", p=128)
            WLOADS.append((t, src))
        for name, t in COLS.items():
            WLOADS.append((t, A[name].rearrange("(c p) -> p c", p=128)))
        for name, t in ROWS.items():
            WLOADS.append((t, A[name].partition_broadcast(128)))
        WLOADS.append((router_b, A["L1_ffn_b_router"].partition_broadcast(128)))
        N_W = len(WLOADS) + 1 + 16
        N_ZERO = 8

        @block.sync
        def _(sp):
            sp.dma_start(x[:, :, :], x_view).then_inc(x_loaded, 16)
            sp.dma_start(consts[:, :], A["consts"]).then_inc(consts_loaded, 16)
            for t, src in WLOADS:
                dst = t[:, :, :] if len(t.shape) == 3 else t[:, :]
                sp.dma_start(dst, src).then_inc(loads, 16)
            sp.dma_start(mask_sb[:, 0:KEYS], A["mask_Bx1x1xS2_ff0"].rearrange("b o q k -> b (o q k)")).then_inc(loads, 16)
            sp.wait_ge(consts_ready, 1)
            for r in range(2):
                for j in range(4):
                    ch = 16 * (4 * r + j)
                    sp.dma_start(co_w[32 * j:32 * j + 16, r, :], A["L1_xattn_co_w"][ch:ch + 16, :]).then_inc(loads, 16)
                    sp.dma_start(cv_b[32 * j:32 * j + 16, r:r + 1],
                                 A["L1_xattn_cv_b"][ch:ch + 16].rearrange("(p a) -> p a", a=1)).then_inc(loads, 16)
            with sp.Fori(0, PAIRS) as i:
                sp.wait_ge(P["l0_v"].sem, i * P["l0_v"].n)
                for b in range(2):
                    row = ctx_in[bass.ds(2 * i + b, 1), :, :].rearrange("b k d -> (b k) d")
                    sp.dma_start(ctx_nat[:, b, 0:FULL, :], row[0:FULL * 128, :].rearrange("(p t) d -> p t d", t=FULL)
                                 ).then_inc(ctx_loaded, 16)
                    sp.dma_start(ctx_nat[0:TAIL, b, FULL, :], row[FULL * 128:KEYS, :]).then_inc(ctx_loaded, 16)
                for b in range(2):
                    at(sp, "l0_a", f"ct{b}3", i)
                    sp.dma_start(scratch[bass.ds(2 * i + b, 1), :, :].rearrange("b p k -> (b p) k"), ctxT[:, b, 0:KEYS]
                                 ).then_inc(ctxT_saved, 16)
            if last_stage >= 2:
                moe_sync(sp, "e0", (A["L0_ffn_experts_w1"], A["L0_ffn_experts_w3"], A["L0_ffn_experts_w2"], None))
            if last_stage >= 3:
                sp.wait_ge(ctxT_saved, 16 * BATCH)
                sp.wait_ge(mask_split, 3)
                for k, src in enumerate((mask_hi, mask_lo)):
                    sp.dma_start(mask_parts[k], src[:, :].bitcast(F32)).then_inc(mask_saved, 16)
                sp.wait_ge(mask_saved, 32)
                sp.wait_ge(consts_ready, 2)
                with sp.Fori(0, PAIRS) as i:
                    sp.wait_ge(P["l1_v"].sem, i * P["l1_v"].n)
                    for b in range(2):
                        sp.dma_start(ctxT[:, b, 0:KEYS], scratch[bass.ds(2 * i + b, 1), :, :].rearrange("b p k -> (b p) k")
                                     ).then_inc(ctxT_loaded, 16)
                    at(sp, "l1_v", "ql", i)
                    for k, src in enumerate((qh, ql, qh)):
                        for g in range(4):
                            sp.dma_start(QS[32 * k:32 * k + 32, g, :, :].rearrange("p b q -> p (b q)").bitcast(F32),
                                         src[32 * g:32 * g + 32, :].bitcast(F32)).then_inc(qs_stacked, 16)
                    for b in range(2):
                        at(sp, "l1_v", f"kl{b}3", i)
                        for k, src in enumerate((kh, kh, kl)):
                            for g in range(4):
                                sp.dma_start(KS[32 * k:32 * k + 32, g, 0:KEYS].bitcast(F32), src[32 * g:32 * g + 32, 0:KEYS].bitcast(F32)
                                             ).then_inc(ks_stacked, 16)
                        for k in range(2):
                            for g in range(4):
                                sp.dma_start(KS[98 + k:99 + k, g, :].bitcast(F32),
                                             mask_parts[k:k + 1, bass.ds(2 * i + b, 1), :].rearrange("k b n -> (k b) n")
                                             ).then_inc(ks_stacked, 16)
                        at(sp, "l1_v", f"nml{b}", i)
                        sp.dma_start(QB[96:97, :].rearrange("a (p c) -> a p c", p=8).bitcast(F32), nmh[:, :].bitcast(F32)).then_inc(nm_stacked, 16)
                        sp.dma_start(QB[97:98, :].rearrange("a (p c) -> a p c", p=8).bitcast(F32), nml[:, :].bitcast(F32)).then_inc(nm_stacked, 16)
            if last_stage >= 5:
                sp.wait_ge(P["e0_v"].sem, 4 * P["e0_v"].n)
                moe_sync(sp, "e1", (A["L1_ffn_W1"], None, A["L1_ffn_W2"], A["L1_ffn_b1"]))
            if last_stage >= 5:
                sp.wait_ge(P["e1_v"].sem, 4 * P["e1_v"].n)
            elif last_stage == 4:
                sp.wait_ge(P["qx_v"].sem, P["qx_v"].n)
            elif last_stage == 3:
                sp.wait_ge(P["l1_v"].sem, PAIRS * P["l1_v"].n)
            elif last_stage == 2:
                sp.wait_ge(P["e0_v"].sem, 4 * P["e0_v"].n)
            else:
                sp.wait_ge(P["l0_v"].sem, PAIRS * P["l0_v"].n)
            sp.dma_start(out_view, x[:, :, :]).then_inc(stored, 16)
            sp.wait_ge(stored, 16)
            sp.wait_ge(ctxT_saved, 16 * BATCH)

        @block.gpsimd
        def _(g):
            G.memset(co_w[:, :, :], 0.0)
            G.memset(cv_b[:, :], 0.0).then_inc(consts_ready, 1)
            G.memset(VA[:, :, :, :], 1.0).then_inc(consts_ready, 1)
            g.wait_ge(consts_loaded, 16)
            with g.Fori(0, PAIRS) as i:
                for pre in ("", "a", "g"):
                    ln_gpsimd("l0", pre, i)
            if last_stage >= 3:
                with g.Fori(0, PAIRS) as i:
                    for pre in ("", "c", "s", "f"):
                        ln_gpsimd("l1", pre, i)
            if last_stage >= 4:
                def all_max(k, step, stage):
                    at(G, stage, step)
                    P["q_all"].done(G.partition_all_reduce(gmax[:, k:k + 1], amax[:, k:k + 1], 128, ABSMAX),
                                    QUANT[k])

                all_max(0, "wi", "qw_v")
                all_max(1, "wo", "qw_v")
                with g.Fori(0, PAIRS) as i:
                    ln_gpsimd("qn", "", i)
                all_max(2, "X", "qx_v")
                all_max(3, "Q", "qx_v")
                all_max(4, "O", "qx_v")
                all_max(5, "Y", "qx_v")
            if last_stage >= 5:
                with g.Fori(0, PAIRS) as i:
                    ln_gpsimd("r", "", i)

        @block.scalar
        def _(act):
            act.wait_ge(loads, 16 * N_W)
            act.wait_ge(consts_loaded, 16)
            with act.Fori(0, PAIRS) as i:
                for b in range(2):
                    for n, (k0, k) in enumerate(TG):
                        at(S, "l0_p", f"ct{b}{n}", i)
                        w = 512 if n < 3 else TAIL
                        P["l0_a"].done(S.activation(ctxT[:, b, k0 * 128:k0 * 128 + w], bank(4 + n % 2, w), ACT.Copy), f"ct{b}{n}")
                at(S, "l0_v", "max", i)
                P["l0_a"].done(S.activation(P0[:, :], PS[:, 0:KEYS], ACT.Exp, bias=l0s[:, 3:4],
                                            scale=float(DIM) ** -0.5, accum_out=l0s[:, 4:5]), "exp")
                for n, (k0, k) in enumerate(TG):
                    at(S, "l0_p", f"p{n}", i)
                    rows = 128 if n < 3 else TAIL
                    P["l0_a"].done(S.activation(P0T[0:rows, k0:k0 + k, :].rearrange("p k q -> p (k q)"),
                                                bank(4 + n % 2, 128 * k, rows), ACT.Copy), f"p{n}")
                self_scalar("l0", "a", i, SEQ)
                route_scalar("l0", "g", i)
            if last_stage >= 2:
                with act.Fori(0, EXPERTS // 2) as i:
                    moe_scalar("e0", True, i)
            if last_stage >= 3:
                with act.Fori(0, PAIRS) as i:
                    for b in range(2):
                        for c, (c0, cw) in enumerate(CHUNKS):
                            cw = min(cw, KEYS - c0)
                            at(S, "l1_p", f"k{b}{c}", i)
                            P["l1_a"].done(S.activation(kh[:, c0:c0 + cw], bank(7 if c % 2 else 6, cw), ACT.Identity,
                                                        bias=COLS["L1_xattn_ck_b"][:, 0:1]), f"kh{b}{c}")
                        for n, (k0, k) in enumerate(TG):
                            at(S, "l1_p", f"v{b}{n}", i)
                            rows = 128 if n < 3 else TAIL
                            P["l1_a"].done(S.activation(VA[0:rows, k0:k0 + k, :, 0:16],
                                                        bank(7 if n % 2 else 6, 128 * k, rows)
                                                        .rearrange("p (k h c) -> p k h c", k=k, h=8), ACT.Copy), f"v{b}{n}")
                        for k in range(KT):
                            rows = 128 if k < FULL else TAIL
                            at(S, "l1_p", f"s{b}{k}", i)
                            if k >= 2:
                                at(S, "l1_pv", f"pv{b}{k - 2}", i)
                            P["l1_a"].done(S.activation(PT[0:rows, k % 2, :], PS[0:rows, 1024 + 1024 * (k % 2):2048 + 1024 * (k % 2)],
                                                        ACT.Exp), f"e{b}{k}")
                        at(S, "l1_p", f"acc{b}", i)
                        P["l1_a"].done(S.activation(acc_sb[:, :, :, :].rearrange("p r h q -> p (r h q)"), bank(6, 256), ACT.Copy), f"acc{b}")
                    self_scalar("l1", "s", i, SEQ)
                    for c in range(FC):
                        at(S, "l1_p", f"f{c}", i)
                        P["l1_a"].done(S.activation(hid[:, c, :], bank(c, 128), ACT.Gelu,
                                                    bias=COLS["L1_xattn_fi_b"][:, c:c + 1]), f"f{c}")
            if last_stage >= 4:
                with act.Fori(0, PAIRS) as i:
                    self_scalar("qa", "", i, 32, unit[:, 0:1])
            if last_stage >= 5:
                with act.Fori(0, PAIRS) as i:
                    route_scalar("r", "", i)
                with act.Fori(0, EXPERTS // 2) as i:
                    moe_scalar("e1", False, i)

        @block.tensor
        def _(pe):
            pe.wait_ge(loads, 16 * N_W)
            pe.wait_ge(consts_loaded, 16)
            P["pre_p"].done(T.transpose(bank(6, 128), W["L0_xattn_Wq"][:, :], ident), "WqT")
            P["pre_p"].done(T.transpose(bank(7, 128), W["L0_xattn_Wv"][:, :], ident), "WvT")
            at(T, "pre_v", "WvT")
            with pe.Fori(0, PAIRS) as i:
                name = "l0_p"
                at(T, "l0_v", "xn", i)
                P[name].done(T.transpose(bank(7, 128), xn[:, :], ident), "xT")
                at(T, "l0_v", "xT", i)
                P[name].done(mm(bank(6, 128), WqT[:, :], xnT[:, :]), "q")
                at(T, "l0_v", "q", i)
                mm(bank(7, 128), W["L0_xattn_Wk"][:, :], l0q[:, :])
                P[name].done(mm(PS[:, 512 * 7 + 256:512 * 7 + 257], l0q[:, :], COLS["L0_xattn_bk"][:, :]), "qk")
                pe.wait_ge(ctx_loaded, 64 * i + 64)
                for b in range(2):
                    for n, (k0, k) in enumerate(TG):
                        m = 4 * b + n
                        if m >= 2:
                            at(T, "l0_a", f"ct{(m - 2) // 4}{(m - 2) % 4}", i)
                        for q in range(k):
                            rows = 128 if k0 + q < FULL else TAIL
                            last = T.transpose(PS[:, 512 * (4 + n % 2) + 128 * q:512 * (4 + n % 2) + 128 * q + rows],
                                               ctx_nat[0:rows, b, k0 + q, :], consts[0:rows, C_ID:C_ID + rows])
                        P[name].done(last, f"ct{b}{n}")
                at(T, "l0_v", "qk", i)
                at(T, "l0_a", "ct13", i)
                for b in range(2):
                    for c0 in range(0, KEYS, 512):
                        w = min(512, KEYS - c0)
                        last = mm(PS[64 * b:64 * b + 64, c0:c0 + w], l0qk[:, 64 * b:64 * b + 64], ctxT[:, b, c0:c0 + w])
                P[name].done(last, "s")
                at(T, "l0_a", "exp", i)
                for n, (k0, k) in enumerate(TG):
                    if n >= 2:
                        at(T, "l0_a", f"p{n - 2}", i)
                    rows = 128 if n < 3 else TAIL
                    for q in range(k):
                        last = T.transpose(PS[0:rows, 512 * (4 + n % 2) + 128 * q:512 * (4 + n % 2) + 128 * q + 128],
                                           P0[:, (k0 + q) * 128:(k0 + q) * 128 + rows], ident)
                    P[name].done(last, f"p{n}")
                at(T, "l0_a", "p3", i)
                for b in range(2):
                    for k in range(KT):
                        rows = 128 if k < FULL else TAIL
                        last = mm(PS[:, 3072 + 64 * b:3136 + 64 * b], ctx_nat[0:rows, b, k, :], P0T[0:rows, k, 64 * b:64 * b + 64],
                                  start=k == 0, stop=k == KT - 1)
                P[name].done(last, "pc")
                at(T, "l0_v", "pc", i)
                P[name].done(mm(bank(7, 128), pcT[:, :], WvT[:, :]), "y")
                at(T, "l0_v", "axn", i)
                P[name].done(T.transpose(bank(7, 128), xn[:, :], ident), "axT")
                at(T, "l0_v", "axT", i)
                mm(PS[:, 0:128], W["L0_attn_W_Q"][:, :], xnT[:, :])
                P[name].done(mm(PS[:, 128:256], W["L0_attn_W_K"][:, :], xnT[:, :]), "aqk")
                self_tensor("l0", "a", i, SEQ, xnT, W["L0_attn_W_V"][:, :], W["L0_attn_W_o"][:, :])
                at(T, "l0_v", "gxn", i)
                P[name].done(T.transpose(bank(7, 128), xn[:, :], ident), "gxT")
                at(T, "l0_v", "gxT", i)
                P[name].done(mm(bank(6, EXPERTS), xnT[:, :], W["L0_ffn_gate"][:, :]), "glog")
            if last_stage >= 2:
                pe.wait_ge(P["l0_v"].sem, PAIRS * P["l0_v"].n)
                with pe.Fori(0, EXPERTS // 2) as i:
                    moe_tensor("e0", True, i)
            if last_stage >= 3:
                pe.wait_ge(P["e0_v"].sem, 4 * P["e0_v"].n)
                pe.wait_ge(consts_ready, 2)
                with pe.Fori(0, PAIRS) as i:
                    name = "l1_p"
                    at(T, "l1_v", "xn", i)
                    P[name].done(T.transpose(bank(7, 128), u[:, :], ident), "xT")
                    at(T, "l1_v", "xT", i)
                    P[name].done(mm(bank(6, 128), W["L1_xattn_cq_w"][:, :], xnT[:, :]), "q")
                    at(T, "l1_v", "ql", i)
                    for b in range(2):
                        pe.wait_ge(ctxT_loaded, 32 * i + 32)
                        for c, (c0, cw) in enumerate(CHUNKS):
                            cw = min(cw, KEYS - c0)
                            if c >= 2:
                                at(T, "l1_v", f"kl{b}{c - 2}", i)
                            elif b:
                                at(T, "l1_a", "acc0", i)
                                at(T, "l1_v", "on0", i)
                            P[name].done(mm(bank(7 if c % 2 else 6, cw), W["L1_xattn_ck_w"][:, :], ctxT[:, b, c0:c0 + cw]), f"k{b}{c}")
                        for n, (k0, k) in enumerate(TG):
                            if n < 2:
                                at(T, "l1_v", f"kl{b}{n + 2}", i)
                            else:
                                at(T, "l1_a", f"v{b}{n - 2}", i)
                            for q in range(k):
                                rows = 128 if k0 + q < FULL else TAIL
                                kc = (k0 + q) * 128
                                o = 512 * (7 if n % 2 else 6) + 128 * q
                                last = mm(PS[0:rows, o:o + 128], ctxT[:, b, kc:kc + rows], W["L1_xattn_cv_w"][:, :])
                            P[name].done(last, f"v{b}{n}")
                        at(T, "l1_v", f"qb{b}", i)
                        pe.wait_ge(ks_stacked, (2 * i + b + 1) * 16 * 20)
                        for p in range(8):
                            for c, (c0, cw) in enumerate(CHUNKS):
                                m = 4 * p + c
                                if m >= 2:
                                    at(T, "l1_v", f"m{b}{(m - 2) // 4}{(m - 2) % 4}", i)
                                P[name].done(mm(bank(m % 2, cw), QB[:, 128 * p:128 * p + 128], KS[:, p // 2, c0:c0 + cw]), f"m{b}{p}{c}")
                        at(T, "l1_v", f"nm{b}", i)
                        at(T, "l1_a", f"v{b}3", i)
                        P[name].done(T.transpose(bank(7, 128, 8), nm[:, :], ident), f"nm{b}")
                        pe.wait_ge(nm_stacked, (2 * i + b + 1) * 32)

                        def values(k):
                            rows = 128 if k < FULL else TAIL
                            at(T, "l1_a", f"e{b}{k}", i)
                            for r in range(2):
                                for j in range(4):
                                    p = 4 * r + j
                                    last = mm(PS[32 * j:32 * j + 32, 3072 + 128 * r:3200 + 128 * r], VA[0:rows, k, p, :],
                                              PT[0:rows, k % 2, 128 * p:128 * p + 128], start=k == 0 and r == 0,
                                              stop=k == KT - 1, skip_group_check=True, tile_position=(0, 32 * j))
                            P["l1_pv"].done(last, f"pv{b}{k}")

                        for k in range(KT):
                            rows = 128 if k < FULL else TAIL
                            if k >= 2:
                                at(T, "l1_a", f"e{b}{k - 2}", i)
                            for g in range(4):
                                o = 1024 + 1024 * (k % 2) + 256 * g
                                last = mm(PS[0:rows, o:o + 256], KS[:, g, 128 * k:128 * k + rows], QB[:, 256 * g:256 * g + 256])
                            P[name].done(last, f"s{b}{k}")
                            if k:
                                values(k - 1)
                        values(KT - 1)
                        P[name].done(mm(bank(7, 2), ident, consts[:, 0:2]), f"acc{b}")
                        at(T, "l1_a", f"acc{b}", i)
                        P[name].done(mm(bank(7, 256), consts[:, C_SEL:C_SEL + 128],
                                        acc_sb[:, :, :, :].rearrange("p r h q -> p (r h q)")), f"sum{b}")
                    at(T, "l1_v", "on1", i)
                    for r in range(2):
                        last = mm(bank(6, 128), onT[:, r, :, :].rearrange("p b q -> p (b q)"), co_w[:, r, :], start=r == 0, stop=r == 1)
                    P[name].done(last, "cy")
                    at(T, "l1_v", "cx", i)
                    P[name].done(T.transpose(bank(7, 128), u[:, :], ident), "sxT")
                    at(T, "l1_v", "sxT", i)
                    mm(PS[:, 0:128], W["L1_xattn_sq_w"][:, :], xnT[:, :])
                    P[name].done(mm(PS[:, 128:256], W["L1_xattn_sk_w"][:, :], xnT[:, :]), "sqk")
                    self_tensor("l1", "s", i, SEQ, xnT, W["L1_xattn_sv_w"][:, :], W["L1_xattn_so_w"][:, :])
                    at(T, "l1_v", "sx", i)
                    P[name].done(T.transpose(bank(7, 128), u[:, :], ident), "fxT")
                    at(T, "l1_v", "fxT", i)
                    for c in range(FC):
                        P[name].done(mm(bank(c, 128), W["L1_xattn_fi_w"][:, 128 * c:128 * c + 128], xnT[:, :]), f"f{c}")
                    at(T, "l1_a", "f3", i)
                    for c in range(FC):
                        last = mm(bank(6, 128), hid[:, c, :], W["L1_xattn_fo_w"][:, c, :], start=c == 0, stop=c == FC - 1)
                    P[name].done(last, "fy")

            if last_stage >= 4:
                at(T, "qw_v", "quantised")
                for c in range(3):
                    last = T.transpose(bank(c, 128), W["L1_attn_in_w"][:, c, :], ident)
                P["qw_p"].done(last, "wiT")
                P["qw_p"].done(T.transpose(bank(3, 128), W["L1_attn_out_w"][:, :], ident), "woT")
                with pe.Fori(0, PAIRS) as i:
                    at(T, "qn_v", "xn", i)
                    P["qn_p"].done(T.transpose(bank(7, 128), xn[:, :], ident), "xT")
                pe.wait_ge(P["qn_v"].sem, PAIRS * P["qn_v"].n)
                for s_ in range(3):
                    for h in range(2):
                        P["qx_p"].done(mm(bank(2 * s_ + h), WiT[:, s_, :], xT_all[:, 512 * h:512 * h + 512]), f"X{s_}{h}")
                with pe.Fori(0, PAIRS) as i:
                    at(T, "qa_v", "load", i)
                    self_tensor("qa", "", i, 32, vT_t[:, :], ident, None)
                at(T, "qo_v", "Oint")
                for t in TS:
                    if t >= 2:
                        at(T, "qo_v", f"oT{t - 2}")
                    P["qo_p"].done(T.transpose(bank(t % 2, 128), O_all[:, t, :], ident), f"oT{t}")
                for t in TS:
                    at(T, "qo_v", f"oT{PAIRS - 1}" if t < 2 else f"y{t - 2}")
                    P["qo_p"].done(mm(bank(t % 2, 128), OT_all[:, 128 * t:128 * t + 128], WoT[:, :]), f"y{t}")
            if last_stage >= 5:
                with pe.Fori(0, PAIRS) as i:
                    at(T, "r_v", "xn", i)
                    P["r_p"].done(T.transpose(bank(7, 128), xn[:, :], ident), "xT")
                    at(T, "r_v", "xT", i)
                    P["r_p"].done(mm(bank(6, EXPERTS), xnT[:, :], W["L1_ffn_W_router"][:, :]), "log")
                    at(T, "r_v", "w", i)
                    P["r_p"].done(T.transpose(bank(7, 128, 8), w_t[:, :], ident), "wT")
                    at(T, "r_v", "wT", i)
                    P["r_p"].done(mm(bank(6, 128), w_tT[:, :], W["L1_ffn_b2"][:, :]), "b2")
                pe.wait_ge(P["r_v"].sem, PAIRS * P["r_v"].n)
                with pe.Fori(0, EXPERTS // 2) as i:
                    moe_tensor("e1", False, i)

        @block.vector
        def _(dve):
            dve.wait_ge(loads, 16 * N_W)
            dve.wait_ge(consts_loaded, 16)
            dve.wait_ge(x_loaded, 16)
            at(V, "pre_p", "WqT")
            vdone(V.tensor_copy(WqT[:, :], bank(6, 128)), "pre_v", "WqT")
            at(V, "pre_p", "WvT")
            vdone(V.tensor_copy(WvT[:, :], bank(7, 128)), "pre_v", "WvT")
            link(V.memset(mask_hi[:, :].bitcast(F32) if False else mask_sb[:, KEYS:KPAD], NEG))
            perm_in = mask_sb[:, 0:FULL * 128].rearrange("b (p t) -> b t p", t=FULL)
            for part in range(2):
                if part == 0:
                    link(V.tensor_copy(mask_hi[:, 0:FULL * 128].rearrange("b (t p) -> b t p", t=FULL), perm_in))
                    V.tensor_copy(mask_hi[:, FULL * 128:KPAD], mask_sb[:, FULL * 128:KPAD]).then_inc(mask_split, 1)
                    dve.wait_ge(mask_split, 1)
                else:
                    V.tensor_tensor(mask_lo[:, 0:FULL * 128].rearrange("b (t p) -> b t p", t=FULL), perm_in,
                                    mask_hi[:, 0:FULL * 128].rearrange("b (t p) -> b t p", t=FULL), ALU.subtract).then_inc(mask_split, 1)
                    V.tensor_tensor(mask_lo[:, FULL * 128:KPAD], mask_sb[:, FULL * 128:KPAD], mask_hi[:, FULL * 128:KPAD],
                                    ALU.subtract).then_inc(mask_split, 1)
                    dve.wait_ge(mask_split, 3)
            link(V.tensor_copy(KS[:, :, :].rearrange("p g k -> p (g k)"), consts[:, C_KROW:C_KROW + 1].broadcast_to([128, 4 * KPAD])))
            link(V.tensor_copy(QS[:, :, :, :].rearrange("p g b q -> p (g b q)"), consts[:, C_QROW:C_QROW + 1].broadcast_to([128, 512])))

            def phase1(i):
                xt = x[:, bass.ds(i, 1), :].rearrange("p t d -> p (t d)")
                vdone(ln_vector(xt, xn[:, :], "l0", "", i), "l0_v", "xn", i)
                at(V, "l0_p", "xT", i)
                vdone(V.tensor_copy(xnT[:, :], bank(7, 128)), "l0_v", "xT", i)
                at(V, "l0_p", "q", i)
                vdone(V.tensor_scalar(l0q[:, :], bank(6, 128), COLS["L0_xattn_bq"][:, 0:1], None, ALU.add), "l0_v", "q", i)
                at(V, "l0_p", "qk", i)
                link(V.tensor_copy(l0s[:, 0:1], PS[:, 512 * 7 + 256:512 * 7 + 257]))
                vdone(V.tensor_copy(l0qk[:, :], bank(7, 128)), "l0_v", "qk", i)
                at(V, "l0_p", "s", i)
                link(V.reduce_max(l0s[:, 1:2], PS[:, 0:KEYS], AX))
                link(V.tensor_tensor(l0s[:, 2:3], l0s[:, 1:2], l0s[:, 0:1], ALU.add))
                link(V.tensor_tensor(l0s[:, 5:6], l0s[:, 0:1], l0s[:, 2:3], ALU.subtract))
                vdone(V.tensor_scalar(l0s[:, 3:4], l0s[:, 5:6], float(DIM) ** -0.5, None, ALU.mult), "l0_v", "max", i)
                at(V, "l0_a", "exp", i)
                link(V.reciprocal(l0s[:, 6:7], l0s[:, 4:5]))
                at(V, "l0_p", "pc", i)
                vdone(V.tensor_copy(pcT[:, :], bank(6, 128)), "l0_v", "pc", i)
                link(V.tensor_tensor(t1[:, :], xt, ROWS["L0_xattn_bv"][:, :], ALU.add))
                at(V, "l0_p", "y", i)
                link(V.scalar_tensor_tensor(xt, bank(7, 128), l0s[:, 6:7], t1[:, :], ALU.mult, ALU.add))
                vdone(ln_vector(xt, xn[:, :], "l0", "a", i), "l0_v", "axn", i)
                at(V, "l0_p", "axT", i)
                vdone(V.tensor_copy(xnT[:, :], bank(7, 128)), "l0_v", "axT", i)
                at(V, "l0_p", "aqk", i)
                vdone(V.tensor_scalar(qT[:, :], PS[:, 0:128], HD ** -0.5, None, ALU.mult), "l0_v", "aq", i)
                kbd_vector("l0", "a", i, SEQ, PS[:, 128:256], None, PS[:, 512:768])
                core_vector("l0", "a", i, SEQ, causal, None)
                out_vector("l0", "a", i)
                link(V.tensor_tensor(xt, bank(6, 128), xt, ALU.add))
                vdone(ln_vector(xt, xn[:, :], "l0", "g", i), "l0_v", "gxn", i)
                at(V, "l0_p", "gxT", i)
                link(V.tensor_copy(xnT[:, :], bank(7, 128)))
                vdone(V.tensor_copy(xT_all[:, bass.ds(i * 128, 128)], bank(7, 128)), "l0_v", "gxT", i)
                at(V, "l0_p", "glog", i)
                link(V.tensor_copy(lg[:, :], bank(6, EXPERTS)))
                vdone(route_vector(tok_w[:, bass.ds(i, 1), :].rearrange("p t e -> p (t e)"), "l0", "g", i), "l0_v", "gend", i)

            with dve.Fori(0, PAIRS) as i:
                in_loop(i, PER["phase1"], lambda: phase1(i))
            state["links"] += PAIRS * PER["phase1"]

            if last_stage >= 2:
                with dve.Fori(0, EXPERTS // 2) as i:
                    in_loop(i, PER["e0"], lambda: moe_vector("e0", True, i))
                state["links"] += EXPERTS // 2 * PER["e0"]

            def post_norm(y, resid, b, g, be, pre, step, i):
                link(V.tensor_tensor(t1[:, :], resid, ROWS[b][:, :], ALU.add))
                link(V.tensor_tensor(t1[:, :], y, t1[:, :], ALU.add))
                link(ln_vector(t1[:, :], t1[:, :], "l1", pre, i))
                link(V.tensor_tensor(t1[:, :], t1[:, :], ROWS[g][:, :], ALU.mult))
                vdone(V.tensor_tensor(u[:, :], t1[:, :], ROWS[be][:, :], ALU.add), "l1_v", step, i)

            def phase3(i):
                xt = x[:, bass.ds(i, 1), :].rearrange("p t d -> p (t d)")
                vdone(ln_vector(xt, u[:, :], "l1", "", i), "l1_v", "xn", i)
                at(V, "l1_p", "xT", i)
                vdone(V.tensor_copy(xnT[:, :], bank(7, 128)), "l1_v", "xT", i)
                at(V, "l1_p", "q", i)
                vdone(V.tensor_scalar(qf[:, :], bank(6, 128), COLS["L1_xattn_cq_b"][:, 0:1], HD ** -0.5, ALU.add, ALU.mult), "l1_v", "q", i)
                vdone(V.tensor_copy(qh[:, :], qf[:, :]), "l1_v", "qh", i)
                vdone(V.tensor_tensor(ql[:, :], qf[:, :], qh[:, :], ALU.subtract), "l1_v", "ql", i)
                for b in range(2):
                    for c, (c0, cw) in enumerate(CHUNKS):
                        cw = min(cw, KEYS - c0)
                        at(V, "l1_a", f"kh{b}{c}", i)
                        if b and c == 0:
                            dve.wait_ge(ks_stacked, (2 * i + 1) * 16 * 20)
                        vdone(V.scalar_tensor_tensor(kl[:, c0:c0 + cw], bank(7 if c % 2 else 6, cw), COLS["L1_xattn_ck_b"][:, 0:1],
                                                     kh[:, c0:c0 + cw], ALU.add, ALU.subtract), "l1_v", f"kl{b}{c}", i)
                    dve.wait_ge(qs_stacked, (i + 1) * 16 * 12)
                    vdone(V.tensor_tensor(QB[:, :].rearrange("p (g h q) -> p g h q", g=4, h=4),
                                          QS[:, :, b, :].unsqueeze(2).broadcast_to([128, 4, 4, SEQ]),
                                          consts[:, C_QM:C_QM + 4].unsqueeze(1).unsqueeze(3).broadcast_to([128, 4, 4, SEQ]),
                                          ALU.mult), "l1_v", f"qb{b}", i)
                    for p in range(8):
                        for c, (c0, cw) in enumerate(CHUNKS):
                            at(V, "l1_p", f"m{b}{p}{c}", i)
                            P["l1_v"].done(V.reduce_max(mx[:, p, c:c + 1], bank((4 * p + c) % 2, cw), AX), f"m{b}{p}{c}")
                    at(V, "l1_v", f"m{b}73", i)
                    vdone(V.tensor_reduce(nm[:, :], mx[:, :, :], AX, ALU.max, negate=True), "l1_v", f"nm{b}", i)
                    at(V, "l1_p", f"nm{b}", i)
                    vdone(V.tensor_copy(nmh[:, :], bank(7, 128, 8)), "l1_v", f"nmh{b}", i)
                    vdone(V.tensor_tensor(nml[:, :], bank(7, 128, 8), nmh[:, :], ALU.subtract), "l1_v", f"nml{b}", i)
                    at(V, "l1_p", f"sum{b}", i)
                    link(V.reciprocal(rsum[:, :], bank(7, 256)))
                    link(V.tensor_tensor(rsum[:, :], acc_sb[:, :, :, :].rearrange("p r h q -> p (r h q)"), rsum[:, :], ALU.mult))
                    r4 = rsum[:, :].rearrange("p (r h q) -> p r h q", r=2, h=2)
                    link(V.tensor_scalar(onT[:, :, b, :], r4[:, :, 0, :], consts[:, C_OM:C_OM + 1], None, ALU.mult))
                    link(V.scalar_tensor_tensor(onT[:, :, b, :], r4[:, :, 1, :], consts[:, C_OM + 1:C_OM + 2], onT[:, :, b, :], ALU.mult, ALU.add))
                    link(V.tensor_scalar(onT[:, 0, b, :], onT[:, 0, b, :], cv_b[:, 0:1], None, ALU.add))
                    vdone(V.tensor_scalar(onT[:, 1, b, :], onT[:, 1, b, :], cv_b[:, 1:2], None, ALU.add), "l1_v", f"on{b}", i)
                at(V, "l1_p", "cy", i)
                post_norm(bank(6, 128), u[:, :], "L1_xattn_co_b", "L1_xattn_co_g", "L1_xattn_co_be", "c", "cx", i)
                at(V, "l1_p", "sxT", i)
                vdone(V.tensor_copy(xnT[:, :], bank(7, 128)), "l1_v", "sxT", i)
                at(V, "l1_p", "sqk", i)
                vdone(V.tensor_scalar(qT[:, :], PS[:, 0:128], COLS["L1_xattn_sq_b"][:, 0:1], HD ** -0.5, ALU.add, ALU.mult), "l1_v", "sq", i)
                kbd_vector("l1", "s", i, SEQ, PS[:, 128:256], COLS["L1_xattn_sk_b"][:, 0:1], PS[:, 512:768])
                core_vector("l1", "s", i, SEQ, None, ROWS["L1_xattn_sv_b"][:, :])
                out_vector("l1", "s", i)
                post_norm(bank(6, 128), u[:, :], "L1_xattn_so_b", "L1_xattn_so_g", "L1_xattn_so_be", "s", "sx", i)
                at(V, "l1_p", "fxT", i)
                vdone(V.tensor_copy(xnT[:, :], bank(7, 128)), "l1_v", "fxT", i)
                at(V, "l1_p", "fy", i)
                link(V.tensor_tensor(t1[:, :], u[:, :], ROWS["L1_xattn_fo_b"][:, :], ALU.add))
                link(V.tensor_tensor(t1[:, :], bank(6, 128), t1[:, :], ALU.add))
                link(ln_vector(t1[:, :], t1[:, :], "l1", "f", i))
                link(V.tensor_tensor(t1[:, :], t1[:, :], ROWS["L1_xattn_fo_g"][:, :], ALU.mult))
                link(V.tensor_tensor(t1[:, :], t1[:, :], ROWS["L1_xattn_fo_be"][:, :], ALU.add))
                vdone(V.tensor_tensor(xt, xt, t1[:, :], ALU.add), "l1_v", "fx", i)

            if last_stage >= 3:
                with dve.Fori(0, PAIRS) as i:
                    in_loop(i, PER["phase3"], lambda: phase3(i))
                state["links"] += PAIRS * PER["phase3"]

            def quant_scale(k):
                at(V, "q_all", QUANT[k])
                link(V.tensor_scalar(qscale[:, k:k + 1], gmax[:, k:k + 1], 1.0 / QMAX, 1e-8, ALU.mult, ALU.max))
                link(V.reciprocal(qinv[:, k:k + 1], qscale[:, k:k + 1]))

            def quantise(t, k):
                link(V.tensor_scalar(t, t, qinv[:, k:k + 1], ROUND, ALU.mult, ALU.add))
                link(V.tensor_scalar(t, t, ROUND, QMAX, ALU.subtract, ALU.min))
                return V.tensor_scalar(t, t, -QMAX - 1.0, None, ALU.max)

            def largest(k, src):
                return V.reduce_max(amax[:, k:k + 1], src, AX, apply_absolute_value=True)

            def qn(i):
                xt = x[:, bass.ds(i, 1), :].rearrange("p t d -> p (t d)")
                vdone(ln_vector(xt, xn[:, :], "qn", "", i), "qn_v", "xn", i)
                at(V, "qn_p", "xT", i)
                vdone(V.tensor_copy(xT_all[:, bass.ds(i * 128, 128)], bank(7, 128)), "qn_v", "xT", i)

            def qa(i):
                for s_, dst in enumerate((qT, kT_t, vT_t)):
                    src = X[:, s_, :].rearrange("p (l s) -> p s l", l=BATCH)[:, bass.ds(8 * i, 8), :]
                    last = V.tensor_copy(dst[:, :].rearrange("p (s l) -> p s l", l=BATCH), src)
                    if s_ < 2:
                        link(last)
                vdone(last, "qa_v", "load", i)
                kbd_vector("qa", "", i, 32, kT_t[:, :], None, PS[:, 512:1024])
                core_vector("qa", "", i, 32, block_mask, None, qscale[:, 2:3])
                vdone(V.tensor_copy(O_all[:, bass.ds(i, 1), :].rearrange("p t d -> p (t d)"), o_sb[:, :]), "qa_v", "saved", i)

            if last_stage >= 4:
                wi = W["L1_attn_in_w"][:, :, :].rearrange("p c n -> p (c n)")
                wo = W["L1_attn_out_w"][:, :]
                vdone(largest(0, wi), "qw_v", "wi")
                vdone(largest(1, wo), "qw_v", "wo")
                quant_scale(0)
                link(quantise(wi, 0))
                quant_scale(1)
                vdone(quantise(wo, 1), "qw_v", "quantised")
                at(V, "qw_p", "woT")
                for c in range(3):
                    link(V.tensor_copy(WiT[:, c, :], bank(c, 128)))
                vdone(V.tensor_copy(WoT[:, :], bank(3, 128)), "qw_v", "wiT")
                with dve.Fori(0, PAIRS) as i:
                    in_loop(i, PER["qn"], lambda: qn(i))
                state["links"] += PAIRS * PER["qn"]
                for s_ in range(3):
                    for h in range(2):
                        at(V, "qx_p", f"X{s_}{h}")
                        link(V.tensor_scalar(X[:, s_, 512 * h:512 * h + 512], bank(2 * s_ + h), qscale[:, 0:1],
                                             COLS["L1_attn_in_b"][:, s_:s_ + 1], ALU.mult, ALU.add))
                Xf = X[:, :, :].rearrange("p s t -> p (s t)")
                vdone(largest(2, Xf), "qx_v", "X")
                quant_scale(2)
                link(quantise(Xf, 2))
                link(V.tensor_scalar(X[:, 0, :], X[:, 0, :], qscale[:, 2:3], HD ** -0.5, ALU.mult, ALU.mult))
                vdone(largest(3, X[:, 0, :]), "qx_v", "Q")
                quant_scale(3)
                link(quantise(X[:, 0, :], 3))
                link(V.tensor_tensor(unit[:, 0:1], qscale[:, 2:3], qscale[:, 3:4], ALU.mult))
                with dve.Fori(0, PAIRS) as i:
                    in_loop(i, PER["qa"], lambda: qa(i))
                state["links"] += PAIRS * PER["qa"]
                Of = O_all.rearrange("p t d -> p (t d)")
                vdone(largest(4, Of), "qx_v", "O")
                quant_scale(4)
                vdone(quantise(Of, 4), "qo_v", "Oint")
                link(V.tensor_tensor(unit[:, 1:2], qscale[:, 1:2], qscale[:, 4:5], ALU.mult))
                for t in TS:
                    at(V, "qo_p", f"oT{t}")
                    P["qo_v"].done(V.tensor_copy(OT_all.rearrange("p (l s) -> p s l", l=BATCH)[:, 8 * t:8 * t + 8, :],
                                                 bank(t % 2, 128).rearrange("p (s l) -> p s l", l=BATCH)), f"oT{t}")
                for t in TS:
                    at(V, "qo_p", f"y{t}")
                    P["qo_v"].done(V.scalar_tensor_tensor(Y_all[:, t, :], bank(t % 2, 128), unit[:, 1:2],
                                                          ROWS["L1_attn_out_b"][:, :], ALU.mult, ALU.add), f"y{t}")
                at(V, "qo_v", f"y{PAIRS - 1}")
                Yf = Y_all.rearrange("p t d -> p (t d)")
                vdone(largest(5, Yf), "qx_v", "Y")
                quant_scale(5)
                link(quantise(Yf, 5))
                xf = x[:, :, :].rearrange("p t d -> p (t d)")
                vdone(V.scalar_tensor_tensor(xf, Yf, qscale[:, 5:6], xf, ALU.mult, ALU.add), "qx_v", "x")

            def route(i):
                xt = x[:, bass.ds(i, 1), :].rearrange("p t d -> p (t d)")
                vdone(ln_vector(xt, xn[:, :], "r", "", i), "r_v", "xn", i)
                at(V, "r_p", "xT", i)
                link(V.tensor_copy(xT_all[:, bass.ds(i * 128, 128)], bank(7, 128)))
                vdone(V.tensor_copy(xnT[:, :], bank(7, 128)), "r_v", "xT", i)
                at(V, "r_p", "log", i)
                link(V.tensor_tensor(lg[:, :], bank(6, EXPERTS), router_b[:, :], ALU.add))
                vdone(route_vector(w_t[:, :], "r", "", i), "r_v", "w", i)
                link(V.tensor_copy(tok_w[:, bass.ds(i, 1), :].rearrange("p t e -> p (t e)"), w_t[:, :]))
                at(V, "r_p", "wT", i)
                vdone(V.tensor_copy(w_tT[:, :], bank(7, 128, 8)), "r_v", "wT", i)
                at(V, "r_p", "b2", i)
                vdone(V.tensor_tensor(xt, xt, bank(6, 128), ALU.add), "r_v", "end", i)

            if last_stage >= 5:
                with dve.Fori(0, PAIRS) as i:
                    in_loop(i, PER["route"], lambda: route(i))
                state["links"] += PAIRS * PER["route"]
                with dve.Fori(0, EXPERTS // 2) as i:
                    in_loop(i, PER["e1"], lambda: moe_vector("e1", False, i))


PER = {"phase1": 29, "e0": 12, "phase3": 36, "e1": 12, "qn": 2, "qa": 10, "route": 13}


def constants():
    import numpy as np
    c = np.zeros((128, C_END), np.float32)
    p = np.arange(128)
    c[:, C_ID:C_ID + 128] = np.eye(128)
    c[:, C_HM:C_HM + 16] = p[:, None] // HD == np.arange(16)[None]
    ch = np.arange(128)[None] // HD
    c[:, C_VM2:C_VM2 + 128] = ch % 2 == p[:, None] // 64
    c[:, C_VM4:C_VM4 + 128] = ch % 4 == p[:, None] // 32
    c[:, C_CAUSAL:C_CAUSAL + 64] = np.where(np.arange(64)[None] <= p[:, None] % 64, 0.0, NEG)
    c[:, C_BLK:C_BLK + 32] = np.where(np.arange(32)[None] // 16 == (p[:, None] % 32) // 16, 0.0, NEG)
    c[:, C_QM:C_QM + 4] = np.where(p[:, None] < 96, (p[:, None] % 32) // HD == np.arange(4)[None], 1.0)
    c[:, C_SEL:C_SEL + 128] = p[:, None] == 32 * (p[None] // 32) + 16
    c[:, C_OM:C_OM + 2] = (p[:, None] % 32 < 16) & ((p[:, None] % 32) // HD == np.arange(2)[None])
    c[:, C_IOTA:C_IOTA + 8] = np.arange(8)[None]
    c[:, C_KROW] = (p == 96) | (p == 97)
    c[:, C_QROW] = (p == 98) | (p == 99)
    c[:, C_HALF] = -0.5
    return c


NAMES = [
    "x", "ctx_1024", "mask_Bx1x1xS2_ff0", "L0_xattn_Wq", "L0_xattn_bq", "L0_xattn_Wk", "L0_xattn_bk", "L0_xattn_Wv",
    "L0_xattn_bv", "L0_attn_W_Q", "L0_attn_W_K", "L0_attn_W_V", "L0_attn_W_o", "L0_ffn_gate", "L0_ffn_experts_w1",
    "L0_ffn_experts_w2", "L0_ffn_experts_w3", "L1_xattn_cq_w", "L1_xattn_cq_b", "L1_xattn_ck_w", "L1_xattn_ck_b",
    "L1_xattn_cv_w", "L1_xattn_cv_b", "L1_xattn_co_w", "L1_xattn_co_b", "L1_xattn_co_g", "L1_xattn_co_be",
    "L1_xattn_sq_w", "L1_xattn_sq_b", "L1_xattn_sk_w", "L1_xattn_sk_b", "L1_xattn_sv_w", "L1_xattn_sv_b",
    "L1_xattn_so_w", "L1_xattn_so_b", "L1_xattn_so_g", "L1_xattn_so_be", "L1_xattn_fi_w", "L1_xattn_fi_b",
    "L1_xattn_fo_w", "L1_xattn_fo_b", "L1_xattn_fo_g", "L1_xattn_fo_be", "L1_attn_in_w", "L1_attn_in_b",
    "L1_attn_out_w", "L1_attn_out_b", "L1_ffn_W_router", "L1_ffn_b_router", "L1_ffn_W1", "L1_ffn_b1", "L1_ffn_W2",
    "L1_ffn_b2"]


def kernel(**inputs):
    import numpy as np
    import concourse.bacc as bacc
    from concourse.bass_utils import run_bass_kernel_spmd as run

    nc = bacc.Bacc("TRN2", target_bir_lowering=False, num_devices=1)
    arrays = {name: np.ascontiguousarray(inputs[name]) for name in NAMES}
    arrays["consts"] = constants()
    aps = {name: nc.dram_tensor("in_" + name, a.shape, F32, kind="ExternalInput").ap() for name, a in arrays.items()}
    out = nc.dram_tensor("out_0", (BATCH, SEQ, DIM), F32, kind="ExternalOutput").ap()
    scratch = nc.dram_tensor("context_transposed", (BATCH, 128, KEYS), F32, kind="Internal").ap()
    mask_parts = nc.dram_tensor("mask_parts", (2, BATCH, KPAD), F32, kind="Internal").ap()
    build(nc, aps, out, scratch, mask_parts)
    r = run(nc, [{"in_" + name: a for name, a in arrays.items()}], core_ids=[0])
    return r.results[0]["out_0"]
```

```python
from contextlib import ExitStack

import concourse.bass as bass
from concourse import mybir

F32 = mybir.dt.float32
F32R = mybir.dt.float32r
U32 = mybir.dt.uint32
ALU = mybir.AluOpType
ACT = mybir.ActivationFunctionType
AX = mybir.AxisListType.X
ABSMAX = bass.bass_isa.ReduceOp.max

STOP = "F"

BATCH, SEQ, DIM = 16, 64, 128
TOKENS = BATCH * SEQ
PAIRS = TOKENS // 128
HEADS, HD = 16, 8
KEYS = 1601
FULL = KEYS // 128
TAIL = KEYS - FULL * 128
KT = FULL + 1
KPAD = KEYS + 1
CHUNKS = [(0, 512), (512, 512), (1024, 512), (1536, KPAD - 1536)]
EXPERTS, FF = 8, 512
FC = FF // 128
EPS = 1e-5
QMAX = 127.0
ROUND = 12582912.0
NEG = -1e30

C_ID, C_HM, C_VM2, C_VM4, C_CAUSAL, C_BLK, C_QM, C_SEL, C_OM, C_IOTA, C_KROW, C_QROW, C_HALF, C_END = (
    0, 128, 144, 272, 400, 464, 496, 500, 628, 630, 638, 639, 640, 641)


class Progress:

    def __init__(self, sem, steps):
        self.sem, self.at, self.n = sem, {s: k + 1 for k, s in enumerate(steps)}, len(steps)
        assert len(self.at) == self.n
        self.steps, self.next = list(steps), 0

    def done(self, ins, step):
        assert self.steps[self.next] == step, (step, self.steps[self.next])
        self.next = (self.next + 1) % self.n
        ins.then_inc(self.sem, 1)

    def value(self, step, i=0):
        return i * self.n + self.at[step]


def build(nc, A, out, scratch, mask_parts):
    ctx = ExitStack()
    with ctx:
        def sb(name, shape, dt=F32):
            return ctx.enter_context(nc.sbuf_tensor(name, shape, dt))

        def sem(name):
            return ctx.enter_context(nc.semaphore(name))

        PS = ctx.enter_context(nc.psum_tensor("PS", [128, 8 * 512], F32))

        def bank(k, n=512, parts=128):
            return PS[0:parts, 512 * k:512 * k + n]

        consts = sb("consts", [128, C_END])
        ident = consts[:, C_ID:C_ID + 128]
        head_mask = consts[:, C_HM:C_HM + 16]
        causal = consts[:, C_CAUSAL:C_CAUSAL + 64]
        block_mask = consts[:, C_BLK:C_BLK + 32]
        minus_half = consts[:, C_HALF:C_HALF + 1]
        iota8 = consts[:, C_IOTA:C_IOTA + 8]

        W = {}
        for name in ("L0_xattn_Wq", "L0_xattn_Wk", "L0_xattn_Wv", "L0_attn_W_Q", "L0_attn_W_K", "L0_attn_W_V",
                     "L0_attn_W_o", "L1_xattn_cq_w", "L1_xattn_ck_w", "L1_xattn_cv_w", "L1_xattn_sq_w",
                     "L1_xattn_sk_w", "L1_xattn_sv_w", "L1_xattn_so_w", "L1_attn_out_w"):
            W[name] = sb("w_" + name, [128, 128])
        W["L1_xattn_fi_w"] = sb("w_fi", [128, FF])
        W["L1_xattn_fo_w"] = sb("w_fo", [128, FC, 128])
        W["L1_attn_in_w"] = sb("w_in", [128, 3, 128])
        W["L0_ffn_gate"] = sb("w_gate", [128, EXPERTS])
        W["L1_ffn_W_router"] = sb("w_router", [128, EXPERTS])
        W["L1_ffn_b2"] = sb("w_b2", [EXPERTS, 128])
        co_w = sb("co_w", [128, 2, 128])
        COLS = {}
        for name, n in (("L0_xattn_bq", 1), ("L0_xattn_bk", 1), ("L1_xattn_cq_b", 1), ("L1_xattn_ck_b", 1),
                        ("L1_xattn_sq_b", 1), ("L1_xattn_sk_b", 1), ("L1_xattn_fi_b", FC), ("L1_attn_in_b", 3)):
            COLS[name] = sb("c_" + name, [128, n])
        cv_b = sb("cv_b", [128, 2])
        ROWS = {}
        for name in ("L0_xattn_bv", "L1_xattn_sv_b", "L1_xattn_co_b", "L1_xattn_co_g", "L1_xattn_co_be",
                     "L1_xattn_so_b", "L1_xattn_so_g", "L1_xattn_so_be", "L1_xattn_fo_b", "L1_xattn_fo_g",
                     "L1_xattn_fo_be", "L1_attn_out_b"):
            ROWS[name] = sb("r_" + name, [128, 128])
        router_b = sb("router_b", [128, EXPERTS])

        x = sb("x", [128, PAIRS, 128])
        xn = sb("xn", [128, 128])
        xnT = sb("xnT", [128, 128])
        xT_all = sb("xT_all", [128, TOKENS])
        tok_w = sb("tok_w", [128, PAIRS, EXPERTS])

        stats = sb("stats", [128, 6])
        mv = sb("mv", [128, 2])
        var_eps = sb("var_eps", [128, 1])
        rstd = sb("rstd", [128, 1])

        qT = sb("qT", [128, 128])
        prT = sb("prT", [128, 1024])
        smax = sb("smax", [128, HEADS])
        ssum = sb("ssum", [128, HEADS])
        o_sb = sb("o_sb", [128, 128])
        oT = sb("oT", [128, 128])

        early = sb("early", [128, 2 * KT * 128])
        work_area = sb("work_area", [128, 3584 + KT * 256])
        tail_area, value_area = work_area[:, 0:3584], work_area[:, 3584:3584 + KT * 256]
        ctx_nat = early[:, :].rearrange("p (b k d) -> p b k d", b=2, k=KT)
        kbd = tail_area[:, 0:2048]
        vbd = tail_area[:, 2048:2560]
        pr = tail_area[:, 2560:3584]
        ctxT = sb("ctxT", [128, 2, KPAD])
        P0 = value_area[:, 0:KEYS]
        P0T = value_area[:, KEYS:KEYS + KT * 128].rearrange("p (k q) -> p k q", k=KT)
        WqT = sb("WqT", [128, 128])
        WvT = sb("WvT", [128, 128])
        l0q = sb("l0q", [128, 128])
        l0qk = sb("l0qk", [128, 128])
        l0s = sb("l0s", [128, 8])
        pcT = sb("pcT", [128, 128])

        kh = sb("kh", [128, KPAD], F32R)
        kl = sb("kl", [128, KPAD], F32R)
        KS = [sb("KS0", [128, 4, KPAD], F32R)[:, :, :],
              sb("KS1", [128, 4, KPAD], F32R)[:, :, :]]
        qh, ql = kh[:, 0:TOKENS], kl[:, 0:TOKENS]
        QS = sb("QS", [128, 4, TOKENS], F32R)
        QB = [sb(f"QB{b}", [128, 1024], F32R) for b in range(2)]
        VA = [value_area.rearrange("p (k h c) -> p k h c", k=KT, h=HEADS // 2),
              early[:, :].rearrange("p (k h c) -> p k h c", k=KT, h=HEADS // 2)]
        PT = sb("PT", [128, 2, 1024])
        mask_sb = PT[0:BATCH, :, :].rearrange("p a n -> p (a n)")[:, 0:KPAD]
        mask_hi, mask_lo = kh[0:BATCH, :], kl[0:BATCH, :]
        mx = sb("mx", [128, 8, 4])
        nm = sb("nm", [128, 8])
        nmh = sb("nmh", [8, 128], F32R)
        nml = sb("nml", [8, 128], F32R)
        acc_sb, rsum = prT[:, 0:256], prT[:, 256:512]
        u_all = sb("u_all", [128, PAIRS, 128])
        t1 = sb("t1", [128, 128])
        stats_all = sb("stats_all", [128, PAIRS, 6])
        mv_all = sb("mv_all", [128, PAIRS, 2])
        var_all = sb("var_all", [128, PAIRS])
        rstd_all = sb("rstd_all", [128, PAIRS])

        expert_area = sb("expert_area", [128, 3 * 2 * FF])
        w1 = expert_area[:, 0:2 * FF].rearrange("p (j f) -> p j f", j=2)
        w3 = expert_area[:, 2 * FF:4 * FF].rearrange("p (j f) -> p j f", j=2)
        w2 = expert_area[:, 4 * FF:6 * FF].rearrange("p (j c n) -> p j c n", j=2, c=FC)
        onT = expert_area[:, 0:2 * TOKENS].rearrange("p (r t) -> p r t", r=2)
        b1 = sb("b1", [128, 2, FC])
        g_act = P0[:, 0:1024].rearrange("p (a n) -> p a n", a=2)
        hidT = PT[:, :, :].rearrange("p a n -> p (a n)").rearrange("p (c n) -> p c n", c=FC)
        wcol = sb("wcol", [128, 2, PAIRS])
        top8 = sb("top8", [128, 8])
        topi = sb("topi", [128, 8], U32)
        topf = sb("topf", [128, 8])
        tops = sb("tops", [128, 8])
        lg = sb("lg", [128, 8])
        one8 = sb("one8", [128, 8])

        nat_l1 = ctxT[:, :, :].rearrange("p b k -> p (b k)")
        Q_all, K_all = nat_l1[:, 0:TOKENS], nat_l1[:, TOKENS:2 * TOKENS]
        t_all = nat_l1[:, 2 * TOKENS:3 * TOKENS].rearrange("p (t d) -> p t d", t=PAIRS)
        hid = work_area[:, 0:FC * TOKENS].rearrange("p (c n) -> p c n", c=FC)
        V_all = expert_area[:, 0:2 * TOKENS]

        X = ctxT[:, :, :].rearrange("p b k -> p (b k)")[:, 0:3 * TOKENS].rearrange("p (s t) -> p s t", s=3)
        O_all = P0T[:, 0:PAIRS, :]
        nat = PT[:, :, :].rearrange("p a n -> p (a n)")
        OT_all = nat[:, 0:TOKENS]
        Y_all = nat[:, TOKENS:2 * TOKENS].rearrange("p (t d) -> p t d", t=PAIRS)
        WiT = early[:, 0:384].rearrange("p (c n) -> p c n", c=3)
        WoT, kT_t, vT_t = early[:, 384:512], early[:, 512:640], early[:, 640:768]
        amax = sb("amax", [128, 8])
        gmax = sb("gmax", [128, 8])
        qscale = sb("qscale", [128, 8])
        qinv = sb("qinv", [128, 8])
        unit = sb("unit", [128, 2])
        blank = sb("blank", [128, 1])
        blank_g = sb("blank_g", [128, 6])
        w_t = sb("w_t", [128, EXPERTS])
        w_tT = sb("w_tT", [EXPERTS, 128])

        P = {}

        def progress(name, steps):
            P[name] = Progress(sem(name), steps)

        def at(eng, name, step, i=0):
            eng.wait_ge(P[name].sem, P[name].value(step, i))

        loads = sem("weights_loaded")
        consts_loaded = sem("consts_loaded")
        n_loads = [0]
        x_loaded = sem("x_loaded")
        dve_link = sem("dve_link")
        state = {"links": 0, "base": 0}

        def link(ins):
            ins.then_inc(dve_link, 1)
            state["links"] += 1
            nc.vector.wait_ge(dve_link, state["base"] + state["links"])

        def vdone(ins, name, step, i=0):
            P[name].done(ins, step)
            at(nc.vector, name, step, i)

        def in_loop(i, per_round, body):
            base, start = state["base"], state["links"]
            state["base"], state["links"] = base + start + i * per_round, 0
            body()
            if state["links"] != per_round:
                print("LINKS", state["links"], per_round)
            state["base"], state["links"] = base, start

        def apart():
            nc.vector.memset(blank[:, :], 0.0)

        def apart_g(n, k):
            if not isinstance(n, int):
                nc.gpsimd.tensor_tensor(blank_g[:, k:k + 1], consts[:, 0:1], consts[:, 0:1], ALU.mult)

        V, T, S, G = nc.vector, nc.tensor, nc.scalar, nc.gpsimd

        def mm(o, l, r, start=True, stop=True, **k):
            return T.matmul(o, l, r, start=start, stop=stop, **k)

        def ln_vector(src, dst, name, pre, i):
            apart()
            link(V.bn_stats(stats[:, :], src))
            apart()
            link(V.bn_aggr(mv[:, :], stats[:, :]))
            vdone(V.tensor_scalar(var_eps[:, :], mv[:, 1:2], EPS, None, ALU.add), name + "_v", pre + "var", i)
            at(V, name + "_g", pre + "rstd", i)
            return V.tensor_scalar(dst, src, mv[:, 0:1], rstd[:, 0:1], ALU.subtract, ALU.mult)

        def ln_gpsimd(name, pre, i):
            at(G, name + "_v", pre + "var", i)
            P[name + "_g"].done(G.tensor_tensor(rstd[:, :], var_eps[:, :], minus_half, ALU.pow), pre + "rstd")

        def ln_all_vector(r, src, dst, transposed=True):
            with V.Fori(0, PAIRS) as t:
                V.bn_stats(stats_all[:, bass.ds(t, 1), :].rearrange("p t s -> p (t s)"),
                           src[:, bass.ds(t, 1), :].rearrange("p t s -> p (t s)")).then_inc(ln_stats, 1)
            V.wait_ge(ln_stats, 2 * PAIRS * r + PAIRS)
            for t in range(PAIRS):
                V.bn_aggr(mv_all[:, t, :], stats_all[:, t, :]).then_inc(ln_stats, 1)
            V.wait_ge(ln_stats, 2 * PAIRS * (r + 1))
            V.tensor_scalar(var_all[:, :].unsqueeze(2), mv_all[:, :, 1:2], EPS, None, ALU.add).then_inc(ln_var, 1)
            V.wait_ge(ln_rstd, r + 1)
            with V.Fori(0, PAIRS) as t:
                V.tensor_scalar(dst[:, bass.ds(t, 1), :].rearrange("p t s -> p (t s)"),
                                src[:, bass.ds(t, 1), :].rearrange("p t s -> p (t s)"),
                                mv_all[:, bass.ds(t, 1), 0:1].rearrange("p t s -> p (t s)"),
                                rstd_all[:, bass.ds(t, 1)], ALU.subtract, ALU.mult).then_inc(ln_xn, 1)
            V.wait_ge(ln_xn, PAIRS * (r + 1))

        def ln_all_gpsimd(r):
            G.wait_ge(ln_var, r + 1)
            G.tensor_tensor(rstd_all[:, :], var_all[:, :], minus_half.broadcast_to([128, PAIRS]), ALU.pow).then_inc(ln_rstd, 1)

        def transpose_vector(r):
            for h in range(2):
                V.wait_ge(ln_T, 2 * r + h + 1)
                V.tensor_copy(xT_all[:, 512 * h:512 * h + 512], bank(6 + h)).then_inc(ln_xT, 1)

        def transpose_tensor(r, src):
            for h in range(2):
                for t in range(4):
                    last = T.transpose(PS[:, 512 * (6 + h) + 128 * t:512 * (6 + h) + 128 * t + 128], src[:, 4 * h + t, :], ident)
                last.then_inc(ln_T, 1)

        def self_tensor(name, pre, i, grp, xT, wv, wo):
            ng, rep = 128 // grp, 128 // grp
            nb = HEADS // rep
            for g in range(ng):
                for r in range(rep):
                    last = mm(PS[r * grp:(r + 1) * grp, 512 + g * 128:512 + (g + 1) * 128],
                              xT[:, g * grp:(g + 1) * grp], wv)
            P[name + "_p"].done(last, pre + "v")
            core_tensor(name, pre, i, grp, wo)

        def core_tensor(name, pre, i, grp, wo):
            ng, rep = 128 // grp, 128 // grp
            nb, width = HEADS // rep, HEADS * grp
            at(T, name + "_v", pre + "kbd", i)
            for g in range(ng):
                for c in range(0, width, 512):
                    last = mm(PS[g * grp:(g + 1) * grp, 1024 + c:1024 + c + 512], qT[:, g * grp:(g + 1) * grp],
                              kbd[:, g * width + c:g * width + c + 512])
            P[name + "_p"].done(last, pre + "s")
            at(T, name + "_a", pre + "exp", i)
            for b in range(nb):
                last = T.transpose(PS[:, 2048 + b * 128:2048 + (b + 1) * 128], pr[:, b * 128:(b + 1) * 128], ident)
            P[name + "_p"].done(last, pre + "pT")
            at(T, name + "_a", pre + "pT", i)
            at(T, name + "_v", pre + "vbd", i)
            for g in range(ng):
                for b in range(nb):
                    last = mm(PS[g * grp:(g + 1) * grp, 3072 + b * rep * HD:3072 + (b + 1) * rep * HD],
                              prT[:, b * 128 + g * grp:b * 128 + (g + 1) * grp],
                              vbd[:, g * 128 + b * rep * HD:g * 128 + (b + 1) * rep * HD])
            P[name + "_p"].done(last, pre + "o")
            if wo is None:
                return
            at(T, name + "_v", pre + "o", i)
            P[name + "_p"].done(T.transpose(bank(7, 128), o_sb[:, :], ident), pre + "oT")
            at(T, name + "_v", pre + "oT", i)
            P[name + "_p"].done(mm(bank(6, 128), oT[:, :], wo), pre + "y")

        def self_scalar(name, pre, i, grp, scale=1.0):
            width = HEADS * grp
            at(S, name + "_v", pre + "sub", i)
            P[name + "_a"].done(S.activation(pr[:, 0:width], pr[:, 0:width], ACT.Exp, scale=scale), pre + "exp")
            at(S, name + "_p", pre + "pT", i)
            P[name + "_a"].done(S.activation(prT[:, 0:width], PS[:, 2048:2048 + width], ACT.Copy), pre + "pT")

        def core_vector(name, pre, i, grp, mask, bias, unit=None):
            width = HEADS * grp
            at(V, name + "_p", pre + "s", i)
            sc = PS[:, 1024:1024 + width].rearrange("p (h k) -> p h k", h=HEADS)
            p3 = pr[:, 0:width].rearrange("p (h k) -> p h k", h=HEADS)
            if mask is not None:
                link(V.tensor_tensor(p3, sc, mask.unsqueeze(1).broadcast_to([128, HEADS, grp]), ALU.add))
                sc = p3
            link(V.reduce_max(smax[:, :], sc, AX))
            vdone(V.tensor_tensor(p3, sc, smax[:, :].unsqueeze(2).broadcast_to([128, HEADS, grp]), ALU.subtract),
                  name + "_v", pre + "sub", i)
            at(V, name + "_a", pre + "exp", i)
            link(V.reduce_sum(ssum[:, :], p3, AX))
            link(V.reciprocal(ssum[:, :], ssum[:, :]))
            if unit is not None:
                link(V.tensor_scalar(ssum[:, :], ssum[:, :], unit, None, ALU.mult))
            at(V, name + "_p", pre + "o", i)
            o3 = o_sb[:, :].rearrange("p (h d) -> p h d", h=HEADS)
            norm = V.tensor_tensor(o3, bank(6, 128).rearrange("p (h d) -> p h d", h=HEADS),
                                   ssum[:, :].unsqueeze(2).broadcast_to([128, HEADS, HD]), ALU.mult)
            if bias is not None:
                link(norm)
                norm = V.tensor_tensor(o_sb[:, :], o_sb[:, :], bias, ALU.add)
            vdone(norm, name + "_v", pre + "o", i)

        def out_vector(name, pre, i):
            at(V, name + "_p", pre + "oT", i)
            vdone(V.tensor_copy(oT[:, :], bank(7, 128)), name + "_v", pre + "oT", i)
            at(V, name + "_p", pre + "y", i)

        def kbd_vector(name, pre, i, grp, k_src, k_bias, v_src):
            ng, rep, width = 128 // grp, 128 // grp, HEADS * grp
            hm = head_mask.unsqueeze(2).broadcast_to([128, HEADS, grp])
            for g in range(ng):
                dst = kbd[:, g * width:(g + 1) * width].rearrange("p (h k) -> p h k", h=HEADS)
                src = k_src[:, g * grp:(g + 1) * grp].unsqueeze(1).broadcast_to([128, HEADS, grp])
                if k_bias is None:
                    last = V.tensor_tensor(dst, src, hm, ALU.mult)
                else:
                    last = V.scalar_tensor_tensor(dst, src, k_bias, hm, ALU.add, ALU.mult)
                if g < ng - 1:
                    link(last)
            vdone(last, name + "_v", pre + "kbd", i)
            at(V, name + "_p", pre + "v", i)
            vm = consts[:, (C_VM2 if rep == 2 else C_VM4):(C_VM2 if rep == 2 else C_VM4) + 128]
            vdone(V.tensor_tensor(vbd[:, 0:ng * 128].rearrange("p (g c) -> p g c", g=ng),
                                  v_src.rearrange("p (g c) -> p g c", g=ng),
                                  vm.unsqueeze(1).broadcast_to([128, ng, 128]), ALU.mult),
                  name + "_v", pre + "vbd", i)

        SELF_P = ["v", "s", "pT", "o"]
        SELF_V = ["kbd", "vbd", "sub", "o"]
        SELF_A = ["exp", "pT"]

        def route_vector(dst, name, pre, i):
            apart()
            link(V.max(top8[:, :], lg[:, :]))
            apart()
            link(V.max_index(topi[:, :], top8[:, :], lg[:, :]))
            link(V.tensor_copy(topf[:, 0:2], topi[:, 0:2]))
            vdone(V.tensor_scalar(tops[:, 0:2], top8[:, 0:2], top8[:, 0:1], None, ALU.subtract),
                  name + "_v", pre + "gap", i)
            at(V, name + "_a", pre + "gate", i)
            link(V.reduce_sum(tops[:, 4:5], tops[:, 2:4], AX))
            link(V.reciprocal(tops[:, 5:6], tops[:, 4:5]))
            link(V.tensor_scalar(tops[:, 6:8], tops[:, 2:4], tops[:, 5:6], None, ALU.mult))
            link(V.tensor_scalar(one8[:, :], iota8, topf[:, 0:1], tops[:, 6:7], ALU.is_equal, ALU.mult))
            link(V.tensor_scalar(lg[:, :], iota8, topf[:, 1:2], tops[:, 7:8], ALU.is_equal, ALU.mult))
            return V.tensor_tensor(dst, one8[:, :], lg[:, :], ALU.add)

        def route_scalar(name, pre, i):
            at(S, name + "_v", pre + "gap", i)
            P[name + "_a"].done(S.activation(tops[:, 2:4], tops[:, 0:2], ACT.Exp), pre + "gate")

        CH = range(FC)
        JT = [(j, t) for j in range(2) for t in range(2)]

        def moe_progress(name, gated):
            progress(name + "_p", [s for j, t in JT for s in [f"h{j}{t}{c}" for c in CH] + [f"y{j}{t}"]])
            progress(name + "_a", [f"h{j}{t}{c}" for j, t in JT for c in CH])
            progress(name + "_v", [s for j, t in JT for s in ([f"w{j}"] if t == 0 else [])
                                   + ([f"h{j}{t}{c}" for c in CH] if gated else []) + [f"y{j}{t}"]])
            P[name + "_w"] = [sem(name + f"_weights{j}") for j in range(2)]

        def moe_load(name, srcs, e, j):
            W1, W3, W2, B1 = srcs
            ld = P[name + "_w"][j]

            def dma(dst, src):
                nc.sync.dma_start(dst, src).then_inc(ld, 16)

            dma(w1[:, j, :], W1[bass.ds(e, 1), :, :].rearrange("e h f -> (e h) f"))
            dma(w2[:, j, :, :], W2[bass.ds(e, 1), :, :].rearrange("e (c p) n -> p (e c) n", p=128))
            if W3 is not None:
                dma(w3[:, j, :], W3[bass.ds(e, 1), :, :].rearrange("e h f -> (e h) f"))
            else:
                dma(b1[:, j, :], B1[bass.ds(e, 1), :].rearrange("e (c p) -> p (e c)", p=128))

        def moe_sync(sp, name, srcs):
            for j in range(2):
                moe_load(name, srcs, j, j)
            with sp.Fori(0, EXPERTS // 2 - 1) as i:
                for j in range(2):
                    at(sp, name + "_p", f"y{j}1", i)
                    moe_load(name, srcs, 2 * i + 2 + j, j)

        def moe_tensor(name, gated, i):
            used = name + ("_v" if gated else "_a")
            for n, (j, t) in enumerate(JT):
                if t == 0:
                    T.wait_ge(P[name + "_w"][j], 48 * i + 48)
                toks = xT_all[:, t * 512:(t + 1) * 512]
                for c in CH:
                    if c >= 2:
                        at(T, used, f"h{j}{t}{c - 2}", i)
                    elif n:
                        at(T, used, "h%d%d%d" % (*JT[n - 1], c + 2), i)
                    else:
                        T.wait_ge(P[used].sem, i * P[used].n)
                    b = 2 * (c % 2)
                    last = mm(bank(b), w1[:, j, c * 128:(c + 1) * 128], toks)
                    if gated:
                        last = mm(bank(b + 1), w3[:, j, c * 128:(c + 1) * 128], toks)
                    P[name + "_p"].done(last, f"h{j}{t}{c}")
                at(T, used, f"h{j}{t}3", i)
                if n >= 2:
                    at(T, name + "_v", "y%d%d" % JT[n - 2], i)
                else:
                    T.wait_ge(P[name + "_v"].sem, i * P[name + "_v"].n)
                for q in range(4):
                    for c in CH:
                        last = mm(PS[:, 512 * (4 + t) + q * 128:512 * (4 + t) + (q + 1) * 128],
                                  hidT[:, c, q * 128:(q + 1) * 128], w2[:, j, c, :], start=c == 0, stop=c == FC - 1)
                P[name + "_p"].done(last, f"y{j}{t}")

        def moe_scalar(name, gated, i):
            for j, t in JT:
                for c in CH:
                    at(S, name + "_p", f"h{j}{t}{c}", i)
                    if gated:
                        ins = S.activation(g_act[:, c % 2, :], bank(2 * (c % 2)), ACT.Silu)
                    else:
                        ins = S.activation(hidT[:, c, :], bank(2 * (c % 2)), ACT.Relu, bias=b1[:, j, c:c + 1])
                    P[name + "_a"].done(ins, f"h{j}{t}{c}")

        def moe_vector(name, gated, i):
            for j, t in JT:
                if t == 0:
                    vdone(V.tensor_copy(wcol[:, j, :].unsqueeze(2), tok_w[:, :, bass.ds(2 * i + j, 1)]), name + "_v", f"w{j}", i)
                if gated:
                    for c in CH:
                        at(V, name + "_a", f"h{j}{t}{c}", i)
                        P[name + "_v"].done(V.tensor_tensor(hidT[:, c, :], g_act[:, c % 2, :],
                                                            bank(2 * (c % 2) + 1), ALU.mult), f"h{j}{t}{c}")
                at(V, name + "_p", f"y{j}{t}", i)
                for q in range(4):
                    last = V.scalar_tensor_tensor(x[:, 4 * t + q, :],
                                                  PS[:, 512 * (4 + t) + q * 128:512 * (4 + t) + (q + 1) * 128],
                                                  wcol[:, j, 4 * t + q:4 * t + q + 1], x[:, 4 * t + q, :],
                                                  ALU.mult, ALU.add)
                    if q < 3:
                        link(last)
                vdone(last, name + "_v", f"y{j}{t}", i)

        QUANT = ["wi", "wo", "X", "Q", "O", "Y"]

        TG = [(0, 4), (4, 4), (8, 4), (12, 1)]
        progress("pre_p", ["WqT", "WvT"])
        progress("pre_v", ["WqT", "WvT"])
        progress("l0_p", ["xT", "q", "qk"] + [f"ct{b}{n}" for b in range(2) for n in range(4)] + ["s"]
                 + [f"p{n}" for n in range(4)] + ["pc", "y"] + ["axT", "aqk"] + ["a" + s for s in SELF_P + ["oT", "y"]]
                 + ["gxT", "glog"])
        progress("l0_v", ["var", "xn", "xT", "q", "qk", "max", "pc"] + ["avar", "axn", "axT", "aq"]
                 + ["a" + s for s in SELF_V + ["oT"]] + ["gvar", "gxn", "gxT", "ggap", "gend"])
        progress("l0_g", ["rstd", "arstd", "grstd"])
        progress("l0_a", [f"ct{b}{n}" for b in range(2) for n in range(4)] + ["exp"] + [f"p{n}" for n in range(4)]
                 + ["a" + s for s in SELF_A] + ["ggate"])
        ctx_loaded = sem("ctx_loaded")
        ctxT_saved = sem("ctxT_saved")

        progress("q3_p", ["q0", "q1"])
        progress("q3_v", ["qf0", "qf1", "qh", "ql"])
        CS = range(len(CHUNKS))
        MAXIMA = [(p, c) for p in range(8) for c in CS]
        progress("keys_p", [f"k{c}" for c in CS])
        progress("keys_a", [f"kh{c}" for c in CS])
        progress("keys_v", [f"kl{c}" for c in CS])
        progress("vals_p", [f"v{n}" for n in range(4)])
        progress("vals_a", [f"v{n}" for n in range(4)])
        progress("qb_g", ["qb"])
        progress("max_p", [f"m{p}{c}" for p, c in MAXIMA] + ["nm"])
        progress("max_v", [f"m{p}{c}" for p, c in MAXIMA] + ["nm", "nmh", "nml"])
        progress("exp_p", [f"s{k}" for k in range(KT)])
        progress("exp_a", [f"e{k}" for k in range(KT)])
        progress("acc_a", ["acc"])
        progress("pv_p", [f"pv{k}" for k in range(KT)])
        progress("sum_p", ["sum"])
        progress("sum_v", ["sum"])
        progress("fin_g", ["scaled", "own", "added", "on"])
        progress("l1_p", ["cy", "q0", "q1", "k0", "k1", "V"])
        progress("l1_v", ["ct", "q0", "q1", "k0", "k1", "V"])
        progress("s1_p", ["v"][:0] + SELF_P[1:] + ["oT", "y"])
        progress("s1_v", SELF_V + ["oT", "t"])
        progress("s1_a", SELF_A)
        progress("ff_p", [f"f{c}{h}" for c in range(FC) for h in range(2)] + ["fy"])
        progress("ff_a", [f"f{c}{h}" for c in range(FC) for h in range(2)])
        progress("l1_u", ["s"])
        ln_stats, ln_var, ln_rstd, ln_xn, ln_T, ln_xT = (sem("ln_" + n) for n in (
            "statistics", "variance", "rstd", "normalised", "transposed", "copied"))
        mask_stacked = sem("mask_stacked")
        ctxT_loaded = [sem(f"ctxT_loaded{q}") for q in range(2)]
        qs_stacked = sem("qs_stacked")
        ks_stacked = [sem(f"ks_stacked{g}") for g in range(4)]
        nm_stacked = sem("nm_stacked")
        mask_split = sem("mask_split")
        mask_saved = sem("mask_saved")

        moe_progress("e0", True)
        moe_progress("e1", False)

        TS = range(PAIRS)
        progress("qw_v", ["wi", "wo", "quantised", "wiT"])
        progress("qw_p", ["wiT", "woT"])
        progress("qn_v", ["var", "xn", "xT"])
        progress("qn_p", ["xT"])
        progress("qn_g", ["rstd"])
        progress("qx_p", [f"X{s}{h}" for s in range(3) for h in range(2)])
        progress("qx_v", ["X", "Q", "O", "Y", "x"])
        progress("q_all", ["wi", "wo", "X", "Q", "O", "Y"])
        progress("qa_v", ["load"] + SELF_V + ["saved"])
        progress("qa_p", SELF_P)
        progress("qa_a", SELF_A)
        progress("qo_v", ["Oint"] + [f"{s}{t}" for s in ("oT", "y") for t in TS])
        progress("qo_p", [f"{s}{t}" for s in ("oT", "y") for t in TS])
        progress("r_v", ["var", "xn", "xT", "gap", "w", "wT", "end"])
        progress("r_p", ["xT", "log", "wT", "b2"])
        progress("r_g", ["rstd"])
        progress("r_a", ["gate"])
        stored = sem("stored")
        x_updated = sem("x_updated")
        consts_ready = sem("consts_ready")

        ctx.enter_context(nc.allow_non_contiguous_dma(reason="bias columns"))
        block = ctx.enter_context(nc.Block())
        ctx_in = A["ctx_1024"]
        x_view = A["x"].rearrange("b s d -> (b s) d").rearrange("(t p) d -> p t d", p=128)
        out_view = out.rearrange("b s d -> (b s) d").rearrange("(t p) d -> p t d", p=128)
        last_stage = "ABCDEF".index(STOP)

        WLOADS = []
        for name, t in W.items():
            src = A[name]
            if name == "L1_xattn_fo_w":
                src = src.rearrange("(c p) n -> p c n", p=128)
            elif name == "L1_attn_in_w":
                src = src.rearrange("(c p) n -> p c n", p=128)
            WLOADS.append((t, src))
        for name, t in COLS.items():
            WLOADS.append((t, A[name].rearrange("(c p) -> p c", p=128)))
        for name, t in ROWS.items():
            WLOADS.append((t, A[name].partition_broadcast(128)))
        WLOADS.append((router_b, A["L1_ffn_b_router"].partition_broadcast(128)))
        N_W = len(WLOADS) + 1 + 16
        N_ZERO = 8

        def slots(eng, slot):
            for n in (-2, -1, 0):
                slot(n, n % 2)
            with eng.Fori(0, 6) as i:
                slot(2 * i + 1, 1)
                slot(2 * i + 2, 0)
            for n in (13, 14, 15, 16):
                slot(n, n % 2)

        BESIDE = {k: ([], None) for k in range(KT)}
        for k, side, count in ((1, "sum", 3), (2, "v0", 3), (3, "v1", 3), (4, "v2", 4), (5, "v3", 4), (6, "k0", 4),
                               (7, "k1", 4), (8, "k2", 4), (9, "k3", 3), (10, "nm", 0)):
            first = sum(len(b[0]) for b in BESIDE.values())
            maxima = ["m%d%d" % MAXIMA[m] for m in range(first, first + count)]
            BESIDE[k] = (maxima, side)
        IN_BANK7 = ["sum", "v0", "v1", "v2", "v3", "k0", "k1", "k2", "k3", "nm"]

        def present(item, n):
            c = isinstance(n, int)
            if item == "sum":
                return not (c and n < 1)
            if item[0] == "k":
                return not (c and n > 13)
            return not (c and (n < -1 or n > 14))

        def maxima(n, k, half=None):
            m = [item for item in BESIDE[k][0] if present(item, n)]
            return m if half is None else m[2 * half:2 * half + 2] if half == 0 else m[2:]

        def side(n, k):
            item = BESIDE[k][1]
            return [item] if item and present(item, n) else []

        def bank7_free(item, n):
            before = [b for b in IN_BANK7[:IN_BANK7.index(item)] if present(b, n)]
            if before:
                last, m = before[-1], n
            elif isinstance(n, int) and n == 16:
                last, m = "sum", 15
            elif isinstance(n, int) and n == -1:
                last, m = "k3", -2
            elif isinstance(n, int) and n < -1:
                return
            else:
                last, m = "nm", n - 1
            if last == "sum":
                at(nc.tensor, "sum_v", "sum", m - 1)
            elif last[0] == "v":
                at(nc.tensor, "vals_a", last, m + 1)
            elif last[0] == "k":
                at(nc.tensor, "keys_v", "kl" + last[1], m + 2)
            else:
                at(nc.tensor, "max_v", "nml", m + 1)

        def load_context(n, q):
            nc.sync.dma_start(ctxT[:, q, 0:KEYS], scratch[bass.ds(n, 1), :, :].rearrange("b p k -> (b p) k")
                              ).then_inc(ctxT_loaded[q], 16)

        def sync_slot(n, q):
            c = isinstance(n, int)
            if not (c and n > 14):
                stack = KS[1 - q]
                if c and n <= 0:
                    at(nc.sync, "keys_v", "kl3", n + 1)
                else:
                    at(nc.sync, "exp_p", f"s{KT - 1}", n - 1)
                nc.sync.dma_start(stack[98:100, :, :].bitcast(F32),
                                  mask_parts[:, bass.ds(n + 1, 1), :].broadcast_to([2, 4, KPAD])).then_inc(mask_stacked, 16)
                for g in range(4):
                    for k, src in enumerate((kh, kh, kl)):
                        nc.sync.dma_start(stack[32 * k:32 * k + 32, g, 0:KEYS].bitcast(F32),
                                          src[32 * g:32 * g + 32, 0:KEYS].bitcast(F32)).then_inc(ks_stacked[g], 16)
                if not (c and n > 12):
                    at(nc.sync, "vals_p", "v3", n + 1)
                    load_context(n + 3, 1 - q)
                at(nc.sync, "max_v", "nml", n + 1)
                for k, src in enumerate((nmh, nml)):
                    nc.sync.dma_start(QB[1 - q][96 + k:97 + k, :].rearrange("a (p c) -> a p c", p=8).bitcast(F32),
                                      src[:, :].bitcast(F32)).then_inc(nm_stacked, 16)

        @block.sync
        def _(sp):
            sp.dma_start(x[:, :, :], x_view).then_inc(x_loaded, 16)
            sp.dma_start(consts[:, :], A["consts"]).then_inc(consts_loaded, 16)
            for t, src in WLOADS:
                dst = t[:, :, :] if len(t.shape) == 3 else t[:, :]
                sp.dma_start(dst, src).then_inc(loads, 16)
            sp.dma_start(mask_sb[:, 0:KEYS], A["mask_Bx1x1xS2_ff0"].rearrange("b o q k -> b (o q k)")).then_inc(loads, 16)
            sp.wait_ge(consts_ready, 1)
            for r in range(2):
                for j in range(4):
                    ch = 16 * (4 * r + j)
                    sp.dma_start(co_w[32 * j:32 * j + 16, r, :], A["L1_xattn_co_w"][ch:ch + 16, :]).then_inc(loads, 16)
                    sp.dma_start(cv_b[32 * j:32 * j + 16, r:r + 1],
                                 A["L1_xattn_cv_b"][ch:ch + 16].rearrange("(p a) -> p a", a=1)).then_inc(loads, 16)
            sp.wait_ge(mask_split, 3)
            for k, src in enumerate((mask_hi, mask_lo)):
                sp.dma_start(mask_parts[k], src[:, :].bitcast(F32)).then_inc(mask_saved, 16)
            with sp.Fori(0, PAIRS) as i:
                sp.wait_ge(P["l0_v"].sem, i * P["l0_v"].n)
                for b in range(2):
                    row = ctx_in[bass.ds(2 * i + b, 1), :, :].rearrange("b k d -> (b k) d")
                    sp.dma_start(ctx_nat[:, b, 0:FULL, :], row[0:FULL * 128, :].rearrange("(p t) d -> p t d", t=FULL)
                                 ).then_inc(ctx_loaded, 16)
                    sp.dma_start(ctx_nat[0:TAIL, b, FULL, :], row[FULL * 128:KEYS, :]).then_inc(ctx_loaded, 16)
                for b in range(2):
                    at(sp, "l0_a", f"ct{b}3", i)
                    sp.dma_start(scratch[bass.ds(2 * i + b, 1), :, :].rearrange("b p k -> (b p) k"), ctxT[:, b, 0:KEYS]
                                 ).then_inc(ctxT_saved, 16)
            if last_stage >= 2:
                moe_sync(sp, "e0", (A["L0_ffn_experts_w1"], A["L0_ffn_experts_w3"], A["L0_ffn_experts_w2"], None))
            if last_stage >= 3:
                sp.wait_ge(ctxT_saved, 16 * BATCH)
                sp.wait_ge(consts_ready, 1)
                sp.wait_ge(mask_saved, 32)
                for b in range(2):
                    load_context(b, b)
                at(sp, "q3_v", "ql")
                for g in range(4):
                    for k, src in enumerate((qh, ql, qh)):
                        sp.dma_start(QS[32 * k:32 * k + 32, g, :].bitcast(F32), src[32 * g:32 * g + 32, :].bitcast(F32)
                                     ).then_inc(qs_stacked, 16)
                sync_slot(-1, 1)
                sync_slot(0, 0)
                with sp.Fori(0, 6) as i:
                    sync_slot(2 * i + 1, 1)
                    sync_slot(2 * i + 2, 0)
                for n in (13, 14, 15):
                    sync_slot(n, n % 2)
            if last_stage >= 5:
                sp.wait_ge(P["e0_v"].sem, 4 * P["e0_v"].n)
                at(sp, "l1_u", "s")
                moe_sync(sp, "e1", (A["L1_ffn_W1"], None, A["L1_ffn_W2"], A["L1_ffn_b1"]))
            if last_stage >= 5:
                sp.wait_ge(P["e1_v"].sem, 4 * P["e1_v"].n)
            elif last_stage == 4:
                sp.wait_ge(P["qx_v"].sem, P["qx_v"].n)
            elif last_stage == 3:
                sp.wait_ge(x_updated, 1)
            elif last_stage == 2:
                sp.wait_ge(P["e0_v"].sem, 4 * P["e0_v"].n)
            else:
                sp.wait_ge(P["l0_v"].sem, PAIRS * P["l0_v"].n)
            sp.dma_start(out_view, x[:, :, :]).then_inc(stored, 16)
            sp.wait_ge(stored, 16)
            sp.wait_ge(ctxT_saved, 16 * BATCH)

        @block.gpsimd
        def _(g):
            G.memset(co_w[:, :, :], 0.0)
            G.memset(cv_b[:, :], 0.0).then_inc(consts_ready, 1)
            g.wait_ge(consts_loaded, 16)
            with g.Fori(0, PAIRS) as i:
                for pre in ("", "a", "g"):
                    ln_gpsimd("l0", pre, i)
            if last_stage >= 3:
                g.wait_ge(P["l0_v"].sem, PAIRS * P["l0_v"].n)
                g.wait_ge(P["e0_v"].sem, 4 * P["e0_v"].n)
                G.memset(VA[0], 1.0).then_inc(consts_ready, 1)
                G.memset(VA[1], 1.0).then_inc(consts_ready, 1)
                ln_all_gpsimd(0)
                g.wait_ge(qs_stacked, 16 * 12)

                def slot(n, q):
                    c = isinstance(n, int)
                    if not (c and (n < -1 or n > 14)):
                        if not (c and n < 1):
                            at(G, "exp_p", f"s{KT - 1}", n - 1)
                        apart_g(n, 0 + 3 * q)
                        P["qb_g"].done(G.tensor_tensor(QB[1 - q][:, :].rearrange("p (g h q) -> p g h q", g=4, h=4),
                                       QS[:, :, bass.ds(SEQ * (n + 1), SEQ)].unsqueeze(2).broadcast_to([128, 4, 4, SEQ]),
                                       consts[:, C_QM:C_QM + 4].unsqueeze(1).unsqueeze(3).broadcast_to([128, 4, 4, SEQ]),
                                       ALU.mult), "qb")
                    if not (c and n < 1):
                        m = n - 1
                        at(G, "sum_v", "sum", m)
                        P["fin_g"].done(G.tensor_tensor(rsum, acc_sb, rsum, ALU.mult), "scaled")
                        at(G, "fin_g", "scaled", m)
                        r4 = rsum.rearrange("p (r h q) -> p r h q", r=2, h=2)
                        P["fin_g"].done(G.tensor_tensor(r4, r4, consts[:, C_OM:C_OM + 2].unsqueeze(1).unsqueeze(3)
                                                        .broadcast_to([128, 2, 2, SEQ]), ALU.mult), "own")
                        at(G, "fin_g", "own", m)
                        apart_g(n, 1 + 3 * q)
                        o3 = onT[:, :, bass.ds(SEQ * m, SEQ)]
                        P["fin_g"].done(G.tensor_tensor(o3, r4[:, :, 0, :], r4[:, :, 1, :], ALU.add), "added")
                        at(G, "fin_g", "added", m)
                        apart_g(n, 2 + 3 * q)
                        P["fin_g"].done(G.tensor_tensor(o3, o3, cv_b[:, :].unsqueeze(2).broadcast_to([128, 2, SEQ]), ALU.add), "on")

                slots(g, slot)
                for r in (1, 2, 3):
                    ln_all_gpsimd(r)
            if last_stage >= 4:
                def all_max(k, step, stage):
                    at(G, stage, step)
                    P["q_all"].done(G.partition_all_reduce(gmax[:, k:k + 1], amax[:, k:k + 1], 128, ABSMAX),
                                    QUANT[k])

                all_max(0, "wi", "qw_v")
                all_max(1, "wo", "qw_v")
                with g.Fori(0, PAIRS) as i:
                    ln_gpsimd("qn", "", i)
                all_max(2, "X", "qx_v")
                all_max(3, "Q", "qx_v")
                all_max(4, "O", "qx_v")
                all_max(5, "Y", "qx_v")
            if last_stage >= 5:
                with g.Fori(0, PAIRS) as i:
                    ln_gpsimd("r", "", i)

        @block.scalar
        def _(act):
            act.wait_ge(loads, 16 * N_W)
            act.wait_ge(consts_loaded, 16)
            with act.Fori(0, PAIRS) as i:
                for b in range(2):
                    for n, (k0, k) in enumerate(TG):
                        at(S, "l0_p", f"ct{b}{n}", i)
                        w = 512 if n < 3 else TAIL
                        P["l0_a"].done(S.activation(ctxT[:, b, k0 * 128:k0 * 128 + w], bank(4 + n % 2, w), ACT.Copy), f"ct{b}{n}")
                at(S, "l0_v", "max", i)
                P["l0_a"].done(S.activation(P0, PS[:, 0:KEYS], ACT.Exp, bias=l0s[:, 3:4],
                                            scale=float(DIM) ** -0.5, accum_out=l0s[:, 4:5]), "exp")
                for n, (k0, k) in enumerate(TG):
                    at(S, "l0_p", f"p{n}", i)
                    rows = 128 if n < 3 else TAIL
                    P["l0_a"].done(S.activation(P0T[0:rows, k0:k0 + k, :].rearrange("p k q -> p (k q)"),
                                                bank(4 + n % 2, 128 * k, rows), ACT.Copy), f"p{n}")
                self_scalar("l0", "a", i, SEQ)
                route_scalar("l0", "g", i)
            if last_stage >= 2:
                with act.Fori(0, EXPERTS // 2) as i:
                    moe_scalar("e0", True, i)
            if last_stage >= 3:
                act.wait_ge(P["e0_v"].sem, 4 * P["e0_v"].n)
                S.activation(KS[1].rearrange("p g k -> p (g k)"), consts[:, C_KROW:C_KROW + 1].broadcast_to([128, 4 * KPAD]),
                             ACT.Copy).then_inc(consts_ready, 1)
                act.wait_ge(qs_stacked, 16 * 12)
                act.wait_ge(consts_ready, 4)

                def empty(item, n, q):
                    if item[0] == "v":
                        g = int(item[1])
                        k0, k = TG[g]
                        rows = 128 if g < 3 else TAIL
                        at(S, "vals_p", item, n + 1)
                        P["vals_a"].done(S.activation(VA[1 - q][0:rows, k0:k0 + k, :, 0:16], bank(7, 128 * k, rows)
                                                      .rearrange("p (k h c) -> p k h c", k=k, h=8), ACT.Copy), item)
                    if item[0] == "k":
                        c = int(item[1])
                        c0, cw = CHUNKS[c]
                        cw = min(cw, KEYS - c0)
                        at(S, "keys_p", item, n + 2)
                        if c == 0 and not (isinstance(n, int) and n < -1):
                            for g in range(4):
                                act.wait_ge(ks_stacked[g], 48 * (n + 2))
                        P["keys_a"].done(S.activation(kh[:, c0:c0 + cw], bank(7, cw), ACT.Identity,
                                                      bias=COLS["L1_xattn_ck_b"][:, 0:1]), f"kh{c}")

                def slot(n, q):
                    c = isinstance(n, int)
                    for k in range(KT):
                        if not (c and (n < 0 or n > 15)):
                            rows = 128 if k < FULL else TAIL
                            par = (k + q) % 2
                            at(S, "exp_p", f"s{k}", n)
                            if k >= 2:
                                at(S, "pv_p", f"pv{k - 2}", n)
                            elif not (c and n < 1):
                                at(S, "pv_p", f"pv{k + KT - 2}", n - 1)
                            P["exp_a"].done(S.activation(PT[0:rows, par, :], PS[0:rows, 1024 + 1024 * par:2048 + 1024 * par],
                                                         ACT.Exp), f"e{k}")
                        if k == 0 and not (c and n < 1):
                            at(S, "pv_p", f"pv{KT - 1}", n - 1)
                            if not (c and n < 2):
                                at(S, "fin_g", "on", n - 2)
                            P["acc_a"].done(S.activation(acc_sb, bank(6, 256), ACT.Copy), "acc")
                        for item in side(n, k):
                            empty(item, n, q)

                slots(act, slot)
                with act.Fori(0, PAIRS) as i:
                    self_scalar("s1", "", i, SEQ)
                for c in range(FC):
                    for h in range(2):
                        at(S, "ff_p", f"f{c}{h}")
                        P["ff_a"].done(S.activation(hid[:, c, 512 * h:512 * h + 512], bank(2 * (c % 2) + h), ACT.Gelu,
                                                    bias=COLS["L1_xattn_fi_b"][:, c:c + 1]), f"f{c}{h}")
            if last_stage >= 4:
                with act.Fori(0, PAIRS) as i:
                    self_scalar("qa", "", i, 32, unit[:, 0:1])
            if last_stage >= 5:
                with act.Fori(0, PAIRS) as i:
                    route_scalar("r", "", i)
                with act.Fori(0, EXPERTS // 2) as i:
                    moe_scalar("e1", False, i)

        @block.tensor
        def _(pe):
            pe.wait_ge(loads, 16 * N_W)
            pe.wait_ge(consts_loaded, 16)
            P["pre_p"].done(T.transpose(bank(6, 128), W["L0_xattn_Wq"][:, :], ident), "WqT")
            P["pre_p"].done(T.transpose(bank(7, 128), W["L0_xattn_Wv"][:, :], ident), "WvT")
            at(T, "pre_v", "WvT")
            with pe.Fori(0, PAIRS) as i:
                name = "l0_p"
                at(T, "l0_v", "xn", i)
                P[name].done(T.transpose(bank(7, 128), xn[:, :], ident), "xT")
                at(T, "l0_v", "xT", i)
                P[name].done(mm(bank(6, 128), WqT[:, :], xnT[:, :]), "q")
                at(T, "l0_v", "q", i)
                mm(bank(7, 128), W["L0_xattn_Wk"][:, :], l0q[:, :])
                P[name].done(mm(PS[:, 512 * 7 + 256:512 * 7 + 257], l0q[:, :], COLS["L0_xattn_bk"][:, :]), "qk")
                pe.wait_ge(ctx_loaded, 64 * i + 64)
                for b in range(2):
                    for n, (k0, k) in enumerate(TG):
                        m = 4 * b + n
                        if m >= 2:
                            at(T, "l0_a", f"ct{(m - 2) // 4}{(m - 2) % 4}", i)
                        for q in range(k):
                            rows = 128 if k0 + q < FULL else TAIL
                            last = T.transpose(PS[:, 512 * (4 + n % 2) + 128 * q:512 * (4 + n % 2) + 128 * q + rows],
                                               ctx_nat[0:rows, b, k0 + q, :], consts[0:rows, C_ID:C_ID + rows])
                        P[name].done(last, f"ct{b}{n}")
                at(T, "l0_v", "qk", i)
                at(T, "l0_a", "ct13", i)
                for b in range(2):
                    for c0 in range(0, KEYS, 512):
                        w = min(512, KEYS - c0)
                        last = mm(PS[64 * b:64 * b + 64, c0:c0 + w], l0qk[:, 64 * b:64 * b + 64], ctxT[:, b, c0:c0 + w])
                P[name].done(last, "s")
                at(T, "l0_a", "exp", i)
                for n, (k0, k) in enumerate(TG):
                    if n >= 2:
                        at(T, "l0_a", f"p{n - 2}", i)
                    rows = 128 if n < 3 else TAIL
                    for q in range(k):
                        last = T.transpose(PS[0:rows, 512 * (4 + n % 2) + 128 * q:512 * (4 + n % 2) + 128 * q + 128],
                                           P0[:, (k0 + q) * 128:(k0 + q) * 128 + rows], ident)
                    P[name].done(last, f"p{n}")
                at(T, "l0_a", "p3", i)
                for b in range(2):
                    for k in range(KT):
                        rows = 128 if k < FULL else TAIL
                        last = mm(PS[:, 3072 + 64 * b:3136 + 64 * b], ctx_nat[0:rows, b, k, :], P0T[0:rows, k, 64 * b:64 * b + 64],
                                  start=k == 0, stop=k == KT - 1)
                P[name].done(last, "pc")
                at(T, "l0_v", "pc", i)
                P[name].done(mm(bank(7, 128), pcT[:, :], WvT[:, :]), "y")
                at(T, "l0_v", "axn", i)
                P[name].done(T.transpose(bank(7, 128), xn[:, :], ident), "axT")
                at(T, "l0_v", "axT", i)
                mm(PS[:, 0:128], W["L0_attn_W_Q"][:, :], xnT[:, :])
                P[name].done(mm(PS[:, 128:256], W["L0_attn_W_K"][:, :], xnT[:, :]), "aqk")
                self_tensor("l0", "a", i, SEQ, xnT, W["L0_attn_W_V"][:, :], W["L0_attn_W_o"][:, :])
                at(T, "l0_v", "gxn", i)
                P[name].done(T.transpose(bank(7, 128), xn[:, :], ident), "gxT")
                at(T, "l0_v", "gxT", i)
                P[name].done(mm(bank(6, EXPERTS), xnT[:, :], W["L0_ffn_gate"][:, :]), "glog")
            if last_stage >= 2:
                pe.wait_ge(P["l0_v"].sem, PAIRS * P["l0_v"].n)
                with pe.Fori(0, EXPERTS // 2) as i:
                    moe_tensor("e0", True, i)
            if last_stage >= 3:
                pe.wait_ge(P["e0_v"].sem, 4 * P["e0_v"].n)
                pe.wait_ge(consts_ready, 4)
                pe.wait_ge(ln_xn, PAIRS)
                transpose_tensor(0, u_all)
                for h in range(2):
                    pe.wait_ge(ln_xT, h + 1)
                    P["q3_p"].done(mm(bank(h), W["L1_xattn_cq_w"][:, :], xT_all[:, 512 * h:512 * h + 512]), f"q{h}")

                def beside(item, n, q):
                    if item[0] != "m":
                        bank7_free(item, n)
                    if item == "sum":
                        at(T, "acc_a", "acc", n - 1)
                        P["sum_p"].done(mm(bank(7, 256), consts[:, C_SEL:C_SEL + 128], acc_sb), "sum")
                    elif item[0] == "v":
                        g = int(item[1])
                        k0, k = TG[g]
                        for j in range(k):
                            rows = 128 if k0 + j < FULL else TAIL
                            kc = (k0 + j) * 128
                            last = mm(PS[0:rows, 3584 + 128 * j:3584 + 128 * j + 128], ctxT[:, 1 - q, kc:kc + rows], W["L1_xattn_cv_w"][:, :])
                        P["vals_p"].done(last, item)
                    elif item[0] == "k":
                        c0, cw = CHUNKS[int(item[1])]
                        cw = min(cw, KEYS - c0)
                        if item == "k0":
                            pe.wait_ge(ctxT_loaded[q], 8 * (n + 2 - q) + 16)
                        P["keys_p"].done(mm(bank(7, cw), W["L1_xattn_ck_w"][:, :], ctxT[:, q, c0:c0 + cw]), item)
                    elif item == "nm":
                        at(T, "max_v", "nm", n + 1)
                        P["max_p"].done(T.transpose(bank(7, 128, 8), nm[:, :], ident), "nm")
                    else:
                        p, c = int(item[1]), int(item[2])
                        m = 4 * p + c
                        if m == 0:
                            at(T, "qb_g", "qb", n + 1)
                            pe.wait_ge(mask_stacked, 16 * (n + 2))
                        if c == 0 and p % 2 == 0:
                            pe.wait_ge(ks_stacked[p // 2], 48 * (n + 2))
                        if m >= 2:
                            at(T, "max_v", "m%d%d" % MAXIMA[m - 2], n + 1)
                        elif not (isinstance(n, int) and n < 0):
                            at(T, "max_v", "m7%d" % (m + 2), n)
                        c0, cw = CHUNKS[c]
                        P["max_p"].done(mm(bank(m % 2, cw), QB[1 - q][:, 128 * p:128 * p + 128], KS[1 - q][:, p // 2, c0:c0 + cw]), item)

                def values(n, k, q):
                    rows = 128 if k < FULL else TAIL
                    at(T, "exp_a", f"e{k}", n)
                    if k == 0:
                        at(T, "vals_a", "v3", n)
                        if not (isinstance(n, int) and n < 1):
                            at(T, "acc_a", "acc", n - 1)
                    for r in range(2):
                        for j in range(4):
                            p = 4 * r + j
                            last = mm(PS[32 * j:32 * j + 32, 3072 + 128 * r:3200 + 128 * r], VA[q][0:rows, k, p, :],
                                      PT[0:rows, (k + q) % 2, 128 * p:128 * p + 128], start=k == 0 and r == 0,
                                      stop=k == KT - 1, skip_group_check=True, tile_position=(0, 32 * j))
                    P["pv_p"].done(last, f"pv{k}")

                def slot(n, q):
                    c = isinstance(n, int)
                    for k in range(KT):
                        if not (c and (n < 0 or n > 15)):
                            rows = 128 if k < FULL else TAIL
                            par = (k + q) % 2
                            if k == 0:
                                pe.wait_ge(nm_stacked, 32 * (n + 1))
                            if k >= 2:
                                at(T, "exp_a", f"e{k - 2}", n)
                            elif not (c and n < 1):
                                at(T, "exp_a", f"e{k + KT - 2}", n - 1)
                            for g in range(4):
                                o = 1024 + 1024 * par + 256 * g
                                last = mm(PS[0:rows, o:o + 256], KS[q][:, g, 128 * k:128 * k + rows], QB[q][:, 256 * g:256 * g + 256])
                            P["exp_p"].done(last, f"s{k}")
                        for item in maxima(n, k, 0):
                            beside(item, n, q)
                        if k and not (c and (n < 0 or n > 15)):
                            values(n, k - 1, q)
                        if k == 0 and not (c and n < 1):
                            values(n - 1, KT - 1, 1 - q)
                        for item in maxima(n, k, 1) + side(n, k):
                            beside(item, n, q)

                slots(pe, slot)
                at(T, "fin_g", "on", BATCH - 1)
                for t in range(PAIRS):
                    for r in range(2):
                        last = mm(PS[:, 128 * t:128 * t + 128], onT[:, r, 128 * t:128 * t + 128], co_w[:, r, :], start=r == 0, stop=r == 1)
                P["l1_p"].done(last, "cy")
                at(T, "l1_v", "ct")
                transpose_tensor(1, u_all)
                for w, name in ((0, "q"), (1, "k")):
                    for h in range(2):
                        pe.wait_ge(ln_xT, 2 + h + 1)
                        P["l1_p"].done(mm(bank(2 * w + h), W[f"L1_xattn_s{name}_w"][:, :], xT_all[:, 512 * h:512 * h + 512]), f"{name}{h}")
                at(T, "l1_v", "k1")
                for g in range(2 * PAIRS):
                    for r in range(2):
                        last = mm(PS[64 * r:64 * r + 64, 128 * g:128 * g + 128], xT_all[:, 64 * g:64 * g + 64], W["L1_xattn_sv_w"][:, :])
                P["l1_p"].done(last, "V")
                at(T, "l1_v", "V")
                with pe.Fori(0, PAIRS) as i:
                    core_tensor("s1", "", i, SEQ, W["L1_xattn_so_w"][:, :])
                pe.wait_ge(ln_xn, 3 * PAIRS)
                at(T, "l1_u", "s")
                transpose_tensor(2, u_all)
                for c in range(FC):
                    for h in range(2):
                        pe.wait_ge(ln_xT, 4 + h + 1)
                        if c >= 2:
                            at(T, "ff_a", f"f{c - 2}{h}")
                        P["ff_p"].done(mm(bank(2 * (c % 2) + h), W["L1_xattn_fi_w"][:, 128 * c:128 * c + 128],
                                          xT_all[:, 512 * h:512 * h + 512]), f"f{c}{h}")
                at(T, "ff_a", f"f{FC - 1}1")
                for t in range(PAIRS):
                    for c in range(FC):
                        last = mm(PS[:, 2048 + 128 * t:2048 + 128 * t + 128], hid[:, c, 128 * t:128 * t + 128],
                                  W["L1_xattn_fo_w"][:, c, :], start=c == 0, stop=c == FC - 1)
                P["ff_p"].done(last, "fy")

            if last_stage >= 4:
                at(T, "qw_v", "quantised")
                for c in range(3):
                    last = T.transpose(bank(c, 128), W["L1_attn_in_w"][:, c, :], ident)
                P["qw_p"].done(last, "wiT")
                P["qw_p"].done(T.transpose(bank(3, 128), W["L1_attn_out_w"][:, :], ident), "woT")
                with pe.Fori(0, PAIRS) as i:
                    at(T, "qn_v", "xn", i)
                    P["qn_p"].done(T.transpose(bank(7, 128), xn[:, :], ident), "xT")
                pe.wait_ge(P["qn_v"].sem, PAIRS * P["qn_v"].n)
                for s_ in range(3):
                    for h in range(2):
                        P["qx_p"].done(mm(bank(2 * s_ + h), WiT[:, s_, :], xT_all[:, 512 * h:512 * h + 512]), f"X{s_}{h}")
                with pe.Fori(0, PAIRS) as i:
                    at(T, "qa_v", "load", i)
                    self_tensor("qa", "", i, 32, vT_t, ident, None)
                at(T, "qo_v", "Oint")
                for t in TS:
                    if t >= 2:
                        at(T, "qo_v", f"oT{t - 2}")
                    P["qo_p"].done(T.transpose(bank(t % 2, 128), O_all[:, t, :], ident), f"oT{t}")
                for t in TS:
                    at(T, "qo_v", f"oT{PAIRS - 1}" if t < 2 else f"y{t - 2}")
                    P["qo_p"].done(mm(bank(t % 2, 128), OT_all[:, 128 * t:128 * t + 128], WoT), f"y{t}")
            if last_stage >= 5:
                with pe.Fori(0, PAIRS) as i:
                    at(T, "r_v", "xn", i)
                    P["r_p"].done(T.transpose(bank(7, 128), xn[:, :], ident), "xT")
                    at(T, "r_v", "xT", i)
                    P["r_p"].done(mm(bank(6, EXPERTS), xnT[:, :], W["L1_ffn_W_router"][:, :]), "log")
                    at(T, "r_v", "w", i)
                    P["r_p"].done(T.transpose(bank(7, 128, 8), w_t[:, :], ident), "wT")
                    at(T, "r_v", "wT", i)
                    P["r_p"].done(mm(bank(6, 128), w_tT[:, :], W["L1_ffn_b2"][:, :]), "b2")
                pe.wait_ge(P["r_v"].sem, PAIRS * P["r_v"].n)
                with pe.Fori(0, EXPERTS // 2) as i:
                    moe_tensor("e1", False, i)

        @block.vector
        def _(dve):
            dve.wait_ge(loads, 16 * N_W)
            dve.wait_ge(consts_loaded, 16)
            dve.wait_ge(x_loaded, 16)
            at(V, "pre_p", "WqT")
            vdone(V.tensor_copy(WqT[:, :], bank(6, 128)), "pre_v", "WqT")
            at(V, "pre_p", "WvT")
            vdone(V.tensor_copy(WvT[:, :], bank(7, 128)), "pre_v", "WvT")
            link(V.memset(mask_sb[:, KEYS:KPAD], NEG))
            perm_in = mask_sb[:, 0:FULL * 128].rearrange("b (p t) -> b t p", t=FULL)
            for part in range(2):
                if part == 0:
                    link(V.tensor_copy(mask_hi[:, 0:FULL * 128].rearrange("b (t p) -> b t p", t=FULL), perm_in))
                    V.tensor_copy(mask_hi[:, FULL * 128:KPAD], mask_sb[:, FULL * 128:KPAD]).then_inc(mask_split, 1)
                    dve.wait_ge(mask_split, 1)
                else:
                    V.tensor_tensor(mask_lo[:, 0:FULL * 128].rearrange("b (t p) -> b t p", t=FULL), perm_in,
                                    mask_hi[:, 0:FULL * 128].rearrange("b (t p) -> b t p", t=FULL), ALU.subtract).then_inc(mask_split, 1)
                    V.tensor_tensor(mask_lo[:, FULL * 128:KPAD], mask_sb[:, FULL * 128:KPAD], mask_hi[:, FULL * 128:KPAD],
                                    ALU.subtract).then_inc(mask_split, 1)
                    dve.wait_ge(mask_split, 3)
            link(V.tensor_copy(KS[0].rearrange("p g k -> p (g k)"), consts[:, C_KROW:C_KROW + 1].broadcast_to([128, 4 * KPAD])))
            link(V.tensor_copy(QS[:, :, :].rearrange("p g t -> p (g t)"), consts[:, C_QROW:C_QROW + 1].broadcast_to([128, 4 * TOKENS])))

            def phase1(i):
                xt = x[:, bass.ds(i, 1), :].rearrange("p t d -> p (t d)")
                vdone(ln_vector(xt, xn[:, :], "l0", "", i), "l0_v", "xn", i)
                at(V, "l0_p", "xT", i)
                vdone(V.tensor_copy(xnT[:, :], bank(7, 128)), "l0_v", "xT", i)
                at(V, "l0_p", "q", i)
                vdone(V.tensor_scalar(l0q[:, :], bank(6, 128), COLS["L0_xattn_bq"][:, 0:1], None, ALU.add), "l0_v", "q", i)
                at(V, "l0_p", "qk", i)
                link(V.tensor_copy(l0s[:, 0:1], PS[:, 512 * 7 + 256:512 * 7 + 257]))
                vdone(V.tensor_copy(l0qk[:, :], bank(7, 128)), "l0_v", "qk", i)
                at(V, "l0_p", "s", i)
                link(V.reduce_max(l0s[:, 1:2], PS[:, 0:KEYS], AX))
                link(V.tensor_tensor(l0s[:, 2:3], l0s[:, 1:2], l0s[:, 0:1], ALU.add))
                link(V.tensor_tensor(l0s[:, 5:6], l0s[:, 0:1], l0s[:, 2:3], ALU.subtract))
                vdone(V.tensor_scalar(l0s[:, 3:4], l0s[:, 5:6], float(DIM) ** -0.5, None, ALU.mult), "l0_v", "max", i)
                at(V, "l0_a", "exp", i)
                link(V.reciprocal(l0s[:, 6:7], l0s[:, 4:5]))
                at(V, "l0_p", "pc", i)
                vdone(V.tensor_copy(pcT[:, :], bank(6, 128)), "l0_v", "pc", i)
                link(V.tensor_tensor(t1[:, :], xt, ROWS["L0_xattn_bv"][:, :], ALU.add))
                at(V, "l0_p", "y", i)
                link(V.scalar_tensor_tensor(xt, bank(7, 128), l0s[:, 6:7], t1[:, :], ALU.mult, ALU.add))
                vdone(ln_vector(xt, xn[:, :], "l0", "a", i), "l0_v", "axn", i)
                at(V, "l0_p", "axT", i)
                vdone(V.tensor_copy(xnT[:, :], bank(7, 128)), "l0_v", "axT", i)
                at(V, "l0_p", "aqk", i)
                vdone(V.tensor_scalar(qT[:, :], PS[:, 0:128], HD ** -0.5, None, ALU.mult), "l0_v", "aq", i)
                kbd_vector("l0", "a", i, SEQ, PS[:, 128:256], None, PS[:, 512:768])
                core_vector("l0", "a", i, SEQ, causal, None)
                out_vector("l0", "a", i)
                link(V.tensor_tensor(xt, bank(6, 128), xt, ALU.add))
                vdone(ln_vector(xt, xn[:, :], "l0", "g", i), "l0_v", "gxn", i)
                at(V, "l0_p", "gxT", i)
                link(V.tensor_copy(xnT[:, :], bank(7, 128)))
                vdone(V.tensor_copy(xT_all[:, bass.ds(i * 128, 128)], bank(7, 128)), "l0_v", "gxT", i)
                at(V, "l0_p", "glog", i)
                link(V.tensor_copy(lg[:, :], bank(6, EXPERTS)))
                vdone(route_vector(tok_w[:, bass.ds(i, 1), :].rearrange("p t e -> p (t e)"), "l0", "g", i), "l0_v", "gend", i)

            with dve.Fori(0, PAIRS) as i:
                in_loop(i, PER["phase1"], lambda: phase1(i))
            state["links"] += PAIRS * PER["phase1"]

            if last_stage >= 2:
                with dve.Fori(0, EXPERTS // 2) as i:
                    in_loop(i, PER["e0"], lambda: moe_vector("e0", True, i))
                state["links"] += EXPERTS // 2 * PER["e0"]

            flat = "p t d -> p (t d)"

            def rows_of(name):
                return ROWS[name][:, :].unsqueeze(1).broadcast_to([128, PAIRS, 128])

            def post_norm(y, resid, b, g, be, r):
                link(V.tensor_tensor(resid, resid, rows_of(b), ALU.add))
                link(V.tensor_tensor(t_all, y, resid, ALU.add))
                ln_all_vector(r, t_all, t_all)
                link(V.tensor_tensor(t_all, t_all, rows_of(g), ALU.mult))
                return V.tensor_tensor(u_all[:, :, :], t_all, rows_of(be), ALU.add)

            def beside(item, n, q):
                if item == "sum":
                    at(V, "sum_p", "sum", n - 1)
                    if not (isinstance(n, int) and n < 2):
                        at(V, "fin_g", "on", n - 2)
                    P["sum_v"].done(V.reciprocal(rsum, bank(7, 256)), "sum")
                elif item[0] == "k":
                    c = int(item[1])
                    c0, cw = CHUNKS[c]
                    cw = min(cw, KEYS - c0)
                    at(V, "keys_a", f"kh{c}", n + 2)
                    P["keys_v"].done(V.scalar_tensor_tensor(kl[:, c0:c0 + cw], bank(7, cw), COLS["L1_xattn_ck_b"][:, 0:1],
                                                            kh[:, c0:c0 + cw], ALU.add, ALU.subtract), f"kl{c}")
                elif item == "nm":
                    at(V, "max_v", f"m73", n + 1)
                    vdone(V.tensor_reduce(nm[:, :], mx[:, :, :], AX, ALU.max, negate=True), "max_v", "nm", n + 1)
                    at(V, "max_p", "nm", n + 1)
                    vdone(V.tensor_copy(nmh[:, :], bank(7, 128, 8)), "max_v", "nmh", n + 1)
                    vdone(V.tensor_tensor(nml[:, :], bank(7, 128, 8), nmh[:, :], ALU.subtract), "max_v", "nml", n + 1)
                elif item[0] == "m":
                    p, c = int(item[1]), int(item[2])
                    at(V, "max_p", item, n + 1)
                    P["max_v"].done(V.reduce_max(mx[:, p, c:c + 1], bank((4 * p + c) % 2, CHUNKS[c][1]), AX), item)

            def slot(n, q):
                for k in range(KT):
                    for item in maxima(n, k, 0) + (side(n, k - 1) if k else []) + maxima(n, k, 1):
                        beside(item, n, q)

            if last_stage >= 3:
                ln_all_vector(0, x, u_all)
                transpose_vector(0)
                for h in range(2):
                    at(V, "q3_p", f"q{h}")
                    vdone(V.tensor_scalar(PT[:, 0, 512 * h:512 * h + 512], bank(h), COLS["L1_xattn_cq_b"][:, 0:1], HD ** -0.5,
                                          ALU.add, ALU.mult), "q3_v", f"qf{h}")
                dve.wait_ge(mask_saved, 32)
                vdone(V.tensor_copy(qh, PT[:, 0, :]), "q3_v", "qh")
                vdone(V.tensor_tensor(ql, PT[:, 0, :], qh, ALU.subtract), "q3_v", "ql")
                dve.wait_ge(qs_stacked, 16 * 12)
                slots(dve, slot)
                at(V, "l1_p", "cy")
                y8 = PS[:, 0:1024].rearrange("p (t d) -> p t d", t=PAIRS)
                vdone(post_norm(y8, u_all[:, :, :], "L1_xattn_co_b", "L1_xattn_co_g", "L1_xattn_co_be", 1), "l1_v", "ct")
                transpose_vector(1)
                for h in range(2):
                    at(V, "l1_p", f"q{h}")
                    P["l1_v"].done(V.tensor_scalar(Q_all[:, 512 * h:512 * h + 512], bank(h), COLS["L1_xattn_sq_b"][:, 0:1], HD ** -0.5,
                                                   ALU.add, ALU.mult), f"q{h}")
                for h in range(2):
                    at(V, "l1_p", f"k{h}")
                    P["l1_v"].done(V.tensor_scalar(K_all[:, 512 * h:512 * h + 512], bank(2 + h), COLS["L1_xattn_sk_b"][:, 0:1], None,
                                                   ALU.add), f"k{h}")
                at(V, "l1_p", "V")
                vdone(V.tensor_tensor(V_all.rearrange("p (g c) -> p g c", g=2 * PAIRS),
                                      PS[:, 0:2048].rearrange("p (g c) -> p g c", g=2 * PAIRS),
                                      consts[:, C_VM2:C_VM2 + 128].unsqueeze(1).broadcast_to([128, 2 * PAIRS, 128]), ALU.mult),
                      "l1_v", "V")

                def self_round(i):
                    link(V.tensor_copy(qT[:, :], Q_all[:, bass.ds(128 * i, 128)]))
                    hm = head_mask.unsqueeze(2).broadcast_to([128, HEADS, SEQ])
                    for g in range(2):
                        src = K_all[:, bass.ds(128 * i + SEQ * g, SEQ)].unsqueeze(1).broadcast_to([128, HEADS, SEQ])
                        last = V.tensor_tensor(kbd[:, 1024 * g:1024 * g + 1024].rearrange("p (h k) -> p h k", h=HEADS), src, hm, ALU.mult)
                        if g == 0:
                            link(last)
                    vdone(last, "s1_v", "kbd", i)
                    vdone(V.tensor_copy(vbd[:, 0:256], V_all[:, bass.ds(256 * i, 256)]), "s1_v", "vbd", i)
                    core_vector("s1", "", i, SEQ, None, ROWS["L1_xattn_sv_b"][:, :])
                    out_vector("s1", "", i)
                    vdone(V.tensor_copy(t_all[:, bass.ds(i, 1), :].rearrange(flat), bank(6, 128)), "s1_v", "t", i)

                with dve.Fori(0, PAIRS) as i:
                    in_loop(i, PER["s1"], lambda: self_round(i))
                state["links"] += PAIRS * PER["s1"]
                vdone(post_norm(t_all, u_all[:, :, :], "L1_xattn_so_b", "L1_xattn_so_g", "L1_xattn_so_be", 2), "l1_u", "s")
                transpose_vector(2)
                at(V, "ff_p", "fy")
                y8 = PS[:, 2048:3072].rearrange("p (t d) -> p t d", t=PAIRS)
                link(post_norm(y8, u_all[:, :, :], "L1_xattn_fo_b", "L1_xattn_fo_g", "L1_xattn_fo_be", 3))
                x_now = x[:, :, :]
                V.tensor_tensor(x_now, x_now, u_all[:, :, :], ALU.add).then_inc(x_updated, 1)
                dve.wait_ge(x_updated, 1)

            def quant_scale(k):
                at(V, "q_all", QUANT[k])
                link(V.tensor_scalar(qscale[:, k:k + 1], gmax[:, k:k + 1], 1.0 / QMAX, 1e-8, ALU.mult, ALU.max))
                link(V.reciprocal(qinv[:, k:k + 1], qscale[:, k:k + 1]))

            def quantise(t, k):
                link(V.tensor_scalar(t, t, qinv[:, k:k + 1], ROUND, ALU.mult, ALU.add))
                link(V.tensor_scalar(t, t, ROUND, QMAX, ALU.subtract, ALU.min))
                return V.tensor_scalar(t, t, -QMAX - 1.0, None, ALU.max)

            def largest(k, src):
                return V.reduce_max(amax[:, k:k + 1], src, AX, apply_absolute_value=True)

            def qn(i):
                xt = x[:, bass.ds(i, 1), :].rearrange("p t d -> p (t d)")
                vdone(ln_vector(xt, xn[:, :], "qn", "", i), "qn_v", "xn", i)
                at(V, "qn_p", "xT", i)
                vdone(V.tensor_copy(xT_all[:, bass.ds(i * 128, 128)], bank(7, 128)), "qn_v", "xT", i)

            def qa(i):
                for s_, dst in enumerate((qT[:, :], kT_t, vT_t)):
                    src = X[:, s_, :].rearrange("p (l s) -> p s l", l=BATCH)[:, bass.ds(8 * i, 8), :]
                    last = V.tensor_copy(dst.rearrange("p (s l) -> p s l", l=BATCH), src)
                    if s_ < 2:
                        link(last)
                vdone(last, "qa_v", "load", i)
                kbd_vector("qa", "", i, 32, kT_t, None, PS[:, 512:1024])
                core_vector("qa", "", i, 32, block_mask, None, qscale[:, 2:3])
                vdone(V.tensor_copy(O_all[:, bass.ds(i, 1), :].rearrange("p t d -> p (t d)"), o_sb[:, :]), "qa_v", "saved", i)

            if last_stage >= 4:
                wi = W["L1_attn_in_w"][:, :, :].rearrange("p c n -> p (c n)")
                wo = W["L1_attn_out_w"][:, :]
                vdone(largest(0, wi), "qw_v", "wi")
                vdone(largest(1, wo), "qw_v", "wo")
                quant_scale(0)
                link(quantise(wi, 0))
                quant_scale(1)
                vdone(quantise(wo, 1), "qw_v", "quantised")
                at(V, "qw_p", "woT")
                for c in range(3):
                    link(V.tensor_copy(WiT[:, c, :], bank(c, 128)))
                vdone(V.tensor_copy(WoT, bank(3, 128)), "qw_v", "wiT")
                with dve.Fori(0, PAIRS) as i:
                    in_loop(i, PER["qn"], lambda: qn(i))
                state["links"] += PAIRS * PER["qn"]
                for s_ in range(3):
                    for h in range(2):
                        at(V, "qx_p", f"X{s_}{h}")
                        link(V.tensor_scalar(X[:, s_, 512 * h:512 * h + 512], bank(2 * s_ + h), qscale[:, 0:1],
                                             COLS["L1_attn_in_b"][:, s_:s_ + 1], ALU.mult, ALU.add))
                Xf = X[:, :, :].rearrange("p s t -> p (s t)")
                vdone(largest(2, Xf), "qx_v", "X")
                quant_scale(2)
                link(quantise(Xf, 2))
                link(V.tensor_scalar(X[:, 0, :], X[:, 0, :], qscale[:, 2:3], HD ** -0.5, ALU.mult, ALU.mult))
                vdone(largest(3, X[:, 0, :]), "qx_v", "Q")
                quant_scale(3)
                link(quantise(X[:, 0, :], 3))
                link(V.tensor_tensor(unit[:, 0:1], qscale[:, 2:3], qscale[:, 3:4], ALU.mult))
                with dve.Fori(0, PAIRS) as i:
                    in_loop(i, PER["qa"], lambda: qa(i))
                state["links"] += PAIRS * PER["qa"]
                Of = O_all.rearrange("p t d -> p (t d)")
                vdone(largest(4, Of), "qx_v", "O")
                quant_scale(4)
                vdone(quantise(Of, 4), "qo_v", "Oint")
                link(V.tensor_tensor(unit[:, 1:2], qscale[:, 1:2], qscale[:, 4:5], ALU.mult))
                for t in TS:
                    at(V, "qo_p", f"oT{t}")
                    P["qo_v"].done(V.tensor_copy(OT_all.rearrange("p (l s) -> p s l", l=BATCH)[:, 8 * t:8 * t + 8, :],
                                                 bank(t % 2, 128).rearrange("p (s l) -> p s l", l=BATCH)), f"oT{t}")
                for t in TS:
                    at(V, "qo_p", f"y{t}")
                    P["qo_v"].done(V.scalar_tensor_tensor(Y_all[:, t, :], bank(t % 2, 128), unit[:, 1:2],
                                                          ROWS["L1_attn_out_b"][:, :], ALU.mult, ALU.add), f"y{t}")
                at(V, "qo_v", f"y{PAIRS - 1}")
                Yf = Y_all.rearrange("p t d -> p (t d)")
                vdone(largest(5, Yf), "qx_v", "Y")
                quant_scale(5)
                link(quantise(Yf, 5))
                xf = x[:, :, :].rearrange("p t d -> p (t d)")
                vdone(V.scalar_tensor_tensor(xf, Yf, qscale[:, 5:6], xf, ALU.mult, ALU.add), "qx_v", "x")

            def route(i):
                xt = x[:, bass.ds(i, 1), :].rearrange("p t d -> p (t d)")
                vdone(ln_vector(xt, xn[:, :], "r", "", i), "r_v", "xn", i)
                at(V, "r_p", "xT", i)
                link(V.tensor_copy(xT_all[:, bass.ds(i * 128, 128)], bank(7, 128)))
                vdone(V.tensor_copy(xnT[:, :], bank(7, 128)), "r_v", "xT", i)
                at(V, "r_p", "log", i)
                link(V.tensor_tensor(lg[:, :], bank(6, EXPERTS), router_b[:, :], ALU.add))
                vdone(route_vector(w_t[:, :], "r", "", i), "r_v", "w", i)
                link(V.tensor_copy(tok_w[:, bass.ds(i, 1), :].rearrange("p t e -> p (t e)"), w_t[:, :]))
                at(V, "r_p", "wT", i)
                vdone(V.tensor_copy(w_tT[:, :], bank(7, 128, 8)), "r_v", "wT", i)
                at(V, "r_p", "b2", i)
                vdone(V.tensor_tensor(xt, xt, bank(6, 128), ALU.add), "r_v", "end", i)

            if last_stage >= 5:
                with dve.Fori(0, PAIRS) as i:
                    in_loop(i, PER["route"], lambda: route(i))
                state["links"] += PAIRS * PER["route"]
                with dve.Fori(0, EXPERTS // 2) as i:
                    in_loop(i, PER["e1"], lambda: moe_vector("e1", False, i))


PER = {"phase1": 29, "e0": 12, "s1": 6, "e1": 12, "qn": 2, "qa": 10, "route": 13}


def constants():
    import numpy as np
    c = np.zeros((128, C_END), np.float32)
    p = np.arange(128)
    c[:, C_ID:C_ID + 128] = np.eye(128)
    c[:, C_HM:C_HM + 16] = p[:, None] // HD == np.arange(16)[None]
    ch = np.arange(128)[None] // HD
    c[:, C_VM2:C_VM2 + 128] = ch % 2 == p[:, None] // 64
    c[:, C_VM4:C_VM4 + 128] = ch % 4 == p[:, None] // 32
    c[:, C_CAUSAL:C_CAUSAL + 64] = np.where(np.arange(64)[None] <= p[:, None] % 64, 0.0, NEG)
    c[:, C_BLK:C_BLK + 32] = np.where(np.arange(32)[None] // 16 == (p[:, None] % 32) // 16, 0.0, NEG)
    c[:, C_QM:C_QM + 4] = np.where(p[:, None] < 96, (p[:, None] % 32) // HD == np.arange(4)[None], 1.0)
    c[:, C_SEL:C_SEL + 128] = p[:, None] == 32 * (p[None] // 32) + 16
    c[:, C_OM:C_OM + 2] = (p[:, None] % 32 < 16) & ((p[:, None] % 32) // HD == np.arange(2)[None])
    c[:, C_IOTA:C_IOTA + 8] = np.arange(8)[None]
    c[:, C_KROW] = (p == 96) | (p == 97)
    c[:, C_QROW] = (p == 98) | (p == 99)
    c[:, C_HALF] = -0.5
    return c


NAMES = [
    "x", "ctx_1024", "mask_Bx1x1xS2_ff0", "L0_xattn_Wq", "L0_xattn_bq", "L0_xattn_Wk", "L0_xattn_bk", "L0_xattn_Wv",
    "L0_xattn_bv", "L0_attn_W_Q", "L0_attn_W_K", "L0_attn_W_V", "L0_attn_W_o", "L0_ffn_gate", "L0_ffn_experts_w1",
    "L0_ffn_experts_w2", "L0_ffn_experts_w3", "L1_xattn_cq_w", "L1_xattn_cq_b", "L1_xattn_ck_w", "L1_xattn_ck_b",
    "L1_xattn_cv_w", "L1_xattn_cv_b", "L1_xattn_co_w", "L1_xattn_co_b", "L1_xattn_co_g", "L1_xattn_co_be",
    "L1_xattn_sq_w", "L1_xattn_sq_b", "L1_xattn_sk_w", "L1_xattn_sk_b", "L1_xattn_sv_w", "L1_xattn_sv_b",
    "L1_xattn_so_w", "L1_xattn_so_b", "L1_xattn_so_g", "L1_xattn_so_be", "L1_xattn_fi_w", "L1_xattn_fi_b",
    "L1_xattn_fo_w", "L1_xattn_fo_b", "L1_xattn_fo_g", "L1_xattn_fo_be", "L1_attn_in_w", "L1_attn_in_b",
    "L1_attn_out_w", "L1_attn_out_b", "L1_ffn_W_router", "L1_ffn_b_router", "L1_ffn_W1", "L1_ffn_b1", "L1_ffn_W2",
    "L1_ffn_b2"]


def kernel(**inputs):
    import numpy as np
    import concourse.bacc as bacc
    from concourse.bass_utils import run_bass_kernel_spmd as run

    nc = bacc.Bacc("TRN2", target_bir_lowering=False, num_devices=1)
    arrays = {name: np.ascontiguousarray(inputs[name]) for name in NAMES}
    arrays["consts"] = constants()
    aps = {name: nc.dram_tensor("in_" + name, a.shape, F32, kind="ExternalInput").ap() for name, a in arrays.items()}
    out = nc.dram_tensor("out_0", (BATCH, SEQ, DIM), F32, kind="ExternalOutput").ap()
    scratch = nc.dram_tensor("context_transposed", (BATCH, 128, KEYS), F32, kind="Internal").ap()
    mask_parts = nc.dram_tensor("mask_parts", (2, BATCH, KPAD), F32, kind="Internal").ap()
    build(nc, aps, out, scratch, mask_parts)
    r = run(nc, [{"in_" + name: a for name, a in arrays.items()}], core_ids=[0])
    return r.results[0]["out_0"]
```

```python
from contextlib import ExitStack

import concourse.bass as bass
from concourse import mybir

F32 = mybir.dt.float32
F32R = mybir.dt.float32r
U32 = mybir.dt.uint32
ALU = mybir.AluOpType
ACT = mybir.ActivationFunctionType
AX = mybir.AxisListType.X
ABSMAX = bass.bass_isa.ReduceOp.max

BATCH, SEQ, DIM = 16, 64, 128
TOKENS = BATCH * SEQ
PAIRS = TOKENS // 128
HEADS, HD = 16, 8
KEYS = 1601
FULL = KEYS // 128
TAIL = KEYS - FULL * 128
KT = FULL + 1
KPAD = KEYS + 1
CHUNKS = [(0, 512), (512, 512), (1024, 512), (1536, KPAD - 1536)]
ROUNDS = PAIRS // 2
EXPERTS, FF = 8, 512
FC = FF // 128
EPS = 1e-5
QMAX = 127.0
ROUND = 12582912.0
NEG = -1e30

(C_ID, C_HM, C_VM2, C_CAUSAL, C_BLK, C_QM, C_SEL, C_OM, C_IOTA, C_KROW, C_QROW, C_HALF, C_HEAD,
 C_ONE, C_END) = (0, 128, 144, 272, 336, 400, 404, 532, 534, 542, 543, 544, 545, 547, 548)


class Progress:

    def __init__(self, sem, steps):
        self.sem, self.at, self.n = sem, {s: k + 1 for k, s in enumerate(steps)}, len(steps)
        assert len(self.at) == self.n
        self.steps, self.next = list(steps), 0

    def done(self, ins, step):
        assert self.steps[self.next] == step, (step, self.steps[self.next])
        self.next = (self.next + 1) % self.n
        ins.then_inc(self.sem, 1)

    def value(self, step, i=0):
        return i * self.n + self.at[step]


def build(nc, A, out, scratch, mask_parts):
    ctx = ExitStack()
    with ctx:
        def sb(name, shape, dt=F32):
            return ctx.enter_context(nc.sbuf_tensor(name, shape, dt))

        def sem(name):
            return ctx.enter_context(nc.semaphore(name))

        PS = ctx.enter_context(nc.psum_tensor("PS", [128, 8 * 512], F32))

        def bank(k, n=512, parts=128):
            return PS[0:parts, 512 * k:512 * k + n]

        consts = sb("consts", [128, C_END])
        ident = consts[:, C_ID:C_ID + 128]
        head_mask = consts[:, C_HM:C_HM + 16]
        causal = consts[:, C_CAUSAL:C_CAUSAL + 64]
        block_mask = consts[:, C_BLK:C_BLK + 64]
        minus_half = consts[:, C_HALF:C_HALF + 1]
        iota8 = consts[:, C_IOTA:C_IOTA + 8]

        W = {}
        for name in ("L0_xattn_Wq", "L0_xattn_Wk", "L0_xattn_Wv", "L0_attn_W_Q", "L0_attn_W_K", "L0_attn_W_V",
                     "L0_attn_W_o", "L1_xattn_cq_w", "L1_xattn_ck_w", "L1_xattn_cv_w", "L1_xattn_sq_w",
                     "L1_xattn_sk_w", "L1_xattn_sv_w", "L1_xattn_so_w", "L1_attn_out_w"):
            W[name] = sb("w_" + name, [128, 128])
        W["L1_xattn_fi_w"] = sb("w_fi", [128, FF])
        W["L1_xattn_fo_w"] = sb("w_fo", [128, FC, 128])
        W["L1_attn_in_w"] = sb("w_in", [128, 3, 128])
        W["L0_ffn_gate"] = sb("w_gate", [128, EXPERTS])
        W["L1_ffn_W_router"] = sb("w_router", [128, EXPERTS])
        W["L1_ffn_b2"] = sb("w_b2", [EXPERTS, 128])
        co_w = sb("co_w", [128, 2, 128])
        COLS = {}
        for name, n in (("L0_xattn_bq", 1), ("L0_xattn_bk", 1), ("L1_xattn_cq_b", 1), ("L1_xattn_ck_b", 1),
                        ("L1_xattn_sq_b", 1), ("L1_xattn_sk_b", 1), ("L1_xattn_fi_b", FC), ("L1_attn_in_b", 3)):
            COLS[name] = sb("c_" + name, [128, n])
        cv_b = sb("cv_b", [128, 2])
        ROWS = {}
        for name in ("L0_xattn_bv", "L1_xattn_sv_b", "L1_xattn_co_b", "L1_xattn_co_g", "L1_xattn_co_be",
                     "L1_xattn_so_b", "L1_xattn_so_g", "L1_xattn_so_be", "L1_xattn_fo_b", "L1_xattn_fo_g",
                     "L1_xattn_fo_be", "L1_attn_out_b"):
            ROWS[name] = sb("r_" + name, [128, 128])
        router_b = sb("router_b", [128, EXPERTS])

        x = sb("x", [128, PAIRS, 128])
        xT_all = sb("xT_all", [128, TOKENS])
        tok_w = sb("tok_w", [128, PAIRS, EXPERTS])


        qT = sb("qT", [128, 128])
        prT = sb("prT", [128, 1024])
        smax = sb("smax", [128, HEADS])
        ssum = sb("ssum", [128, HEADS])
        o_sb = sb("o_sb", [128, 128])

        early = sb("early", [128, 2 * KT * 128])
        expert_area = sb("expert_area", [128, 2 * KT * 128])
        ctx_nat = [a[:, :].rearrange("p (b k d) -> p b k d", b=2, k=KT) for a in (early, expert_area)]
        work_area = sb("work_area", [128, 3584 + KT * 256])
        tail_area, value_area = work_area[:, 0:3584], work_area[:, 3584:3584 + KT * 256]
        ctxT = sb("ctxT", [128, 2, KPAD])
        P0 = value_area[:, 0:KEYS]
        P0T = value_area[:, KEYS:KEYS + KT * 128].rearrange("p (k q) -> p k q", k=KT)
        WqT = sb("WqT", [128, 128])
        WvT = sb("WvT", [128, 128])
        l0q, l0qk_all = tail_area[:, 0:TOKENS], tail_area[:, TOKENS:2 * TOKENS]
        l0qk = sb("l0qk", [128, 2, 128])
        qb_all = sb("qb_all", [128, PAIRS])
        l0s = sb("l0s", [128, 8])
        pcT = sb("pcT", [128, 128])

        kh = sb("kh", [128, KPAD], F32R)
        kl = sb("kl", [128, KPAD], F32R)
        KS = [sb("KS0", [128, 4, KPAD], F32R)[:, :, :],
              sb("KS1", [128, 4, KPAD], F32R)[:, :, :]]
        qh, ql = kh[:, 0:TOKENS], kl[:, 0:TOKENS]
        QS = sb("QS", [128, 4, TOKENS], F32R)
        QB = [sb(f"QB{b}", [128, 1024], F32R) for b in range(2)]
        VA = [value_area.rearrange("p (k h c) -> p k h c", k=KT, h=HEADS // 2),
              early[:, :].rearrange("p (k h c) -> p k h c", k=KT, h=HEADS // 2)]
        PT = sb("PT", [128, 2, 1024])
        mask_sb = PT[0:BATCH, :, :].rearrange("p a n -> p (a n)")[:, 0:KPAD]
        mask_hi, mask_lo = kh[0:BATCH, :], kl[0:BATCH, :]
        mx = sb("mx", [128, 8, 4])
        nm = sb("nm", [128, 8])
        nmh = sb("nmh", [8, 128], F32R)
        nml = sb("nml", [8, 128], F32R)
        acc_sb, rsum = prT[:, 0:256], prT[:, 256:512]
        u_all = sb("u_all", [128, PAIRS, 128])
        stats_all = sb("stats_all", [128, PAIRS, 6])
        mv_all = sb("mv_all", [128, PAIRS, 2])
        var_all = sb("var_all", [128, PAIRS])
        rstd_all = sb("rstd_all", [128, PAIRS])

        w1 = expert_area[:, 0:2 * FF].rearrange("p (j f) -> p j f", j=2)
        w3 = expert_area[:, 2 * FF:4 * FF].rearrange("p (j f) -> p j f", j=2)
        w2 = expert_area[:, 4 * FF:6 * FF].rearrange("p (j c n) -> p j c n", j=2, c=FC)
        onT = expert_area[:, 0:2 * TOKENS].rearrange("p (r t) -> p r t", r=2)
        b1 = sb("b1", [128, 2, FC])
        g_act = P0[:, 0:1024].rearrange("p (a n) -> p a n", a=2)
        hidT = [a.rearrange("p (c n) -> p c n", c=FC)
                for a in (PT[:, :, :].rearrange("p a n -> p (a n)"), tail_area[:, 0:FC * 512])]
        split_x = [q[:, :] for q in QB]
        split_w = [[[QS[:, 2 * j + k, 512 * part:512 * part + 512] for part in range(2)] for k in range(2)] for j in range(2)]
        one = consts[:, C_ONE:C_ONE + 1]
        wcol = sb("wcol", [128, 2, PAIRS])
        top8 = sb("top8", [128, PAIRS, 8])
        topi = sb("topi", [128, PAIRS, 8], U32)
        gates = sb("gates", [128, 4, PAIRS, 2])
        den = sb("den", [128, PAIRS])
        hot = sb("hot", [128, PAIRS, EXPERTS])
        lg = sb("lg", [128, PAIRS, EXPERTS])

        nat_l1 = ctxT[:, :, :].rearrange("p b k -> p (b k)")
        Q_all, K_all = nat_l1[:, 0:TOKENS], nat_l1[:, TOKENS:2 * TOKENS]
        t_all = nat_l1[:, 2 * TOKENS:3 * TOKENS].rearrange("p (t d) -> p t d", t=PAIRS)
        hid = work_area[:, 0:FC * TOKENS].rearrange("p (c n) -> p c n", c=FC)
        V_all = expert_area[:, 0:2 * TOKENS]

        LANE = [dict(kbd=tail_area[:, 0:2048], pr=tail_area[:, 2048:3072], prT=prT[:, :],
                     values=tail_area[:, 3072:3360], bank=0),
                dict(kbd=PT[:, :, :].rearrange("p a n -> p (a n)"), pr=value_area[:, 0:1024],
                     prT=value_area[:, 1024:2048], values=value_area[:, 2048:2336], bank=4)]
        LANE[0].update(q=qT[:, :], smax=smax[:, :], ssum=ssum[:, :])
        LANE[1].update(q=o_sb[:, :], smax=sb("smax1", [128, HEADS])[:, :], ssum=sb("ssum1", [128, HEADS])[:, :])

        X = ctxT[:, :, :].rearrange("p b k -> p (b k)")[:, 0:3 * TOKENS].rearrange("p (s t) -> p s t", s=3)
        Y_all = PT[:, 0, :].rearrange("p (t d) -> p t d", t=PAIRS)
        WiT = early[:, 0:384].rearrange("p (c n) -> p c n", c=3)
        WoT = early[:, 384:512]
        xmax = sb("xmax", [128, 3])
        amax = sb("amax", [128, 8])
        gmax = sb("gmax", [128, 8])
        qscale = sb("qscale", [128, 8])
        qinv = sb("qinv", [128, 8])
        unit = sb("unit", [128, 2])
        blank = sb("blank", [128, 1])
        blank_g = sb("blank_g", [128, 6])
        w_tT = prT[0:EXPERTS, :]

        P = {}

        def progress(name, steps):
            P[name] = Progress(sem(name), steps)

        def at(eng, name, step, i=0):
            eng.wait_ge(P[name].sem, P[name].value(step, i))

        loads = sem("weights_loaded")
        first_loads = sem("first_weights_loaded")
        mask_loaded = sem("mask_loaded")
        consts_loaded = sem("consts_loaded")
        x_loaded = sem("x_loaded")
        dve_link = sem("dve_link")
        state = {"links": 0, "base": 0}

        def link(ins):
            ins.then_inc(dve_link, 1)
            state["links"] += 1
            nc.vector.wait_ge(dve_link, state["base"] + state["links"])

        def vdone(ins, name, step, i=0):
            P[name].done(ins, step)
            at(nc.vector, name, step, i)

        def in_loop(i, per_round, body):
            base, start = state["base"], state["links"]
            state["base"], state["links"] = base + start + i * per_round, 0
            body()
            assert state["links"] == per_round, (state["links"], per_round)
            state["base"], state["links"] = base, start

        def apart():
            nc.vector.memset(blank[:, :], 0.0)

        def apart_g(n, k):
            if not isinstance(n, int):
                nc.gpsimd.tensor_tensor(blank_g[:, k:k + 1], consts[:, 0:1], consts[:, 0:1], ALU.mult)

        V, T, S, G = nc.vector, nc.tensor, nc.scalar, nc.gpsimd

        def mm(o, l, r, start=True, stop=True, **k):
            return T.matmul(o, l, r, start=start, stop=stop, **k)

        def ln_all_vector(r, src, dst):
            for t in range(PAIRS):
                V.bn_stats(stats_all[:, t, :], src[:, t, :]).then_inc(ln_stats, 1)
            V.wait_ge(ln_stats, 2 * PAIRS * r + PAIRS)
            for t in range(PAIRS):
                V.bn_aggr(mv_all[:, t, :], stats_all[:, t, :]).then_inc(ln_stats, 1)
            V.wait_ge(ln_stats, 2 * PAIRS * (r + 1))
            V.tensor_scalar(var_all[:, :].unsqueeze(2), mv_all[:, :, 1:2], EPS, None, ALU.add).then_inc(ln_var, 1)
            V.wait_ge(ln_rstd, r + 1)
            for t in range(PAIRS):
                V.tensor_scalar(dst[:, t, :], src[:, t, :], mv_all[:, t, 0:1], rstd_all[:, t:t + 1],
                                ALU.subtract, ALU.mult).then_inc(ln_xn, 1)
            V.wait_ge(ln_xn, PAIRS * (r + 1))

        def ln_all_gpsimd(r):
            G.wait_ge(ln_var, r + 1)
            G.tensor_tensor(rstd_all[:, :], var_all[:, :], minus_half.broadcast_to([128, PAIRS]), ALU.pow).then_inc(ln_rstd, 1)

        def transpose_vector(r):
            for h in range(2):
                V.wait_ge(ln_T, 2 * r + h + 1)
                V.tensor_copy(xT_all[:, 512 * h:512 * h + 512], bank(6 + h)).then_inc(ln_xT, 1)

        def transpose_tensor(r, src):
            for h in range(2):
                for t in range(4):
                    last = T.transpose(PS[:, 512 * (6 + h) + 128 * t:512 * (6 + h) + 128 * t + 128], src[:, 4 * h + t, :], ident)
                last.then_inc(ln_T, 1)

        def attn_tensor(st, r, wq, wk, wv, wo):
            for w, name in ((wq, "q"), (wk, "k")):
                for h in range(2):
                    T.wait_ge(ln_xT, 2 * r + h + 1)
                    P[st + "_p"].done(mm(bank((0 if name == "q" else 2) + h), w, xT_all[:, 512 * h:512 * h + 512]), f"{name}{h}")
            heads_tensor(st, xT_all[:, :], wv)
            heads_done(nc.tensor, st)
            transpose_heads()
            for t in range(PAIRS):
                if t % 4 == 0:
                    T.wait_ge(heads_copied, 2 * int(st[1]) + t // 4 + 1)
                last = mm(PS[:, 128 * t:128 * t + 128], K_all[:, 128 * t:128 * t + 128], wo)
            P[st + "_p"].done(last, "y")

        def transpose_heads():
            for h in range(2):
                for t in range(4):
                    last = T.transpose(PS[:, 512 * (6 + h) + 128 * t:512 * (6 + h) + 128 * t + 128], t_all[:, 4 * h + t, :], ident)
                last.then_inc(heads_T, 1)

        def heads_tensor(st, src, wv):
            for g in range(2 * PAIRS):
                for h in range(2):
                    last = mm(PS[64 * h:64 * h + 64, 2048 + 128 * g:2176 + 128 * g], src[:, 64 * g:64 * g + 64], wv)
            P[st + "_p"].done(last, "V")
            at(T, st + "_v", "V")
            T.wait_ge(sum_columns, 2 * int(st[1]) + 2)

            def scores(i, lane):
                L, n = LANE[lane], str(lane)
                at(T, st + "_k" + n, "kbd", i)
                at(T, st + "_g" + n, "kbd", i)
                for g in range(2):
                    for c in range(2):
                        last = mm(PS[SEQ * g:SEQ * g + SEQ, 512 * (L["bank"] + c):512 * (L["bank"] + c) + 512],
                                  L["q"][:, SEQ * g:SEQ * g + SEQ], L["kbd"][:, 1024 * g + 512 * c:1024 * g + 512 * c + 512])
                P[st + "_s" + n].done(last, "s")

            def two_tiles(i):
                for lane in range(2):
                    L, n = LANE[lane], str(lane)
                    at(T, st + "_a" + n, "exp", i)
                    for b in range(8):
                        last = T.transpose(PS[:, 512 * (L["bank"] + 2) + 128 * b:512 * (L["bank"] + 2) + 128 * b + 128],
                                           L["pr"][:, 128 * b:128 * b + 128], ident)
                    P[st + "_p" + n].done(last, "pT")
                    if not (isinstance(i, int) and i == ROUNDS - 1):
                        scores(i + 1, lane)
                    at(T, st + "_a" + n, "pT", i)
                    for g in range(2):
                        for b in range(8):
                            last = mm(PS[SEQ * g:SEQ * g + SEQ, 512 * (L["bank"] + 2) + 18 * b:512 * (L["bank"] + 2) + 18 * b + 18],
                                      L["prT"][:, 128 * b + SEQ * g:128 * b + SEQ * g + SEQ],
                                      L["values"][:, 144 * g + 18 * b:144 * g + 18 * b + 18])
                    P[st + "_o" + n].done(last, "o")

            for lane in range(2):
                scores(0, lane)
            two_tiles(0)
            with T.Fori(0, ROUNDS - 2) as i:
                two_tiles(i + 1)
            two_tiles(ROUNDS - 1)

        def heads_done(eng, st):
            if st == "a1":
                at(eng, st + "_v", "o")
            else:
                for lane in "01":
                    at(eng, st + "_v" + lane, "o", ROUNDS - 1)

        def attn_scalar(st, scale=1.0):
            with S.Fori(0, PAIRS // 2) as i:
                for lane in range(2):
                    at(S, st + f"_v{lane}", "sub", i)
                    P[st + f"_a{lane}"].done(S.activation(LANE[lane]["pr"], LANE[lane]["pr"], ACT.Exp, scale=scale), "exp")
                    P[st + f"_a{lane}"].done(
                        S.activation(LANE[lane]["values"].rearrange("p (b c) -> p b c", c=18)[:, :, 0:16],
                                     V_all[:, bass.ds(512 * i + 256 * lane, 256)].rearrange("p (b c) -> p b c", c=16),
                                     ACT.Copy), "values")
                    at(S, st + f"_p{lane}", "pT", i)
                    b = 512 * (LANE[lane]["bank"] + 2)
                    P[st + f"_a{lane}"].done(S.activation(LANE[lane]["prT"], PS[:, b:b + 1024], ACT.Copy), "pT")

        def spread_keys(eng, dst, tile, g):
            hm = head_mask.unsqueeze(2).broadcast_to([128, HEADS, SEQ])
            src = K_all[:, bass.ds(128 * tile + SEQ * g, SEQ)].unsqueeze(1).broadcast_to([128, HEADS, SEQ])
            return eng.tensor_tensor(dst[:, 1024 * g:1024 * g + 1024].rearrange("p (h k) -> p h k", h=HEADS), src, hm, ALU.mult)

        def attn_gpsimd(st):
            with G.Fori(0, PAIRS // 2) as i:
                for lane in range(2):
                    at(G, st + f"_k{lane}", "q", i)
                    apart_g(i, lane)
                    P[st + f"_g{lane}"].done(spread_keys(G, LANE[lane]["kbd"], 2 * i + lane, 1), "kbd")

        def attn_vector(st, q_bias, k_bias, v_bias, mask):
            for h in range(2):
                at(V, st + "_p", f"q{h}")
                dst = Q_all[:, 512 * h:512 * h + 512]
                if q_bias is None:
                    ins = V.tensor_scalar(dst, bank(h), HD ** -0.5, None, ALU.mult)
                else:
                    ins = V.tensor_scalar(dst, bank(h), q_bias, HD ** -0.5, ALU.add, ALU.mult)
                P[st + "_v"].done(ins, f"q{h}")
            for h in range(2):
                at(V, st + "_p", f"k{h}")
                dst = K_all[:, 512 * h:512 * h + 512]
                if k_bias is None:
                    ins = V.tensor_copy(dst, bank(2 + h))
                else:
                    ins = V.tensor_scalar(dst, bank(2 + h), k_bias, None, ALU.add)
                P[st + "_v"].done(ins, f"k{h}")
            at(V, st + "_v", "k1")
            heads_vector(st, mask)
            if v_bias is not None:
                for lane in "01":
                    at(V, st + "_v" + lane, "o", ROUNDS - 1)
                P[st + "_v"].done(V.tensor_tensor(t_all, t_all, v_bias, ALU.add), "o")
            for h in range(2):
                V.wait_ge(heads_T, 2 * int(st[1]) + h + 1)
                V.tensor_copy(K_all[:, 512 * h:512 * h + 512], bank(6 + h)).then_inc(heads_copied, 1)
            at(V, st + "_p", "y")

        def heads_vector(st, mask, unit=None):
            for L in LANE:
                V.tensor_copy(L["values"].rearrange("p (b c) -> p b c", c=18)[:, :, 16:18],
                              consts[:, C_HEAD:C_HEAD + 2].unsqueeze(1).broadcast_to([128, 16, 2])).then_inc(sum_columns, 1)

            def keys(i, lane):
                L = LANE[lane]
                vdone(V.tensor_copy(L["q"], Q_all[:, bass.ds(256 * i + 128 * lane, 128)]), st + f"_k{lane}", "q", i)
                P[st + f"_k{lane}"].done(spread_keys(V, L["kbd"], 2 * i + lane, 0), "kbd")

            def subtract_max(i, lane):
                L = LANE[lane]
                at(V, st + f"_s{lane}", "s", i)
                sc = PS[:, 512 * L["bank"]:512 * L["bank"] + 1024].rearrange("p (h k) -> p h k", h=HEADS)
                p3 = L["pr"].rearrange("p (h k) -> p h k", h=HEADS)
                if mask is not None:
                    link(V.tensor_tensor(p3, sc, mask.unsqueeze(1).broadcast_to([128, HEADS, SEQ]), ALU.add))
                    sc = p3
                link(V.reduce_max(L["smax"], sc, AX))
                P[st + f"_v{lane}"].done(V.tensor_tensor(p3, sc, L["smax"].unsqueeze(2).broadcast_to([128, HEADS, SEQ]),
                                                         ALU.subtract), "sub")

            def normalise(i, lane):
                L = LANE[lane]
                at(V, st + f"_o{lane}", "o", i)
                blocks = PS[:, 512 * (L["bank"] + 2):512 * (L["bank"] + 2) + 144].rearrange("p (b c) -> p b c", c=18)
                s2 = L["ssum"].rearrange("p (b h) -> p b h", h=2)
                link(V.reciprocal(s2, blocks[:, :, 16:18]))
                if unit is not None:
                    link(V.tensor_scalar(L["ssum"], L["ssum"], unit, None, ALU.mult))
                P[st + f"_v{lane}"].done(
                    V.tensor_tensor(t_all[:, bass.ds(2 * i + lane, 1), :].rearrange("p t (b h d) -> p (t b) h d", b=8, h=2),
                                    blocks[:, :, 0:16].rearrange("p b (h d) -> p b h d", h=2),
                                    s2.unsqueeze(3).broadcast_to([128, 8, 2, HD]), ALU.mult), "o")

            def two_tiles(i):
                for lane in range(2):
                    subtract_max(i, lane)
                    if not (isinstance(i, int) and i == ROUNDS - 1):
                        keys(i + 1, lane)
                    if lane == 1:
                        normalise(i, 0)
                    elif not (isinstance(i, int) and i == 0):
                        normalise(i - 1, 1)

            for lane in range(2):
                keys(0, lane)
            at(V, st + "_p", "V")
            vdone(V.tensor_tensor(V_all.rearrange("p (g c) -> p g c", g=2 * PAIRS),
                                  PS[:, 2048:4096].rearrange("p (g c) -> p g c", g=2 * PAIRS),
                                  consts[:, C_VM2:C_VM2 + 128].unsqueeze(1).broadcast_to([128, 2 * PAIRS, 128]), ALU.mult),
                  st + "_v", "V")
            two_tiles(0)
            with V.Fori(0, ROUNDS - 2) as i:
                in_loop(i, PER[st], lambda: two_tiles(i + 1))
            state["links"] += (ROUNDS - 2) * PER[st]
            two_tiles(ROUNDS - 1)
            normalise(ROUNDS - 1, 1)

        def route_tensor(st, r, gate):
            for t in range(PAIRS):
                if t % 4 == 0:
                    T.wait_ge(ln_xT, 2 * r + t // 4 + 1)
                last = mm(bank(4)[:, EXPERTS * t:EXPERTS * (t + 1)], xT_all[:, 128 * t:128 * t + 128], gate)
            P[st + "_p"].done(last, "log")

        def weights_transposed():
            at(T, "r1_v", "w")
            for t in range(PAIRS):
                last = T.transpose(PS[0:EXPERTS, 3072 + 128 * t:3200 + 128 * t], tok_w[:, t, :], ident)
            P["r1_p"].done(last, "wT")

        def biases_weighted():
            at(T, "r1_v", "wT")
            for t in range(PAIRS):
                last = mm(PS[:, 3072 + 128 * t:3200 + 128 * t], w_tT[:, 128 * t:128 * t + 128], W["L1_ffn_b2"][:, :])
            P["r1_p"].done(last, "b2")

        def route_scalar(st):
            at(S, st + "_v", "gap")
            P[st + "_a"].done(S.activation(gates[:, 2, :, :], gates[:, 1, :, :], ACT.Exp), "gate")

        def route_vector(st, bias=None):
            at(V, st + "_p", "log")
            logits = bank(4, EXPERTS * PAIRS).rearrange("p (t e) -> p t e", t=PAIRS)
            if bias is None:
                link(V.tensor_copy(lg[:, :, :], logits))
            else:
                link(V.tensor_tensor(lg[:, :, :], logits, bias.unsqueeze(1).broadcast_to([128, PAIRS, EXPERTS]), ALU.add))
            found = 2 * PAIRS * int(st[1])
            for t in range(PAIRS):
                V.max(top8[:, t, :], lg[:, t, :]).then_inc(top_found, 1)
            V.wait_ge(top_found, found + PAIRS)
            for t in range(PAIRS):
                V.max_index(topi[:, t, :], top8[:, t, :], lg[:, t, :]).then_inc(top_found, 1)
            V.wait_ge(top_found, found + 2 * PAIRS)
            link(V.tensor_copy(gates[:, 0, :, :], topi[:, :, 0:2]))
            vdone(V.tensor_tensor(gates[:, 1, :, :], top8[:, :, 0:2], top8[:, :, 0:1].broadcast_to([128, PAIRS, 2]), ALU.subtract),
                  st + "_v", "gap")
            at(V, st + "_a", "gate")
            link(V.reduce_sum(den[:, :], gates[:, 2, :, :], AX))
            link(V.reciprocal(den[:, :], den[:, :]))
            link(V.tensor_tensor(gates[:, 3, :, :], gates[:, 2, :, :], den[:, :].unsqueeze(2).broadcast_to([128, PAIRS, 2]), ALU.mult))
            every = [128, PAIRS, EXPERTS]
            for k, dst in enumerate((hot[:, :, :], tok_w[:, :, :])):
                link(V.tensor_tensor(dst, iota8.unsqueeze(1).broadcast_to(every), gates[:, 0, :, k:k + 1].broadcast_to(every), ALU.is_equal))
                link(V.tensor_tensor(dst, dst, gates[:, 3, :, k:k + 1].broadcast_to(every), ALU.mult))
            vdone(V.tensor_tensor(tok_w[:, :, :], tok_w[:, :, :], hot[:, :, :], ALU.add), st + "_v", "w")

        CH = range(FC)
        JT = [(j, t) for j in range(2) for t in range(2)]

        EXPERT_STEPS = []
        for n in range(len(JT)):
            EXPERT_STEPS += [("h", n, 0), ("h", n, 1)] + ([("y", n - 1, None)] if n else []) + [("h", n, 2), ("h", n, 3)]
        EXPERT_STEPS.append(("y", len(JT) - 1, None))

        def step_name(kind, n, c):
            return "%s%d%d" % (kind, *JT[n]) + ("" if c is None else str(c))

        def moe_progress(name, gated):
            progress(name + "_p", [step_name(*step) for step in EXPERT_STEPS])
            progress(name + "_a", [step_name(*step) for step in EXPERT_STEPS if step[0] == "h"])
            progress(name + "_v", ["w0", "w1"] + [step_name(*step) for step in EXPERT_STEPS if gated or step[0] == "y"])
            progress(name + "_x", ["hi", "lo"])
            progress(name + "_g", [f"{w}{part}{j}" for j in range(2) for w in (("w1", "w3") if gated else ("w1",))
                                   for part in ("hi", "lo")])
            P[name + "_w"] = [sem(name + f"_weights{j}") for j in range(2)]

        def moe_gpsimd(name, gated, i):
            for j in range(2):
                G.wait_ge(P[name + "_w"][j], 48 * i + 48)
                for k, w in enumerate((w1, w3) if gated else (w1,)):
                    hi, lo = split_w[j][k]
                    P[name + "_g"].done(G.tensor_tensor(hi, w[:, j, :], one.broadcast_to([128, FF]), ALU.mult), f"w{2 * k + 1}hi{j}")
                    at(G, name + "_g", f"w{2 * k + 1}hi{j}", i)
                    P[name + "_g"].done(G.tensor_tensor(lo, w[:, j, :], hi, ALU.subtract), f"w{2 * k + 1}lo{j}")

        def split_tokens(name, r):
            V.wait_ge(ln_xT, 2 * r + 2)
            vdone(V.tensor_copy(split_x[0], xT_all[:, :]), name + "_x", "hi")
            P[name + "_x"].done(V.tensor_tensor(split_x[1], xT_all[:, :], split_x[0], ALU.subtract), "lo")

        def moe_load(name, srcs, e, j):
            W1, W3, W2, B1 = srcs
            ld = P[name + "_w"][j]

            def dma(dst, src):
                nc.sync.dma_start(dst, src).then_inc(ld, 16)

            dma(w1[:, j, :], W1[bass.ds(e, 1), :, :].rearrange("e h f -> (e h) f"))
            dma(w2[:, j, :, :], W2[bass.ds(e, 1), :, :].rearrange("e (c p) n -> p (e c) n", p=128))
            if W3 is not None:
                dma(w3[:, j, :], W3[bass.ds(e, 1), :, :].rearrange("e h f -> (e h) f"))
            else:
                dma(b1[:, j, :], B1[bass.ds(e, 1), :].rearrange("e (c p) -> p (e c)", p=128))

        def moe_sync(sp, name, srcs):
            for j in range(2):
                moe_load(name, srcs, j, j)
            with sp.Fori(0, EXPERTS // 2 - 1) as i:
                for j in range(2):
                    at(sp, name + "_p", f"y{j}1", i)
                    moe_load(name, srcs, 2 * i + 2 + j, j)

        def moe_tensor(name, gated, i, beside={}):
            used = name + ("_v" if gated else "_a")
            for kind, n, c in EXPERT_STEPS:
                j, t = JT[n]
                if kind == "h":
                    if c >= 2:
                        at(T, used, step_name("h", n, c - 2), i)
                    elif n:
                        at(T, used, step_name("h", n - 1, c + 2), i)
                    elif c == 0 and not isinstance(i, int):
                        at(T, name + "_v", "w1", i)
                    if t == 0 and c == 0:
                        at(T, name + "_g", f"w{3 if gated else 1}lo{j}", i)
                    toks = slice(512 * t, 512 * t + 512)
                    for k in range(2 if gated else 1):
                        o = bank(2 * (c % 2) + k)
                        hi, lo = (part[:, 128 * c:128 * c + 128] for part in split_w[j][k])
                        mm(o, hi, split_x[0][:, toks], stop=False)
                        mm(o, hi, split_x[1][:, toks], start=False, stop=False)
                        last = mm(o, lo, split_x[0][:, toks], start=False)
                    P[name + "_p"].done(last, step_name("h", n, c))
                    beside.get((n, c), lambda: None)()
                    continue
                at(T, used, step_name("h", n, 3), i)
                if n == 0 and isinstance(i, int):
                    at(T, name + "_v", "w1", i)
                if n >= 2:
                    at(T, name + "_v", step_name("y", n - 2, None), i)
                for q in range(4):
                    for c in CH:
                        last = mm(PS[:, 512 * (4 + t) + q * 128:512 * (4 + t) + (q + 1) * 128],
                                  hidT[n % 2][:, c, q * 128:(q + 1) * 128], w2[:, j, c, :], start=c == 0, stop=c == FC - 1)
                P[name + "_p"].done(last, step_name("y", n, None))

        def moe_scalar(name, gated, i, beside={}):
            for kind, n, c in EXPERT_STEPS:
                if kind == "y":
                    continue
                at(S, name + "_p", step_name("h", n, c), i)
                if gated:
                    ins = S.activation(g_act[:, c % 2, :], bank(2 * (c % 2)), ACT.Silu)
                else:
                    j = JT[n][0]
                    ins = S.activation(hidT[n % 2][:, c, :], bank(2 * (c % 2)), ACT.Relu, bias=b1[:, j, c:c + 1])
                P[name + "_a"].done(ins, step_name("h", n, c))
                beside.get((n, c), lambda: None)()

        def moe_vector(name, gated, i, first=lambda: None):
            for j in range(2):
                vdone(V.tensor_copy(wcol[:, j, :].unsqueeze(2), tok_w[:, :, bass.ds(2 * i + j, 1)]), name + "_v", f"w{j}", i)
            first()
            for kind, n, c in EXPERT_STEPS:
                j, t = JT[n]
                if kind == "h":
                    if gated:
                        at(V, name + "_a", step_name("h", n, c), i)
                        P[name + "_v"].done(V.tensor_tensor(hidT[n % 2][:, c, :], g_act[:, c % 2, :],
                                                            bank(2 * (c % 2) + 1), ALU.mult), step_name("h", n, c))
                    continue
                at(V, name + "_p", step_name("y", n, None), i)
                for q in range(4):
                    last = V.scalar_tensor_tensor(x[:, 4 * t + q, :],
                                                  PS[:, 512 * (4 + t) + q * 128:512 * (4 + t) + (q + 1) * 128],
                                                  wcol[:, j, 4 * t + q:4 * t + q + 1], x[:, 4 * t + q, :],
                                                  ALU.mult, ALU.add)
                    if q < 3:
                        link(last)
                vdone(last, name + "_v", step_name("y", n, None), i)

        QUANT = ["wi", "wo", "X", "Q", "O", "Y"]

        TG = [(0, 4), (4, 4), (8, 4), (12, 1)]
        progress("pre_p", ["WqT", "WvT"])
        progress("pre_v", ["WqT", "WvT"])
        CT = [(b, g) for b in range(2) for g in range(4)]
        progress("q0_p", ["q0", "q1", "qk", "qb"])
        progress("q0_v", ["q0", "q1", "qk"])
        progress("qk_v", ["qk"])
        progress("ct_p", [f"ct{b}{g}" for b, g in CT])
        progress("ct_a", [f"ct{b}{g}" for b, g in CT])
        progress("ca_p", ["s"] + [f"p{g}" for g in range(4)] + ["pc", "y"])
        progress("ca_v", ["max"] + [f"p{g}" for g in range(4)] + ["pc", "y"])
        progress("ca_a", ["exp"])
        for st in ("a0", "a1", "a2"):
            progress(st + "_p", ["q0", "q1", "k0", "k1", "V", "y"] if st < "a2" else ["V"])
            progress(st + "_v", ["q0", "q1", "k0", "k1", "V", "o"] if st < "a2" else ["V"])
            for lane in "01":
                progress(st + "_s" + lane, ["s"])
                progress(st + "_p" + lane, ["pT"])
                progress(st + "_o" + lane, ["o"])
                progress(st + "_k" + lane, ["q", "kbd"])
                progress(st + "_v" + lane, ["sub", "o"])
                progress(st + "_g" + lane, ["kbd"])
                progress(st + "_a" + lane, ["exp", "values", "pT"])
        for st in ("r0", "r1"):
            progress(st + "_p", ["log"] + (["wT", "b2"] if st == "r1" else []))
            progress(st + "_v", ["gap", "w"] + (["wT", "end"] if st == "r1" else []))
            progress(st + "_a", ["gate"])
        sum_columns = sem("sum_columns")
        top_found = sem("top_found")
        heads_T, heads_copied = sem("heads_transposed"), sem("heads_copied")
        ctx_loaded = [sem(f"ctx_loaded{q}") for q in range(2)]
        ctxT_saved = [sem(f"ctxT_saved{b}") for b in range(2)]

        progress("q3_p", ["q0", "q1"])
        progress("q3_v", ["qf0", "qf1", "qh", "ql"])
        CS = range(len(CHUNKS))
        MAXIMA = [(p, c) for p in range(8) for c in CS]
        progress("keys_p", [f"k{c}" for c in CS])
        progress("keys_a", [f"kh{c}" for c in CS])
        progress("keys_v", [f"kl{c}" for c in CS])
        progress("vals_p", [f"v{n}" for n in range(4)])
        progress("vals_a", [f"v{n}" for n in range(4)])
        progress("qb_g", ["qb"])
        progress("max_p", [f"m{p}{c}" for p, c in MAXIMA] + ["nm"])
        progress("max_v", [f"m{p}{c}" for p, c in MAXIMA] + ["nm", "nmh", "nml"])
        progress("exp_p", [f"s{k}" for k in range(KT)])
        progress("exp_a", [f"e{k}" for k in range(KT)])
        progress("acc_a", ["acc"])
        progress("pv_p", [f"pv{k}" for k in range(KT)])
        progress("sum_p", ["sum"])
        progress("sum_v", ["sum"])
        progress("fin_g", ["scaled", "own", "added", "on"])
        progress("l1_p", ["cy"])
        progress("l1_v", ["ct"])
        progress("ff_p", [f"f{c}{h}" for c in range(FC) for h in range(2)] + ["fy"])
        progress("ff_a", [f"f{c}{h}" for c in range(FC) for h in range(2)])
        progress("l1_u", ["s"])
        ln_stats, ln_var, ln_rstd, ln_xn, ln_T, ln_xT = (sem("ln_" + n) for n in (
            "statistics", "variance", "rstd", "normalised", "transposed", "copied"))
        mask_stacked = sem("mask_stacked")
        ctxT_loaded = [sem(f"ctxT_loaded{q}") for q in range(2)]
        qs_stacked = sem("qs_stacked")
        ks_stacked = [sem(f"ks_stacked{g}") for g in range(4)]
        nm_stacked = sem("nm_stacked")
        mask_split = sem("mask_split")
        mask_padded = sem("mask_padded")
        mask_saved = sem("mask_saved")

        moe_progress("e0", True)
        moe_progress("e1", False)

        progress("qw_v", ["wi", "wo", "quantised", "wiT"])
        progress("qw_p", ["wiT", "woT"])
        progress("qx_p", [f"X{s}{h}" for s in range(3) for h in range(2)])
        progress("qx_v", ["X", "Q", "O", "Y", "x"])
        progress("q_all", ["wi", "wo", "X", "Q", "O", "Y"])
        progress("qo_v", ["V", "Oint"])
        progress("qo_p", ["y"])
        stored = sem("stored")
        x_updated = sem("x_updated")
        consts_ready = sem("consts_ready")
        stacks_ready = sem("stacks_ready")

        ctx.enter_context(nc.allow_non_contiguous_dma(reason="bias columns"))
        block = ctx.enter_context(nc.Block())
        ctx_in = A["ctx_1024"]
        x_view = A["x"].rearrange("b s d -> (b s) d").rearrange("(t p) d -> p t d", p=128)
        out_view = out.rearrange("b s d -> (b s) d").rearrange("(t p) d -> p t d", p=128)

        WLOADS = []
        for name, t in W.items():
            src = A[name]
            if name == "L1_xattn_fo_w":
                src = src.rearrange("(c p) n -> p c n", p=128)
            elif name == "L1_attn_in_w":
                src = src.rearrange("(c p) n -> p c n", p=128)
            WLOADS.append((t, src))
        for name, t in COLS.items():
            WLOADS.append((t, A[name].rearrange("(c p) -> p c", p=128)))
        for name, t in ROWS.items():
            WLOADS.append((t, A[name].partition_broadcast(128)))
        WLOADS.append((router_b, A["L1_ffn_b_router"].partition_broadcast(128)))
        FIRST = [w for w in WLOADS if w[0] in (W["L0_xattn_Wq"], W["L0_xattn_Wk"], W["L0_xattn_Wv"],
                                               COLS["L0_xattn_bq"], COLS["L0_xattn_bk"], ROWS["L0_xattn_bv"])]
        WLOADS = [w for w in WLOADS if w not in FIRST]
        N_W = len(WLOADS) + 16

        def pairs(eng, pair):
            with eng.Fori(0, 3) as i:
                pair(2 * i, 0)
                pair(2 * i + 1, 1)
            pair(6, 0)
            pair(7, 1)

        def slots(eng, slot):
            for n in (-2, -1, 0, 1):
                slot(n, n % 2)
            with eng.Fori(0, 5) as i:
                slot(2 * i + 2, 0)
                slot(2 * i + 3, 1)
            for n in (12, 13, 14, 15, 16):
                slot(n, n % 2)

        BESIDE = {k: ([], None) for k in range(KT)}
        for k, side, count in SCHEDULE:
            first = sum(len(b[0]) for b in BESIDE.values())
            maxima = ["m%d%d" % MAXIMA[m] for m in range(first, first + count)]
            BESIDE[k] = (maxima, side)
        IN_BANK7 = ["sum", "v0", "v1", "v2", "v3", "k0", "k1", "k2", "k3", "nm"]

        def present(item, n):
            c = isinstance(n, int)
            if item == "sum":
                return not (c and n < 1)
            if item[0] == "k":
                return not (c and n > 13)
            return not (c and (n < -1 or n > 14))

        def maxima(n, k, part=None):
            m = [item for item in BESIDE[k][0] if present(item, n)]
            return m if part is None else (m[:2], m[2:])[part]

        def side(n, k):
            item = BESIDE[k][1]
            return [item] if item and present(item, n) else []

        def bank7_free(item, n):
            before = [b for b in IN_BANK7[:IN_BANK7.index(item)] if present(b, n)]
            if before:
                last, m = before[-1], n
            elif isinstance(n, int) and n == 16:
                last, m = "sum", 15
            elif isinstance(n, int) and n == -1:
                last, m = "k3", -2
            elif isinstance(n, int) and n < -1:
                return
            else:
                last, m = "nm", n - 1
            if last == "sum":
                at(nc.tensor, "sum_v", "sum", m - 1)
            elif last[0] == "v":
                at(nc.tensor, "vals_a", last, m + 1)
            elif last[0] == "k":
                at(nc.tensor, "keys_v", "kl" + last[1], m + 2)
            else:
                at(nc.tensor, "max_v", "nml", m + 1)

        def load_pair(n, q):
            for b in range(2):
                row = ctx_in[bass.ds(2 * n + b, 1), :, :].rearrange("b k d -> (b k) d")
                nc.sync.dma_start(ctx_nat[q][:, b, 0:FULL, :], row[0:FULL * 128, :].rearrange("(p t) d -> p t d", t=FULL)
                                  ).then_inc(ctx_loaded[q], 16)
                nc.sync.dma_start(ctx_nat[q][0:TAIL, b, FULL, :], row[FULL * 128:KEYS, :]).then_inc(ctx_loaded[q], 16)

        def load_context(n, q):
            nc.sync.dma_start(ctxT[:, q, 0:KEYS], scratch[bass.ds(n, 1), :, :].rearrange("b p k -> (b p) k")
                              ).then_inc(ctxT_loaded[q], 16)

        def sync_slot(n, q):
            c = isinstance(n, int)
            if not (c and n > 14):
                stack = KS[1 - q]
                if c and n <= 0:
                    at(nc.sync, "keys_v", "kl3", n + 1)
                else:
                    at(nc.sync, "exp_p", f"s{KT - 1}", n - 1)
                nc.sync.dma_start(stack[98:100, :, :].bitcast(F32),
                                  mask_parts[:, bass.ds(n + 1, 1), :].broadcast_to([2, 4, KPAD])).then_inc(mask_stacked, 16)
                for g in range(4):
                    for k, src in enumerate((kh, kh, kl)):
                        nc.sync.dma_start(stack[32 * k:32 * k + 32, g, 0:KEYS].bitcast(F32),
                                          src[32 * g:32 * g + 32, 0:KEYS].bitcast(F32)).then_inc(ks_stacked[g], 16)
                if not (c and n > 12):
                    at(nc.sync, "vals_p", "v3", n + 1)
                    load_context(n + 3, 1 - q)
                at(nc.sync, "max_v", "nml", n + 1)
                for k, src in enumerate((nmh, nml)):
                    nc.sync.dma_start(QB[1 - q][96 + k:97 + k, :].rearrange("a (p c) -> a p c", p=8).bitcast(F32),
                                      src[:, :].bitcast(F32)).then_inc(nm_stacked, 16)

        @block.sync
        def _(sp):
            sp.dma_start(x[:, :, :], x_view).then_inc(x_loaded, 16)
            sp.dma_start(consts[:, :], A["consts"]).then_inc(consts_loaded, 16)
            for t, src in FIRST:
                sp.dma_start(t[:, :], src).then_inc(first_loads, 16)
            load_pair(0, 0)
            sp.dma_start(mask_sb[:, 0:KEYS], A["mask_Bx1x1xS2_ff0"].rearrange("b o q k -> b (o q k)")).then_inc(mask_loaded, 16)
            load_pair(1, 1)
            for t, src in WLOADS:
                dst = t[:, :, :] if len(t.shape) == 3 else t[:, :]
                sp.dma_start(dst, src).then_inc(loads, 16)
            sp.wait_ge(consts_ready, 1)
            for r in range(2):
                for j in range(4):
                    ch = 16 * (4 * r + j)
                    sp.dma_start(co_w[32 * j:32 * j + 16, r, :], A["L1_xattn_co_w"][ch:ch + 16, :]).then_inc(loads, 16)
                    sp.dma_start(cv_b[32 * j:32 * j + 16, r:r + 1],
                                 A["L1_xattn_cv_b"][ch:ch + 16].rearrange("(p a) -> p a", a=1)).then_inc(loads, 16)
            sp.wait_ge(mask_split, 3)
            for k, src in enumerate((mask_hi, mask_lo)):
                sp.dma_start(mask_parts[k], src[:, :].bitcast(F32)).then_inc(mask_saved, 16)

            def save(n):
                for b in range(2):
                    at(sp, "ct_a", f"ct{b}3", n)
                    sp.dma_start(scratch[bass.ds(2 * n + b, 1), :, :].rearrange("b p k -> (b p) k"), ctxT[:, b, 0:KEYS]
                                 ).then_inc(ctxT_saved[b], 16)

            def save_and_load(n, q):
                save(n + 1)
                at(sp, "ca_p", "pc", n)
                load_pair(n + 2, q)

            save(0)
            with sp.Fori(0, 3) as i:
                save_and_load(2 * i, 0)
                save_and_load(2 * i + 1, 1)
            save(7)
            heads_done(sp, "a0")
            moe_sync(sp, "e0", (A["L0_ffn_experts_w1"], A["L0_ffn_experts_w3"], A["L0_ffn_experts_w2"], None))
            for b in range(2):
                sp.wait_ge(ctxT_saved[b], 16 * PAIRS)
            sp.wait_ge(consts_ready, 1)
            sp.wait_ge(mask_saved, 32)
            for b in range(2):
                load_context(b, b)
            at(sp, "q3_v", "ql")
            sp.wait_ge(stacks_ready, 3)
            for g in range(4):
                for k, src in enumerate((qh, ql, qh)):
                    sp.dma_start(QS[32 * k:32 * k + 32, g, :].bitcast(F32), src[32 * g:32 * g + 32, :].bitcast(F32)
                                 ).then_inc(qs_stacked, 16)
            for n in (-1, 0, 1):
                sync_slot(n, n % 2)
            with sp.Fori(0, 5) as i:
                sync_slot(2 * i + 2, 0)
                sync_slot(2 * i + 3, 1)
            for n in (12, 13, 14, 15):
                sync_slot(n, n % 2)
            sp.wait_ge(P["e0_v"].sem, 4 * P["e0_v"].n)
            heads_done(sp, "a2")
            moe_sync(sp, "e1", (A["L1_ffn_W1"], None, A["L1_ffn_W2"], A["L1_ffn_b1"]))
            for t in range(2):
                at(sp, "e1_v", f"y1{t}", EXPERTS // 2 - 1)
                sp.dma_start(out_view[:, 4 * t:4 * t + 4, :], x[:, 4 * t:4 * t + 4, :]).then_inc(stored, 16)
            sp.wait_ge(stored, 32)
            for b in range(2):
                sp.wait_ge(ctxT_saved[b], 16 * PAIRS)

        @block.gpsimd
        def _(g):
            G.memset(co_w[:, :, :], 0.0)
            G.memset(cv_b[:, :], 0.0).then_inc(consts_ready, 1)
            g.wait_ge(consts_loaded, 16)
            ln_all_gpsimd(0)
            g.wait_ge(mask_loaded, 16)
            G.memset(mask_sb[:, KEYS:KPAD], NEG).then_inc(mask_padded, 1)
            g.wait_ge(mask_padded, 1)
            tiles = "b (t p) -> b t p"
            perm_in = mask_sb[:, 0:FULL * 128].rearrange("b (p t) -> b t p", t=FULL)
            G.tensor_copy(mask_hi[:, 0:FULL * 128].rearrange(tiles, t=FULL), perm_in).then_inc(mask_padded, 1)
            G.tensor_copy(mask_hi[:, FULL * 128:KPAD], mask_sb[:, FULL * 128:KPAD]).then_inc(mask_split, 1)
            g.wait_ge(mask_padded, 2)
            g.wait_ge(mask_split, 1)
            G.tensor_tensor(mask_lo[:, 0:FULL * 128].rearrange(tiles, t=FULL), perm_in,
                            mask_hi[:, 0:FULL * 128].rearrange(tiles, t=FULL), ALU.subtract).then_inc(mask_split, 1)
            G.tensor_tensor(mask_lo[:, FULL * 128:KPAD], mask_sb[:, FULL * 128:KPAD], mask_hi[:, FULL * 128:KPAD],
                            ALU.subtract).then_inc(mask_split, 1)

            def all_max(k, step, stage):
                at(G, stage, step)
                P["q_all"].done(G.partition_all_reduce(gmax[:, k:k + 1], amax[:, k:k + 1], 128, ABSMAX),
                                QUANT[k])

            all_max(0, "wi", "qw_v")
            all_max(1, "wo", "qw_v")
            ln_all_gpsimd(1)
            attn_gpsimd("a0")
            ln_all_gpsimd(2)
            with g.Fori(0, EXPERTS // 2) as i:
                moe_gpsimd("e0", True, i)
            g.wait_ge(P["e0_v"].sem, 4 * P["e0_v"].n)
            G.memset(VA[0], 1.0).then_inc(consts_ready, 1)
            G.memset(VA[1], 1.0).then_inc(consts_ready, 1)
            ln_all_gpsimd(3)
            g.wait_ge(qs_stacked, 16 * 12)

            def slot(n, q):
                c = isinstance(n, int)
                if not (c and (n < -1 or n > 14)):
                    if not (c and n < 1):
                        at(G, "exp_p", f"s{KT - 1}", n - 1)
                    apart_g(n, 0 + 3 * q)
                    P["qb_g"].done(G.tensor_tensor(QB[1 - q][:, :].rearrange("p (g h q) -> p g h q", g=4, h=4),
                                   QS[:, :, bass.ds(SEQ * (n + 1), SEQ)].unsqueeze(2).broadcast_to([128, 4, 4, SEQ]),
                                   consts[:, C_QM:C_QM + 4].unsqueeze(1).unsqueeze(3).broadcast_to([128, 4, 4, SEQ]),
                                   ALU.mult), "qb")
                if not (c and n < 1):
                    m = n - 1
                    at(G, "sum_v", "sum", m)
                    P["fin_g"].done(G.tensor_tensor(rsum, acc_sb, rsum, ALU.mult), "scaled")
                    at(G, "fin_g", "scaled", m)
                    r4 = rsum.rearrange("p (r h q) -> p r h q", r=2, h=2)
                    P["fin_g"].done(G.tensor_tensor(r4, r4, consts[:, C_OM:C_OM + 2].unsqueeze(1).unsqueeze(3)
                                                    .broadcast_to([128, 2, 2, SEQ]), ALU.mult), "own")
                    at(G, "fin_g", "own", m)
                    apart_g(n, 1 + 3 * q)
                    o3 = onT[:, :, bass.ds(SEQ * m, SEQ)]
                    P["fin_g"].done(G.tensor_tensor(o3, r4[:, :, 0, :], r4[:, :, 1, :], ALU.add), "added")
                    at(G, "fin_g", "added", m)
                    apart_g(n, 2 + 3 * q)
                    P["fin_g"].done(G.tensor_tensor(o3, o3, cv_b[:, :].unsqueeze(2).broadcast_to([128, 2, SEQ]), ALU.add), "on")

            slots(g, slot)
            ln_all_gpsimd(4)
            attn_gpsimd("a1")
            ln_all_gpsimd(5)
            ln_all_gpsimd(6)
            ln_all_gpsimd(7)
            all_max(2, "X", "qx_v")
            all_max(3, "Q", "qx_v")
            attn_gpsimd("a2")
            all_max(4, "O", "qx_v")
            all_max(5, "Y", "qx_v")
            ln_all_gpsimd(8)
            with g.Fori(0, EXPERTS // 2) as i:
                moe_gpsimd("e1", False, i)

        @block.scalar
        def _(act):
            act.wait_ge(first_loads, 16 * len(FIRST))
            act.wait_ge(consts_loaded, 16)
            def copy_context(b, g, n):
                if g == 0 and not (isinstance(n, int) and n < 1):
                    act.wait_ge(ctxT_saved[b], 16 * n)
                    at(S, "ca_p", "s", n - 1)
                at(S, "ct_p", f"ct{b}{g}", n)
                w = 512 if g < 3 else TAIL
                P["ct_a"].done(S.activation(ctxT[:, b, 512 * g:512 * g + w], bank(4 + g % 2, w), ACT.Copy), f"ct{b}{g}")

            def pair(n, q):
                for m, (b, g) in enumerate(CT):
                    if m == 3:
                        at(S, "ca_v", "max", n)
                        P["ca_a"].done(S.activation(P0, PS[:, 0:KEYS], ACT.Exp, bias=l0s[:, 3:4],
                                                    scale=float(DIM) ** -0.5, accum_out=l0s[:, 4:5]), "exp")
                    if not (isinstance(n, int) and n > 6):
                        copy_context(b, g, n + 1)

            for b, g in CT:
                copy_context(b, g, 0)
            pairs(act, pair)
            for stack in KS:
                S.activation(stack.rearrange("p g k -> p (g k)"), consts[:, C_KROW:C_KROW + 1].broadcast_to([128, 4 * KPAD]),
                             ACT.Copy).then_inc(stacks_ready, 1)
            act.wait_ge(loads, 16 * N_W)
            attn_scalar("a0")
            route_scalar("r0")
            with act.Fori(0, EXPERTS // 2) as i:
                moe_scalar("e0", True, i)
            act.wait_ge(P["e0_v"].sem, EXPERTS // 2 * P["e0_v"].n)
            S.activation(QS[:, :, :].rearrange("p g t -> p (g t)"), consts[:, C_QROW:C_QROW + 1].broadcast_to([128, 4 * TOKENS]),
                         ACT.Copy).then_inc(stacks_ready, 1)
            act.wait_ge(qs_stacked, 16 * 12)
            act.wait_ge(consts_ready, 3)

            def empty(item, n, q):
                if item[0] == "v":
                    g = int(item[1])
                    k0, k = TG[g]
                    rows = 128 if g < 3 else TAIL
                    at(S, "vals_p", item, n + 1)
                    P["vals_a"].done(S.activation(VA[1 - q][0:rows, k0:k0 + k, :, 0:16], bank(7, 128 * k, rows)
                                                  .rearrange("p (k h c) -> p k h c", k=k, h=8), ACT.Copy), item)
                if item[0] == "k":
                    c = int(item[1])
                    c0, cw = CHUNKS[c]
                    cw = min(cw, KEYS - c0)
                    at(S, "keys_p", item, n + 2)
                    if c == 0 and not (isinstance(n, int) and n < -1):
                        for g in range(4):
                            act.wait_ge(ks_stacked[g], 48 * (n + 2))
                    P["keys_a"].done(S.activation(kh[:, c0:c0 + cw], bank(7, cw), ACT.Identity,
                                                  bias=COLS["L1_xattn_ck_b"][:, 0:1]), f"kh{c}")

            def slot(n, q):
                c = isinstance(n, int)
                for k in range(KT):
                    if not (c and (n < 0 or n > 15)):
                        rows = 128 if k < FULL else TAIL
                        par = (k + q) % 2
                        at(S, "exp_p", f"s{k}", n)
                        if k >= 2:
                            at(S, "pv_p", f"pv{k - 2}", n)
                        elif not (c and n < 1):
                            at(S, "pv_p", f"pv{k + KT - 2}", n - 1)
                        P["exp_a"].done(S.activation(PT[0:rows, par, :], PS[0:rows, 1024 + 1024 * par:2048 + 1024 * par],
                                                     ACT.Exp), f"e{k}")
                    if k == 0 and not (c and n < 1):
                        at(S, "pv_p", f"pv{KT - 1}", n - 1)
                        if not (c and n < 2):
                            at(S, "fin_g", "on", n - 2)
                        P["acc_a"].done(S.activation(acc_sb, bank(6, 256), ACT.Copy), "acc")
                    for item in side(n, k):
                        empty(item, n, q)

            slots(act, slot)
            attn_scalar("a1")
            for c in range(FC):
                for h in range(2):
                    at(S, "ff_p", f"f{c}{h}")
                    P["ff_a"].done(S.activation(hid[:, c, 512 * h:512 * h + 512], bank(2 * (c % 2) + h), ACT.Gelu,
                                                bias=COLS["L1_xattn_fi_b"][:, c:c + 1]), f"f{c}{h}")
            attn_scalar("a2", unit[:, 0:1])
            moe_scalar("e1", False, 0, {(0, 1): lambda: route_scalar("r1")})
            with act.Fori(0, EXPERTS // 2 - 1) as i:
                moe_scalar("e1", False, i + 1)

        @block.tensor
        def _(pe):
            pe.wait_ge(first_loads, 16 * len(FIRST))
            pe.wait_ge(consts_loaded, 16)
            P["pre_p"].done(T.transpose(bank(6, 128), W["L0_xattn_Wq"][:, :], ident), "WqT")
            P["pre_p"].done(T.transpose(bank(7, 128), W["L0_xattn_Wv"][:, :], ident), "WvT")
            at(T, "pre_v", "WvT")
            pe.wait_ge(ln_xn, PAIRS)
            transpose_tensor(0, u_all)
            for h in range(2):
                pe.wait_ge(ln_xT, h + 1)
                P["q0_p"].done(mm(bank(h), WqT[:, :], xT_all[:, 512 * h:512 * h + 512]), f"q{h}")
            for h in range(2):
                at(T, "q0_v", f"q{h}")
                last = mm(bank(2 + h), W["L0_xattn_Wk"][:, :], l0q[:, 512 * h:512 * h + 512])
            P["q0_p"].done(last, "qk")
            for t in range(PAIRS):
                last = mm(PS[:, t:t + 1], l0q[:, 128 * t:128 * t + 128], COLS["L0_xattn_bk"][:, :])
            P["q0_p"].done(last, "qb")

            def transpose_context(b, g, n, q):
                m = 4 * b + g
                if m == 0:
                    pe.wait_ge(ctx_loaded[q], 32 * (n - q) + 64)
                if m >= 2:
                    at(T, "ct_a", "ct%d%d" % CT[m - 2], n)
                elif not (isinstance(n, int) and n < 1):
                    at(T, "ct_a", "ct%d%d" % CT[m + 6], n - 1)
                k0, k = TG[g]
                for j in range(k):
                    rows = 128 if k0 + j < FULL else TAIL
                    last = T.transpose(PS[:, 512 * (4 + g % 2) + 128 * j:512 * (4 + g % 2) + 128 * j + rows],
                                       ctx_nat[q][0:rows, b, k0 + j, :], consts[0:rows, C_ID:C_ID + rows])
                P["ct_p"].done(last, f"ct{b}{g}")

            def probabilities(g, n):
                if g == 0:
                    at(T, "ca_a", "exp", n)
                if g >= 2:
                    at(T, "ca_v", f"p{g - 2}", n)
                k0, k = TG[g]
                rows = 128 if g < 3 else TAIL
                for j in range(k):
                    o = 512 * (6 + g % 2) + 128 * j
                    last = T.transpose(PS[0:rows, o:o + 128], P0[:, (k0 + j) * 128:(k0 + j) * 128 + rows], ident)
                P["ca_p"].done(last, f"p{g}")

            def pair(n, q):
                beside = [] if isinstance(n, int) and n > 6 else CT
                at(T, "qk_v", "qk", n)
                at(T, "ct_a", "ct13", n)
                for b in range(2):
                    for c0 in range(0, KEYS, 512):
                        w = min(512, KEYS - c0)
                        last = mm(PS[64 * b:64 * b + 64, c0:c0 + w], l0qk[:, q, 64 * b:64 * b + 64], ctxT[:, b, c0:c0 + w])
                P["ca_p"].done(last, "s")
                for b, g in beside[:6]:
                    transpose_context(b, g, n + 1, 1 - q)
                for g in (0, 1):
                    probabilities(g, n)
                for b, g in beside[6:7]:
                    transpose_context(b, g, n + 1, 1 - q)
                for g in (2, 3):
                    probabilities(g, n)
                for b, g in beside[7:]:
                    transpose_context(b, g, n + 1, 1 - q)
                at(T, "ca_v", "p3", n)
                for b in range(2):
                    for k in range(KT):
                        rows = 128 if k < FULL else TAIL
                        last = mm(PS[:, 1664 + 64 * b:1728 + 64 * b], ctx_nat[q][0:rows, b, k, :], P0T[0:rows, k, 64 * b:64 * b + 64],
                                  start=k == 0, stop=k == KT - 1)
                P["ca_p"].done(last, "pc")
                at(T, "ca_v", "pc", n)
                P["ca_p"].done(mm(PS[:, 1792:1920], pcT[:, :], WvT[:, :]), "y")

            at(T, "q0_v", "qk")
            for b, g in CT:
                transpose_context(b, g, 0, 0)
            pairs(pe, pair)
            pe.wait_ge(loads, 16 * N_W)
            pe.wait_ge(ln_xn, 2 * PAIRS)
            transpose_tensor(1, u_all)
            attn_tensor("a0", 1, *(W["L0_attn_W_" + n][:, :] for n in "QKVo"))
            pe.wait_ge(ln_xn, 3 * PAIRS)
            transpose_tensor(2, u_all)
            route_tensor("r0", 2, W["L0_ffn_gate"][:, :])
            at(T, "e0_x", "lo")
            with pe.Fori(0, EXPERTS // 2) as i:
                moe_tensor("e0", True, i)
            pe.wait_ge(P["e0_v"].sem, 4 * P["e0_v"].n)
            pe.wait_ge(consts_ready, 3)
            pe.wait_ge(ln_xn, 4 * PAIRS)
            transpose_tensor(3, u_all)
            for h in range(2):
                pe.wait_ge(ln_xT, 6 + h + 1)
                P["q3_p"].done(mm(bank(h), W["L1_xattn_cq_w"][:, :], xT_all[:, 512 * h:512 * h + 512]), f"q{h}")

            def beside(item, n, q):
                if item[0] != "m":
                    bank7_free(item, n)
                if item == "sum":
                    at(T, "acc_a", "acc", n - 1)
                    P["sum_p"].done(mm(bank(7, 256), consts[:, C_SEL:C_SEL + 128], acc_sb), "sum")
                elif item[0] == "v":
                    g = int(item[1])
                    k0, k = TG[g]
                    for j in range(k):
                        rows = 128 if k0 + j < FULL else TAIL
                        kc = (k0 + j) * 128
                        last = mm(PS[0:rows, 3584 + 128 * j:3584 + 128 * j + 128], ctxT[:, 1 - q, kc:kc + rows], W["L1_xattn_cv_w"][:, :])
                    P["vals_p"].done(last, item)
                elif item[0] == "k":
                    c0, cw = CHUNKS[int(item[1])]
                    cw = min(cw, KEYS - c0)
                    if item == "k0":
                        pe.wait_ge(ctxT_loaded[q], 8 * (n + 2 - q) + 16)
                    P["keys_p"].done(mm(bank(7, cw), W["L1_xattn_ck_w"][:, :], ctxT[:, q, c0:c0 + cw]), item)
                elif item == "nm":
                    at(T, "max_v", "nm", n + 1)
                    P["max_p"].done(T.transpose(bank(7, 128, 8), nm[:, :], ident), "nm")
                else:
                    p, c = int(item[1]), int(item[2])
                    m = 4 * p + c
                    if m == 0:
                        at(T, "qb_g", "qb", n + 1)
                        pe.wait_ge(mask_stacked, 16 * (n + 2))
                    if c == 0 and p % 2 == 0:
                        pe.wait_ge(ks_stacked[p // 2], 48 * (n + 2))
                    if m >= 2:
                        at(T, "max_v", "m%d%d" % MAXIMA[m - 2], n + 1)
                    elif not (isinstance(n, int) and n < 0):
                        at(T, "max_v", "m7%d" % (m + 2), n)
                    c0, cw = CHUNKS[c]
                    P["max_p"].done(mm(bank(m % 2, cw), QB[1 - q][:, 128 * p:128 * p + 128], KS[1 - q][:, p // 2, c0:c0 + cw]), item)

            def values(n, k, q):
                rows = 128 if k < FULL else TAIL
                at(T, "exp_a", f"e{k}", n)
                if k == 0:
                    at(T, "vals_a", "v3", n)
                    if not (isinstance(n, int) and n < 1):
                        at(T, "acc_a", "acc", n - 1)
                for r in range(2):
                    for j in range(4):
                        p = 4 * r + j
                        last = mm(PS[32 * j:32 * j + 32, 3072 + 128 * r:3200 + 128 * r], VA[q][0:rows, k, p, :],
                                  PT[0:rows, (k + q) % 2, 128 * p:128 * p + 128], start=k == 0 and r == 0,
                                  stop=k == KT - 1, skip_group_check=True, tile_position=(0, 32 * j))
                P["pv_p"].done(last, f"pv{k}")

            def slot(n, q):
                c = isinstance(n, int)
                for k in range(KT):
                    if not (c and (n < 0 or n > 15)):
                        rows = 128 if k < FULL else TAIL
                        par = (k + q) % 2
                        if k == 0:
                            pe.wait_ge(nm_stacked, 32 * (n + 1))
                        if k >= 2:
                            at(T, "exp_a", f"e{k - 2}", n)
                        elif not (c and n < 1):
                            at(T, "exp_a", f"e{k + KT - 2}", n - 1)
                        for g in range(4):
                            o = 1024 + 1024 * par + 256 * g
                            last = mm(PS[0:rows, o:o + 256], KS[q][:, g, 128 * k:128 * k + rows], QB[q][:, 256 * g:256 * g + 256])
                        P["exp_p"].done(last, f"s{k}")
                    for item in maxima(n, k, 0):
                        beside(item, n, q)
                    if k and not (c and (n < 0 or n > 15)):
                        values(n, k - 1, q)
                    if k == 0 and not (c and n < 1):
                        values(n - 1, KT - 1, 1 - q)
                    for item in maxima(n, k, 1) + side(n, k):
                        beside(item, n, q)

            slots(pe, slot)
            at(T, "fin_g", "on", BATCH - 1)
            for t in range(PAIRS):
                for r in range(2):
                    last = mm(PS[:, 128 * t:128 * t + 128], onT[:, r, 128 * t:128 * t + 128], co_w[:, r, :], start=r == 0, stop=r == 1)
            P["l1_p"].done(last, "cy")
            at(T, "l1_v", "ct")
            transpose_tensor(4, u_all)
            attn_tensor("a1", 4, *(W[f"L1_xattn_s{n}_w"][:, :] for n in "qkvo"))
            at(T, "l1_u", "s")
            transpose_tensor(5, u_all)
            for c in range(FC):
                for h in range(2):
                    pe.wait_ge(ln_xT, 10 + h + 1)
                    if c >= 2:
                        at(T, "ff_a", f"f{c - 2}{h}")
                    P["ff_p"].done(mm(bank(2 * (c % 2) + h), W["L1_xattn_fi_w"][:, 128 * c:128 * c + 128],
                                      xT_all[:, 512 * h:512 * h + 512]), f"f{c}{h}")
            at(T, "ff_a", f"f{FC - 1}1")
            for t in range(PAIRS):
                for c in range(FC):
                    last = mm(PS[:, 2048 + 128 * t:2048 + 128 * t + 128], hid[:, c, 128 * t:128 * t + 128],
                              W["L1_xattn_fo_w"][:, c, :], start=c == 0, stop=c == FC - 1)
            P["ff_p"].done(last, "fy")

            at(T, "qw_v", "quantised")
            for c in range(3):
                last = T.transpose(bank(c, 128), W["L1_attn_in_w"][:, c, :], ident)
            P["qw_p"].done(last, "wiT")
            P["qw_p"].done(T.transpose(bank(3, 128), W["L1_attn_out_w"][:, :], ident), "woT")
            pe.wait_ge(ln_xn, 8 * PAIRS)
            transpose_tensor(6, u_all)
            pe.wait_ge(ln_xT, 14)
            for s_ in range(3):
                for h in range(2):
                    P["qx_p"].done(mm(bank(2 * s_ + h), WiT[:, s_, :], xT_all[:, 512 * h:512 * h + 512]), f"X{s_}{h}")
            at(T, "qo_v", "V")
            heads_tensor("a2", X[:, 2, :], ident)
            at(T, "qo_v", "Oint")
            transpose_heads()
            pe.wait_ge(heads_copied, 6)
            for t in range(PAIRS):
                last = mm(PS[:, 128 * t:128 * t + 128], K_all[:, 128 * t:128 * t + 128], WoT)
            P["qo_p"].done(last, "y")
            pe.wait_ge(ln_xn, 9 * PAIRS)
            transpose_tensor(7, u_all)
            route_tensor("r1", 7, W["L1_ffn_W_router"][:, :])
            at(T, "e1_x", "lo")
            moe_tensor("e1", False, 0, {(0, 3): weights_transposed, (1, 1): biases_weighted})
            with pe.Fori(0, EXPERTS // 2 - 1) as i:
                moe_tensor("e1", False, i + 1)

        @block.vector
        def _(dve):
            dve.wait_ge(first_loads, 16 * len(FIRST))
            dve.wait_ge(consts_loaded, 16)
            dve.wait_ge(x_loaded, 16)
            at(V, "pre_p", "WqT")
            vdone(V.tensor_copy(WqT[:, :], bank(6, 128)), "pre_v", "WqT")
            at(V, "pre_p", "WvT")
            vdone(V.tensor_copy(WvT[:, :], bank(7, 128)), "pre_v", "WvT")
            flat = "p t d -> p (t d)"

            def rows_of(name):
                return ROWS[name][:, :].unsqueeze(1).broadcast_to([128, PAIRS, 128])

            x_now = x[:, :, :]
            ln_all_vector(0, x, u_all)
            transpose_vector(0)
            link(V.tensor_tensor(x_now, x_now, rows_of("L0_xattn_bv"), ALU.add))
            for h in range(2):
                at(V, "q0_p", f"q{h}")
                vdone(V.tensor_scalar(l0q[:, 512 * h:512 * h + 512], bank(h), COLS["L0_xattn_bq"][:, 0:1], None, ALU.add), "q0_v", f"q{h}")
            at(V, "q0_p", "qk")
            link(V.tensor_copy(l0qk_all, PS[:, 1024:2048]))
            at(V, "q0_p", "qb")
            vdone(V.tensor_copy(qb_all[:, :], PS[:, 0:PAIRS]), "q0_v", "qk")

            def copy_queries(n, q):
                P["qk_v"].done(V.tensor_copy(l0qk[:, q, :], l0qk_all[:, bass.ds(128 * n, 128)]), "qk")

            def pair(n, q, meanwhile=None):
                at(V, "ca_p", "s", n)
                link(V.reduce_max(l0s[:, 1:2], PS[:, 0:KEYS], AX))
                qb = qb_all[:, bass.ds(n, 1)]
                link(V.tensor_tensor(l0s[:, 2:3], l0s[:, 1:2], qb, ALU.add))
                link(V.tensor_tensor(l0s[:, 5:6], qb, l0s[:, 2:3], ALU.subtract))
                vdone(V.tensor_scalar(l0s[:, 3:4], l0s[:, 5:6], float(DIM) ** -0.5, None, ALU.mult), "ca_v", "max", n)
                if meanwhile is not None:
                    meanwhile()
                for g, (k0, k) in enumerate(TG):
                    at(V, "ca_p", f"p{g}", n)
                    rows = 128 if g < 3 else TAIL
                    P["ca_v"].done(V.tensor_copy(P0T[0:rows, k0:k0 + k, :].rearrange("p k q -> p (k q)"),
                                                 bank(6 + g % 2, 128 * k, rows)), f"p{g}")
                link(V.reciprocal(l0s[:, 6:7], l0s[:, 4:5]))
                at(V, "ca_p", "pc", n)
                P["ca_v"].done(V.tensor_copy(pcT[:, :], PS[:, 1664:1792]), "pc")
                at(V, "ca_p", "y", n)
                xt = x[:, bass.ds(n, 1), :].rearrange(flat)
                vdone(V.scalar_tensor_tensor(xt, PS[:, 1792:1920], l0s[:, 6:7], xt, ALU.mult, ALU.add), "ca_v", "y", n)
                if not (isinstance(n, int) and n > 6):
                    copy_queries(n + 1, 1 - q)

            def quant_scale(k):
                at(V, "q_all", QUANT[k])
                link(V.tensor_scalar(qscale[:, k:k + 1], gmax[:, k:k + 1], 1.0 / QMAX, 1e-8, ALU.mult, ALU.max))
                link(V.reciprocal(qinv[:, k:k + 1], qscale[:, k:k + 1]))

            def quantise(t, k):
                link(V.tensor_scalar(t, t, qinv[:, k:k + 1], ROUND, ALU.mult, ALU.add))
                link(V.tensor_scalar(t, t, ROUND, QMAX, ALU.subtract, ALU.min))
                return V.tensor_scalar(t, t, -QMAX - 1.0, None, ALU.max)

            def largest(k, src):
                return V.reduce_max(amax[:, k:k + 1], src, AX, apply_absolute_value=True)

            def weights_largest():
                dve.wait_ge(loads, 16 * N_W)
                vdone(largest(0, wi), "qw_v", "wi")
                vdone(largest(1, wo), "qw_v", "wo")

            def weights_quantised():
                quant_scale(0)
                link(quantise(wi, 0))
                quant_scale(1)
                vdone(quantise(wo, 1), "qw_v", "quantised")

            wi = W["L1_attn_in_w"][:, :, :].rearrange("p c n -> p (c n)")
            wo = W["L1_attn_out_w"][:, :]
            copy_queries(0, 0)
            with dve.Fori(0, 3) as i:
                def two_pairs():
                    pair(2 * i, 0)
                    pair(2 * i + 1, 1)
                in_loop(i, PER["ca"], two_pairs)
            state["links"] += 3 * PER["ca"]
            pair(6, 0, weights_largest)
            pair(7, 1, weights_quantised)
            ln_all_vector(1, x, u_all)
            transpose_vector(1)
            dve.wait_ge(mask_split, 3)
            dve.wait_ge(loads, 16 * N_W)
            for b in range(2):
                dve.wait_ge(ctxT_saved[b], 16 * PAIRS)
            attn_vector("a0", None, None, None, causal)
            y8 = PS[:, 0:1024].rearrange("p (t d) -> p t d", t=PAIRS)
            link(V.tensor_tensor(x_now, x_now, y8, ALU.add))
            ln_all_vector(2, x, u_all)
            transpose_vector(2)
            split_tokens("e0", 2)
            route_vector("r0")

            with dve.Fori(0, EXPERTS // 2) as i:
                in_loop(i, PER["e0"], lambda: moe_vector("e0", True, i))
            state["links"] += EXPERTS // 2 * PER["e0"]

            def add_bias(b):
                link(V.tensor_tensor(u_all[:, :, :], u_all[:, :, :], rows_of(b), ALU.add))

            def post_norm(y, g, be, r):
                link(V.tensor_tensor(t_all, y, u_all[:, :, :], ALU.add))
                ln_all_vector(r, t_all, t_all)
                link(V.tensor_tensor(t_all, t_all, rows_of(g), ALU.mult))
                return V.tensor_tensor(u_all[:, :, :], t_all, rows_of(be), ALU.add)

            def beside(item, n, q):
                if item == "sum":
                    at(V, "sum_p", "sum", n - 1)
                    if not (isinstance(n, int) and n < 2):
                        at(V, "fin_g", "on", n - 2)
                    P["sum_v"].done(V.reciprocal(rsum, bank(7, 256)), "sum")
                elif item[0] == "k":
                    c = int(item[1])
                    c0, cw = CHUNKS[c]
                    cw = min(cw, KEYS - c0)
                    at(V, "keys_a", f"kh{c}", n + 2)
                    P["keys_v"].done(V.scalar_tensor_tensor(kl[:, c0:c0 + cw], bank(7, cw), COLS["L1_xattn_ck_b"][:, 0:1],
                                                            kh[:, c0:c0 + cw], ALU.add, ALU.subtract), f"kl{c}")
                elif item == "nm":
                    at(V, "max_v", f"m73", n + 1)
                    vdone(V.tensor_reduce(nm[:, :], mx[:, :, :], AX, ALU.max, negate=True), "max_v", "nm", n + 1)
                    at(V, "max_p", "nm", n + 1)
                    vdone(V.tensor_copy(nmh[:, :], bank(7, 128, 8)), "max_v", "nmh", n + 1)
                    vdone(V.tensor_tensor(nml[:, :], bank(7, 128, 8), nmh[:, :], ALU.subtract), "max_v", "nml", n + 1)
                elif item[0] == "m":
                    p, c = int(item[1]), int(item[2])
                    at(V, "max_p", item, n + 1)
                    P["max_v"].done(V.reduce_max(mx[:, p, c:c + 1], bank((4 * p + c) % 2, CHUNKS[c][1]), AX), item)

            def slot(n, q):
                for k in range(KT):
                    passed = side(n, k - 1) if k else []
                    for item in passed + maxima(n, k) if k == 2 else maxima(n, k, 0) + passed + maxima(n, k, 1):
                        beside(item, n, q)

            ln_all_vector(3, x, u_all)
            transpose_vector(3)
            for h in range(2):
                at(V, "q3_p", f"q{h}")
                vdone(V.tensor_scalar(PT[:, 0, 512 * h:512 * h + 512], bank(h), COLS["L1_xattn_cq_b"][:, 0:1], HD ** -0.5,
                                      ALU.add, ALU.mult), "q3_v", f"qf{h}")
            dve.wait_ge(mask_saved, 32)
            vdone(V.tensor_copy(qh, PT[:, 0, :]), "q3_v", "qh")
            vdone(V.tensor_tensor(ql, PT[:, 0, :], qh, ALU.subtract), "q3_v", "ql")
            dve.wait_ge(qs_stacked, 16 * 12)
            add_bias("L1_xattn_co_b")
            slots(dve, slot)
            at(V, "l1_p", "cy")
            y8 = PS[:, 0:1024].rearrange("p (t d) -> p t d", t=PAIRS)
            vdone(post_norm(y8, "L1_xattn_co_g", "L1_xattn_co_be", 4), "l1_v", "ct")
            transpose_vector(4)
            add_bias("L1_xattn_so_b")
            attn_vector("a1", COLS["L1_xattn_sq_b"][:, 0:1], COLS["L1_xattn_sk_b"][:, 0:1], rows_of("L1_xattn_sv_b"), None)
            vdone(post_norm(y8, "L1_xattn_so_g", "L1_xattn_so_be", 5), "l1_u", "s")
            transpose_vector(5)
            add_bias("L1_xattn_fo_b")
            at(V, "ff_p", "fy")
            y8 = PS[:, 2048:3072].rearrange("p (t d) -> p t d", t=PAIRS)
            link(post_norm(y8, "L1_xattn_fo_g", "L1_xattn_fo_be", 6))
            V.tensor_tensor(x_now, x_now, u_all[:, :, :], ALU.add).then_inc(x_updated, 1)
            dve.wait_ge(x_updated, 1)

            at(V, "qw_p", "woT")
            for c in range(3):
                link(V.tensor_copy(WiT[:, c, :], bank(c, 128)))
            vdone(V.tensor_copy(WoT, bank(3, 128)), "qw_v", "wiT")
            ln_all_vector(7, x, u_all)
            transpose_vector(6)
            for s_ in range(3):
                for h in range(2):
                    at(V, "qx_p", f"X{s_}{h}")
                    link(V.tensor_scalar(X[:, s_, :].rearrange("p (s l) -> p l s", l=BATCH)[:, 8 * h:8 * h + 8, :],
                                         bank(2 * s_ + h).rearrange("p (l s) -> p l s", s=SEQ), qscale[:, 0:1],
                                         COLS["L1_attn_in_b"][:, s_:s_ + 1], ALU.mult, ALU.add))
                link(V.reduce_max(xmax[:, s_:s_ + 1], X[:, s_, :], AX, apply_absolute_value=True))
            vdone(V.reduce_max(amax[:, 2:3], xmax[:, :], AX), "qx_v", "X")
            quant_scale(2)
            vdone(quantise(X[:, 2, :], 2), "qo_v", "V")
            link(quantise(X[:, 0, :], 2))
            link(V.tensor_scalar(X[:, 0, :], X[:, 0, :], qscale[:, 2:3], HD ** -0.5, ALU.mult, ALU.mult))
            vdone(largest(3, X[:, 0, :]), "qx_v", "Q")
            link(quantise(X[:, 1, :], 2))
            quant_scale(3)
            link(quantise(X[:, 0, :], 3))
            link(V.tensor_tensor(unit[:, 0:1], qscale[:, 2:3], qscale[:, 3:4], ALU.mult))
            heads_vector("a2", block_mask, qscale[:, 2:3])
            for lane in "01":
                at(V, "a2_v" + lane, "o", ROUNDS - 1)
            Of = t_all.rearrange("p t d -> p (t d)")
            vdone(largest(4, Of), "qx_v", "O")
            quant_scale(4)
            vdone(quantise(Of, 4), "qo_v", "Oint")
            link(V.tensor_tensor(unit[:, 1:2], qscale[:, 1:2], qscale[:, 4:5], ALU.mult))
            for h in range(2):
                dve.wait_ge(heads_T, 4 + h + 1)
                V.tensor_copy(K_all.rearrange("p (l s) -> p s l", l=BATCH)[:, 32 * h:32 * h + 32, :],
                              bank(6 + h).rearrange("p (s l) -> p s l", l=BATCH)).then_inc(heads_copied, 1)
            at(V, "qo_p", "y")
            link(V.scalar_tensor_tensor(Y_all, PS[:, 0:1024].rearrange("p (t d) -> p t d", t=PAIRS), unit[:, 1:2],
                                        rows_of("L1_attn_out_b"), ALU.mult, ALU.add))
            Yf = Y_all.rearrange("p t d -> p (t d)")
            vdone(largest(5, Yf), "qx_v", "Y")
            quant_scale(5)
            link(quantise(Yf, 5))
            xf = x[:, :, :].rearrange("p t d -> p (t d)")
            vdone(V.scalar_tensor_tensor(xf, Yf, qscale[:, 5:6], xf, ALU.mult, ALU.add), "qx_v", "x")

            ln_all_vector(8, x, u_all)
            transpose_vector(7)
            split_tokens("e1", 7)
            route_vector("r1", router_b[:, :])

            def biases_added():
                at(V, "r1_p", "wT")
                P["r1_v"].done(V.tensor_copy(w_tT, PS[0:EXPERTS, 3072:4096]), "wT")
                at(V, "r1_p", "b2")
                vdone(V.tensor_tensor(x_now, x_now, PS[:, 3072:4096].rearrange("p (t d) -> p t d", t=PAIRS), ALU.add),
                      "r1_v", "end")

            moe_vector("e1", False, 0, biases_added)
            with dve.Fori(0, EXPERTS // 2 - 1) as i:
                in_loop(i, PER["e1"], lambda: moe_vector("e1", False, i + 1))


SCHEDULE = ((1, "sum", 0), (2, "v0", 3), (3, "v1", 4), (4, "v2", 4), (5, "v3", 4), (6, "k0", 4),
            (7, "k1", 4), (8, "k2", 4), (9, "k3", 5), (10, "nm", 0))
PER = {"ca": 8, "a0": 6, "e0": 12, "a1": 4, "a2": 8, "e1": 12}


def constants():
    import numpy as np
    c = np.zeros((128, C_END), np.float32)
    p = np.arange(128)
    c[:, C_ID:C_ID + 128] = np.eye(128)
    c[:, C_HM:C_HM + 16] = p[:, None] // HD == np.arange(16)[None]
    ch = np.arange(128)[None] // HD
    c[:, C_VM2:C_VM2 + 128] = ch % 2 == p[:, None] // 64
    c[:, C_CAUSAL:C_CAUSAL + 64] = np.where(np.arange(64)[None] <= p[:, None] % 64, 0.0, NEG)
    c[:, C_BLK:C_BLK + 64] = np.where(np.arange(64)[None] // BATCH == (p[:, None] % 64) // BATCH, 0.0, NEG)
    c[:, C_QM:C_QM + 4] = np.where(p[:, None] < 96, (p[:, None] % 32) // HD == np.arange(4)[None], 1.0)
    c[:, C_SEL:C_SEL + 128] = p[:, None] == 32 * (p[None] // 32) + 16
    c[:, C_OM:C_OM + 2] = (p[:, None] % 32 < 16) & ((p[:, None] % 32) // HD == np.arange(2)[None])
    c[:, C_IOTA:C_IOTA + 8] = np.arange(8)[None]
    c[:, C_KROW] = (p == 96) | (p == 97)
    c[:, C_QROW] = (p == 98) | (p == 99)
    c[:, C_HALF] = -0.5
    c[:, C_ONE] = 1.0
    c[:, C_HEAD:C_HEAD + 2] = p[:, None] // 64 == np.arange(2)[None]
    return c


NAMES = [
    "x", "ctx_1024", "mask_Bx1x1xS2_ff0", "L0_xattn_Wq", "L0_xattn_bq", "L0_xattn_Wk", "L0_xattn_bk", "L0_xattn_Wv",
    "L0_xattn_bv", "L0_attn_W_Q", "L0_attn_W_K", "L0_attn_W_V", "L0_attn_W_o", "L0_ffn_gate", "L0_ffn_experts_w1",
    "L0_ffn_experts_w2", "L0_ffn_experts_w3", "L1_xattn_cq_w", "L1_xattn_cq_b", "L1_xattn_ck_w", "L1_xattn_ck_b",
    "L1_xattn_cv_w", "L1_xattn_cv_b", "L1_xattn_co_w", "L1_xattn_co_b", "L1_xattn_co_g", "L1_xattn_co_be",
    "L1_xattn_sq_w", "L1_xattn_sq_b", "L1_xattn_sk_w", "L1_xattn_sk_b", "L1_xattn_sv_w", "L1_xattn_sv_b",
    "L1_xattn_so_w", "L1_xattn_so_b", "L1_xattn_so_g", "L1_xattn_so_be", "L1_xattn_fi_w", "L1_xattn_fi_b",
    "L1_xattn_fo_w", "L1_xattn_fo_b", "L1_xattn_fo_g", "L1_xattn_fo_be", "L1_attn_in_w", "L1_attn_in_b",
    "L1_attn_out_w", "L1_attn_out_b", "L1_ffn_W_router", "L1_ffn_b_router", "L1_ffn_W1", "L1_ffn_b1", "L1_ffn_W2",
    "L1_ffn_b2"]


def kernel(**inputs):
    import numpy as np
    import concourse.bacc as bacc
    from concourse.bass_utils import run_bass_kernel_spmd as run

    nc = bacc.Bacc("TRN2", target_bir_lowering=False, num_devices=1)
    arrays = {name: np.ascontiguousarray(inputs[name]) for name in NAMES}
    arrays["consts"] = constants()
    aps = {name: nc.dram_tensor("in_" + name, a.shape, F32, kind="ExternalInput").ap() for name, a in arrays.items()}
    out = nc.dram_tensor("out_0", (BATCH, SEQ, DIM), F32, kind="ExternalOutput").ap()
    scratch = nc.dram_tensor("context_transposed", (BATCH, 128, KEYS), F32, kind="Internal").ap()
    mask_parts = nc.dram_tensor("mask_parts", (2, BATCH, KPAD), F32, kind="Internal").ap()
    build(nc, aps, out, scratch, mask_parts)
    r = run(nc, [{"in_" + name: a for name, a in arrays.items()}], core_ids=[0])
    return r.results[0]["out_0"]
```
